# Optimizing a Trainium2 kernel written in Bass

```python
import numpy as np
import jax
import jax.numpy as jnp

def _softmax(x, axis=-1):
    return jax.nn.softmax(x, axis=axis)

def _gelu(x):
    return jax.nn.gelu(x, approximate=True)

def _silu(x):
    return jax.nn.silu(x)

def _sigmoid(x):
    return jax.nn.sigmoid(x)

def _layernorm(x, axis=-1, eps=1e-05):
    m = jnp.mean(x, axis=axis, keepdims=True)
    v = jnp.var(x, axis=axis, keepdims=True)
    return (x - m) / jnp.sqrt(v + eps)

def _scatter_add(tgt, idx, src, axis=0):
    return tgt.at[idx].add(src)

def _segment_sum(src, seg, n):
    return jax.ops.segment_sum(src, seg, n)
kernel_name = 'mk_macaron_d2_jaxref_r8_a18908'

def setup_inputs(seed: int=0):
    np.random.seed(seed)
    _w = jnp.asarray

    def _L0_attn_setup():
        import jax, jax.numpy as jnp
        import numpy as np
        _PAIRS4 = [(0, 1), (0, 2), (0, 3), (1, 2), (1, 3), (2, 3)]
        _J6 = jnp.array([[0, 0, 0, 0, 0, 1], [0, 0, 0, 0, -1, 0], [0, 0, 0, 1, 0, 0], [0, 0, 1, 0, 0, 0], [0, -1, 0, 0, 0, 0], [1, 0, 0, 0, 0, 0]], dtype=jnp.float32)
        H = 16
        PD = 4
        DECAY = 0.99

        def exterior(p1, p2):
            parts = jnp.stack([p1[..., i] * p2[..., j] - p1[..., j] * p2[..., i] for i, j in _PAIRS4], axis=-1)
            n = jnp.maximum(jnp.linalg.norm(parts, axis=-1, keepdims=True), 1e-12)
            return parts / n
        key = jax.random.key(seed)
        ks = jax.random.split(key, 12)
        B, T, D = (1, 256, 128)
        s = 0.02
        return {'x': jax.random.normal(ks[0], (B, T, D), jnp.float32), 'qkv_w': jax.random.normal(ks[1], (D, 3 * D), jnp.float32) * s, 'qkv_b': jnp.zeros((3 * D,), jnp.float32), 'w1w': jax.random.normal(ks[2], (D, PD * H), jnp.float32) * s, 'w2w': jax.random.normal(ks[3], (D, PD * H), jnp.float32) * s, 'r1w': jax.random.normal(ks[4], (D, PD * H), jnp.float32) * s, 'r2w': jax.random.normal(ks[5], (D, PD * H), jnp.float32) * s, 'memv_w': jax.random.normal(ks[6], (D, D), jnp.float32) * s, 'memv_b': jnp.zeros((D,), jnp.float32), 'memg_w': jax.random.normal(ks[7], (D, H), jnp.float32) * s, 'memg_b': jnp.zeros((H,), jnp.float32), 'mem_scale': jnp.full((H,), 0.1, jnp.float32), 'out_w': jax.random.normal(ks[8], (D, D), jnp.float32) * s, 'out_b': jnp.zeros((D,), jnp.float32)}
    _L0_attn_in = _L0_attn_setup()

    def _L0_ffn_setup():
        import jax, jax.numpy as jnp
        import numpy as np
        B, S, D, F, E, K = (2, 256, 128, 512, 8, 2)
        key = jax.random.key(seed)
        ks = jax.random.split(key, 5)
        x = jax.random.normal(ks[0], (B, S, D), dtype=jnp.float32)
        Wg = jax.random.normal(ks[1], (D, E), dtype=jnp.float32) * 0.02
        W1 = jax.random.normal(ks[2], (E, D, F), dtype=jnp.float32) * 0.02
        b1 = jnp.zeros((E, F), dtype=jnp.float32)
        W2 = jax.random.normal(ks[3], (E, F, D), dtype=jnp.float32) * 0.02
        b2 = jnp.zeros((E, D), dtype=jnp.float32)
        return {'x': x, 'Wg': Wg, 'W1': W1, 'b1': b1, 'W2': W2, 'b2': b2}
    _L0_ffn_in = _L0_ffn_setup()

    def _L1_attn_setup():
        import jax, jax.numpy as jnp
        import numpy as np
        import math
        EMBED_DIM = 128
        NUM_HEADS = 16
        HEAD_DIM = EMBED_DIM // NUM_HEADS
        WINDOW_SIZE = 32
        SCALING = math.sqrt(HEAD_DIM)
        key = jax.random.key(seed)
        ks = jax.random.split(key, 9)
        B, S, E = (2, 256, EMBED_DIM)
        s = 1.0 / math.sqrt(E)
        inp = {'hidden_states': jax.random.normal(ks[0], (B, S, E), dtype=jnp.float32), 'q_w': jax.random.uniform(ks[1], (E, E), jnp.float32, -s, s), 'q_b': jax.random.uniform(ks[2], (E,), jnp.float32, -s, s), 'k_w': jax.random.uniform(ks[3], (E, E), jnp.float32, -s, s), 'k_b': jax.random.uniform(ks[4], (E,), jnp.float32, -s, s), 'v_w': jax.random.uniform(ks[5], (E, E), jnp.float32, -s, s), 'v_b': jax.random.uniform(ks[6], (E,), jnp.float32, -s, s), 'o_w': jax.random.uniform(ks[7], (E, E), jnp.float32, -s, s), 'o_b': jax.random.uniform(ks[8], (E,), jnp.float32, -s, s)}
        return inp
    _L1_attn_in = _L1_attn_setup()

    def _L1_ffn_setup():
        import jax, jax.numpy as jnp
        import numpy as np
        DIM, HEADS, FFN, E = (128, 16, 512, 8)
        B, S = (2, 128)
        EPS = 1e-05

        def _ln(x, g, b):
            mu = jnp.mean(x, axis=-1, keepdims=True)
            var = jnp.mean((x - mu) ** 2, axis=-1, keepdims=True)
            return (x - mu) * jax.lax.rsqrt(var + EPS) * g + b
        key = jax.random.key(seed)
        ks = jax.random.split(key, 20)
        sd = 0.02
        d, f = (DIM, FFN)
        return {'x': jax.random.normal(ks[0], (B, S, d), jnp.float32), 'ln1_g': jnp.ones((d,), jnp.float32), 'ln1_b': jnp.zeros((d,), jnp.float32), 'Wqkv': jax.random.normal(ks[1], (d, 3 * d), jnp.float32) * sd, 'bqkv': jnp.zeros((3 * d,), jnp.float32), 'Wo': jax.random.normal(ks[2], (d, d), jnp.float32) * sd, 'bo': jnp.zeros((d,), jnp.float32), 'ln2_g': jnp.ones((d,), jnp.float32), 'ln2_b': jnp.zeros((d,), jnp.float32), 'gate_w': jax.random.normal(ks[3], (d, E), jnp.float32) * sd, 'W1': jax.random.normal(ks[4], (E, d, f), jnp.float32) * sd, 'b1': jnp.zeros((E, f), jnp.float32), 'W2': jax.random.normal(ks[5], (E, f, d), jnp.float32) * sd, 'b2': jnp.zeros((E, d), jnp.float32), 'rW1': jax.random.normal(ks[6], (d, f), jnp.float32) * sd, 'rb1': jnp.zeros((f,), jnp.float32), 'rW2': jax.random.normal(ks[7], (f, d), jnp.float32) * sd, 'rb2': jnp.zeros((d,), jnp.float32), 'coef_w': jax.random.normal(ks[8], (d, 2), jnp.float32) * sd, 'coef_b': jnp.zeros((2,), jnp.float32)}
    _L1_ffn_in = _L1_ffn_setup()
    _d = {'L0_attn_x': _L0_attn_in['x'], 'L0_attn_qkv_w': _L0_attn_in['qkv_w'], 'L0_attn_qkv_b': _L0_attn_in['qkv_b'], 'L0_attn_w1w': _L0_attn_in['w1w'], 'L0_attn_w2w': _L0_attn_in['w2w'], 'L0_attn_r1w': _L0_attn_in['r1w'], 'L0_attn_r2w': _L0_attn_in['r2w'], 'L0_attn_memv_w': _L0_attn_in['memv_w'], 'L0_attn_memv_b': _L0_attn_in['memv_b'], 'L0_attn_memg_w': _L0_attn_in['memg_w'], 'L0_attn_memg_b': _L0_attn_in['memg_b'], 'L0_attn_mem_scale': _L0_attn_in['mem_scale'], 'L0_attn_out_w': _L0_attn_in['out_w'], 'L0_attn_out_b': _L0_attn_in['out_b'], 'L0_ffn_Wg': _L0_ffn_in['Wg'], 'L0_ffn_W1': _L0_ffn_in['W1'], 'L0_ffn_b1': _L0_ffn_in['b1'], 'L0_ffn_W2': _L0_ffn_in['W2'], 'L0_ffn_b2': _L0_ffn_in['b2'], 'L1_attn_q_w': _L1_attn_in['q_w'], 'L1_attn_q_b': _L1_attn_in['q_b'], 'L1_attn_k_w': _L1_attn_in['k_w'], 'L1_attn_k_b': _L1_attn_in['k_b'], 'L1_attn_v_w': _L1_attn_in['v_w'], 'L1_attn_v_b': _L1_attn_in['v_b'], 'L1_attn_o_w': _L1_attn_in['o_w'], 'L1_attn_o_b': _L1_attn_in['o_b'], 'L1_ffn_ln1_g': _L1_ffn_in['ln1_g'], 'L1_ffn_ln1_b': _L1_ffn_in['ln1_b'], 'L1_ffn_Wqkv': _L1_ffn_in['Wqkv'], 'L1_ffn_bqkv': _L1_ffn_in['bqkv'], 'L1_ffn_Wo': _L1_ffn_in['Wo'], 'L1_ffn_bo': _L1_ffn_in['bo'], 'L1_ffn_ln2_g': _L1_ffn_in['ln2_g'], 'L1_ffn_ln2_b': _L1_ffn_in['ln2_b'], 'L1_ffn_gate_w': _L1_ffn_in['gate_w'], 'L1_ffn_W1': _L1_ffn_in['W1'], 'L1_ffn_b1': _L1_ffn_in['b1'], 'L1_ffn_W2': _L1_ffn_in['W2'], 'L1_ffn_b2': _L1_ffn_in['b2'], 'L1_ffn_rW1': _L1_ffn_in['rW1'], 'L1_ffn_rb1': _L1_ffn_in['rb1'], 'L1_ffn_rW2': _L1_ffn_in['rW2'], 'L1_ffn_rb2': _L1_ffn_in['rb2'], 'L1_ffn_coef_w': _L1_ffn_in['coef_w'], 'L1_ffn_coef_b': _L1_ffn_in['coef_b']}
    _x0 = _d['L0_attn_x']
    _d['L0_attn_x'] = jax.random.normal(jax.random.fold_in(jax.random.key(seed), 1), (2, 1024, 128), dtype=_x0.dtype)
    del _x0
    return _d

def reference(L0_attn_x, L0_attn_qkv_w, L0_attn_qkv_b, L0_attn_w1w, L0_attn_w2w, L0_attn_r1w, L0_attn_r2w, L0_attn_memv_w, L0_attn_memv_b, L0_attn_memg_w, L0_attn_memg_b, L0_attn_mem_scale, L0_attn_out_w, L0_attn_out_b, L0_ffn_Wg, L0_ffn_W1, L0_ffn_b1, L0_ffn_W2, L0_ffn_b2, L1_attn_q_w, L1_attn_q_b, L1_attn_k_w, L1_attn_k_b, L1_attn_v_w, L1_attn_v_b, L1_attn_o_w, L1_attn_o_b, L1_ffn_ln1_g, L1_ffn_ln1_b, L1_ffn_Wqkv, L1_ffn_bqkv, L1_ffn_Wo, L1_ffn_bo, L1_ffn_ln2_g, L1_ffn_ln2_b, L1_ffn_gate_w, L1_ffn_W1, L1_ffn_b1, L1_ffn_W2, L1_ffn_b2, L1_ffn_rW1, L1_ffn_rb1, L1_ffn_rW2, L1_ffn_rb2, L1_ffn_coef_w, L1_ffn_coef_b):

    def _L0_attn_ref(x, qkv_w, qkv_b, w1w, w2w, r1w, r2w, memv_w, memv_b, memg_w, memg_b, mem_scale, out_w, out_b):
        import jax, jax.numpy as jnp
        import numpy as np
        _PAIRS4 = [(0, 1), (0, 2), (0, 3), (1, 2), (1, 3), (2, 3)]
        _J6 = jnp.array([[0, 0, 0, 0, 0, 1], [0, 0, 0, 0, -1, 0], [0, 0, 0, 1, 0, 0], [0, 0, 1, 0, 0, 0], [0, -1, 0, 0, 0, 0], [1, 0, 0, 0, 0, 0]], dtype=jnp.float32)
        H = 16
        PD = 4
        DECAY = 0.99

        def exterior(p1, p2):
            parts = jnp.stack([p1[..., i] * p2[..., j] - p1[..., j] * p2[..., i] for i, j in _PAIRS4], axis=-1)
            n = jnp.maximum(jnp.linalg.norm(parts, axis=-1, keepdims=True), 1e-12)
            return parts / n
        B, T, D = x.shape
        dh = D // H
        scale = dh ** (-0.5)
        qkv = (x @ qkv_w + qkv_b).reshape(B, T, 3, H, dh)
        q = qkv[:, :, 0].transpose(0, 2, 1, 3)
        k = qkv[:, :, 1].transpose(0, 2, 1, 3)
        v = qkv[:, :, 2].transpose(0, 2, 1, 3)
        scores = jnp.einsum('bhtd,bhsd->bhts', q, k) * scale
        upper = jnp.triu(jnp.ones((T, T), bool), 1)
        scores = jnp.where(upper[None, None], -jnp.inf, scores)
        attn = jax.nn.softmax(scores, axis=-1)
        seq_out = jnp.einsum('bhts,bhsd->bhtd', attn, v).transpose(0, 2, 1, 3).reshape(B, T, D)
        x_prev = jnp.concatenate([jnp.zeros((B, 1, D), x.dtype), x[:, :-1]], axis=1)
        w1 = (x_prev @ w1w).reshape(B, T, H, PD)
        w2 = (x @ w2w).reshape(B, T, H, PD)
        write_lines = exterior(w1, w2)
        r1 = (x @ r1w).reshape(B, T, H, PD)
        r2 = (x @ r2w).reshape(B, T, H, PD)
        read_lines = exterior(r1, r2)
        jw = jnp.einsum('bthi,ij->bthj', write_lines, _J6)
        inc = jnp.einsum('bthi,bshi->bhts', read_lines, jw)
        pos = jnp.arange(T, dtype=x.dtype)
        w = jnp.tril(DECAY ** (pos[:, None] - pos[None, :]), -1)
        mem_score = jnp.einsum('bhts,ts->bht', inc * inc, w)
        mem_val = x @ memv_w + memv_b
        gate = jax.nn.sigmoid(x @ memg_w + memg_b)
        gated = jax.nn.sigmoid(mem_score.transpose(0, 2, 1) * mem_scale[None, None, :]) * gate
        gated = gated.mean(axis=-1, keepdims=True)
        return (seq_out + gated * mem_val) @ out_w + out_b

    def _L0_ffn_ref(x, Wg, W1, b1, W2, b2):
        import jax, jax.numpy as jnp
        import numpy as np
        B, S, D, F, E, K = (2, 256, 128, 512, 8, 2)
        b, s, d = x.shape
        e = Wg.shape[1]
        T = b * s
        C = 2 * K * T // e
        xt = x.reshape(T, d)
        logits = xt.astype(jnp.float32) @ Wg.astype(jnp.float32)
        gates = jax.nn.softmax(logits, axis=-1)
        idx1 = jnp.argmax(gates, axis=-1)
        mask1 = jax.nn.one_hot(idx1, e, dtype=gates.dtype)
        gate1 = jnp.sum(gates * mask1, axis=-1)
        logits2 = jnp.where(mask1 > 0, -jnp.inf, logits)
        idx2 = jnp.argmax(logits2, axis=-1)
        mask2 = jax.nn.one_hot(idx2, e, dtype=gates.dtype)
        gate2 = jnp.sum(gates * mask2, axis=-1)
        denom = gate1 + gate2 + 1e-09
        w1 = gate1 / denom
        w2 = gate2 / denom
        p1 = jnp.cumsum(mask1, axis=0) - mask1
        pos1 = jnp.sum(p1 * mask1, axis=-1).astype(jnp.int32)
        off = jnp.sum(mask1, axis=0)
        p2 = jnp.cumsum(mask2, axis=0) - mask2 + off[None, :]
        pos2 = jnp.sum(p2 * mask2, axis=-1).astype(jnp.int32)
        keep1 = (pos1 < C).astype(xt.dtype)
        keep2 = (pos2 < C).astype(xt.dtype)
        pos1 = jnp.clip(pos1, 0, C - 1)
        pos2 = jnp.clip(pos2, 0, C - 1)
        xe = jnp.zeros((e, C, d), dtype=xt.dtype)
        xe = xe.at[idx1, pos1].add(xt * keep1[:, None])
        xe = xe.at[idx2, pos2].add(xt * keep2[:, None])
        h = jax.nn.gelu(jnp.einsum('ecd,edf->ecf', xe, W1) + b1[:, None, :], approximate=False)
        ye = jnp.einsum('ecf,efd->ecd', h, W2) + b2[:, None, :]
        out = ye[idx1, pos1] * (w1 * keep1)[:, None] + ye[idx2, pos2] * (w2 * keep2)[:, None]
        return out.reshape(b, s, d)

    def _L1_attn_ref(hidden_states, q_w, q_b, k_w, k_b, v_w, v_b, o_w, o_b):
        import jax, jax.numpy as jnp
        import numpy as np
        import math
        EMBED_DIM = 128
        NUM_HEADS = 16
        HEAD_DIM = EMBED_DIM // NUM_HEADS
        WINDOW_SIZE = 32
        SCALING = math.sqrt(HEAD_DIM)
        B, S, E = hidden_states.shape
        H, D, w = (NUM_HEADS, HEAD_DIM, WINDOW_SIZE)
        W = 2 * w + 1
        q = hidden_states @ q_w.T + q_b
        k = hidden_states @ k_w.T + k_b
        v = hidden_states @ v_w.T + v_b
        q = q.reshape(B, S, H, D).transpose(0, 2, 1, 3)
        k = k.reshape(B, S, H, D).transpose(0, 2, 1, 3)
        v = v.reshape(B, S, H, D).transpose(0, 2, 1, 3)
        k_pad = jnp.pad(k, ((0, 0), (0, 0), (w, w), (0, 0)))
        v_pad = jnp.pad(v, ((0, 0), (0, 0), (w, w), (0, 0)))
        idx = jnp.arange(S)[:, None] + jnp.arange(W)[None, :]
        k_slice = k_pad[:, :, idx]
        v_slice = v_pad[:, :, idx]
        score = jnp.einsum('bhsd,bhswd->bhsw', q, k_slice) / SCALING
        p = jax.nn.softmax(score, axis=-1)
        attn = jnp.einsum('bhsw,bhswd->bhsd', p, v_slice)
        attn = attn.transpose(0, 2, 1, 3).reshape(B, S, E)
        return attn @ o_w.T + o_b

    def _L1_ffn_ref(x, ln1_g, ln1_b, Wqkv, bqkv, Wo, bo, ln2_g, ln2_b, gate_w, W1, b1, W2, b2, rW1, rb1, rW2, rb2, coef_w, coef_b):
        import jax, jax.numpy as jnp
        import numpy as np
        DIM, HEADS, FFN, E = (128, 16, 512, 8)
        B, S = (2, 128)
        EPS = 1e-05

        def _ln(x, g, b):
            mu = jnp.mean(x, axis=-1, keepdims=True)
            var = jnp.mean((x - mu) ** 2, axis=-1, keepdims=True)
            return (x - mu) * jax.lax.rsqrt(var + EPS) * g + b
        b, s, d = x.shape
        h, dh = (HEADS, d // HEADS)
        xn = _ln(x, ln1_g, ln1_b)
        qkv = xn @ Wqkv + bqkv
        q, k, v = jnp.split(qkv, 3, axis=-1)
        q = q.reshape(b, s, h, dh)
        k = k.reshape(b, s, h, dh)
        v = v.reshape(b, s, h, dh)
        scores = jnp.einsum('bqhd,bkhd->bhqk', q, k) / jnp.sqrt(jnp.float32(dh))
        attn = jax.nn.softmax(scores, axis=-1)
        ctx = jnp.einsum('bhqk,bkhd->bqhd', attn, v).reshape(b, s, d)
        x = x + ctx @ Wo + bo
        xn2 = _ln(x, ln2_g, ln2_b)
        xt = xn2.reshape(b * s, d)
        probs = jax.nn.softmax(xt @ gate_w, axis=-1)
        gate_val = jnp.max(probs, axis=-1, keepdims=True)
        expert_idx = jnp.argmax(probs, axis=-1)
        oh = jax.nn.one_hot(expert_idx, E, dtype=xt.dtype)
        xe = jnp.einsum('te,td->etd', oh, xt)
        he = jax.nn.gelu(jnp.einsum('etd,edf->etf', xe, W1) + b1[:, None, :], approximate=False)
        ye = jnp.einsum('etf,efd->etd', he, W2) + b2[:, None, :]
        moe_out = jnp.einsum('te,etd->td', oh, ye) * gate_val
        rm = jax.nn.gelu(xt @ rW1 + rb1, approximate=False) @ rW2 + rb2
        coef = jax.nn.softmax(xt @ coef_w + coef_b, axis=-1)
        ff = moe_out * coef[:, 0:1] + rm * coef[:, 1:2]
        return x + ff.reshape(b, s, d)
    x = L0_attn_x
    x = x + 0.5 * _L0_ffn_ref(_layernorm(x, axis=-1), L0_ffn_Wg, L0_ffn_W1, L0_ffn_b1, L0_ffn_W2, L0_ffn_b2)
    x = x + _L0_attn_ref(_layernorm(x, axis=-1), L0_attn_qkv_w, L0_attn_qkv_b, L0_attn_w1w, L0_attn_w2w, L0_attn_r1w, L0_attn_r2w, L0_attn_memv_w, L0_attn_memv_b, L0_attn_memg_w, L0_attn_memg_b, L0_attn_mem_scale, L0_attn_out_w, L0_attn_out_b)
    x = x + 0.5 * _L0_ffn_ref(_layernorm(x, axis=-1), L0_ffn_Wg, L0_ffn_W1, L0_ffn_b1, L0_ffn_W2, L0_ffn_b2)
    x = x + 0.5 * _L1_ffn_ref(_layernorm(x, axis=-1), L1_ffn_ln1_g, L1_ffn_ln1_b, L1_ffn_Wqkv, L1_ffn_bqkv, L1_ffn_Wo, L1_ffn_bo, L1_ffn_ln2_g, L1_ffn_ln2_b, L1_ffn_gate_w, L1_ffn_W1, L1_ffn_b1, L1_ffn_W2, L1_ffn_b2, L1_ffn_rW1, L1_ffn_rb1, L1_ffn_rW2, L1_ffn_rb2, L1_ffn_coef_w, L1_ffn_coef_b)
    x = x + _L1_attn_ref(_layernorm(x, axis=-1), L1_attn_q_w, L1_attn_q_b, L1_attn_k_w, L1_attn_k_b, L1_attn_v_w, L1_attn_v_b, L1_attn_o_w, L1_attn_o_b)
    x = x + 0.5 * _L1_ffn_ref(_layernorm(x, axis=-1), L1_ffn_ln1_g, L1_ffn_ln1_b, L1_ffn_Wqkv, L1_ffn_bqkv, L1_ffn_Wo, L1_ffn_bo, L1_ffn_ln2_g, L1_ffn_ln2_b, L1_ffn_gate_w, L1_ffn_W1, L1_ffn_b1, L1_ffn_W2, L1_ffn_b2, L1_ffn_rW1, L1_ffn_rb1, L1_ffn_rW2, L1_ffn_rb2, L1_ffn_coef_w, L1_ffn_coef_b)
    return x

_drawn_inputs = setup_inputs


def setup_inputs(seed=0):
    import zlib

    import numpy as np

    out = dict(_drawn_inputs(seed))
    spreads = {'L0_attn_qkv_b': (0.0, 0.338),
     'L0_attn_memv_b': (0.0, 0.8),
     'L0_attn_memg_b': (0.0, 0.8),
     'L0_attn_mem_scale': (0.10000000149011612, 0.6),
     'L0_attn_out_b': (0.0, 0.1),
     'L0_ffn_b1': (0.0, 0.474),
     'L0_ffn_b2': (0.0, 0.1),
     'L1_ffn_ln1_g': (1.0, 0.6),
     'L1_ffn_ln1_b': (0.0, 0.8),
     'L1_ffn_bqkv': (0.0, 0.573),
     'L1_ffn_bo': (0.0, 0.1),
     'L1_ffn_ln2_g': (1.0, 0.6),
     'L1_ffn_ln2_b': (0.0, 0.8),
     'L1_ffn_b1': (0.0, 0.8),
     'L1_ffn_b2': (0.0, 0.8),
     'L1_ffn_rb1': (0.0, 0.8),
     'L1_ffn_rb2': (0.0, 0.267),
     'L1_ffn_coef_b': (0.0, 0.8)}
    factors = {'L0_attn_qkv_w': 8.0,
     'L0_attn_w1w': 8.0,
     'L0_attn_w2w': 8.0,
     'L0_attn_r1w': 25.101,
     'L0_attn_r2w': 31.673,
     'L0_attn_memv_w': 2.793,
     'L0_attn_memg_w': 8.0,
     'L1_attn_q_w': 4.928,
     'L1_attn_q_b': 8.0,
     'L1_attn_k_w': 4.901,
     'L1_attn_k_b': 64.0,
     'L1_attn_v_b': 2.827,
     'L1_ffn_Wqkv': 8.0,
     'L1_ffn_Wo': 3.837,
     'L1_ffn_gate_w': 8.0,
     'L1_ffn_W1': 8.0,
     'L1_ffn_W2': 8.0,
     'L1_ffn_rW1': 3.543,
     'L1_ffn_rW2': 3.149,
     'L1_ffn_coef_w': 8.0}
    for name, (base, spread) in spreads.items():
        noise = np.random.default_rng([zlib.crc32(name.encode()), seed]).standard_normal(out[name].shape)
        drawn = base * np.exp(spread * noise) if base else spread * noise
        out[name] = jnp.asarray(drawn.astype(out[name].dtype))
    for name, factor in factors.items():
        out[name] = (out[name] * factor).astype(out[name].dtype)
    return out
```

```python
from contextlib import ExitStack

import numpy as np

import concourse.bass as bass
from concourse import mybir

ALU = mybir.AluOpType
ACT = mybir.ActivationFunctionType
AX_X = mybir.AxisListType.X
F32 = mybir.dt.float32
BF16 = mybir.dt.bfloat16

P = 128
BATCH, SEQ, DIM = 2, 1024, 128
TB = SEQ // P
NT = BATCH * TB
HEADS, DH = 16, DIM // 16
WIN = 32
PADDED = SEQ + 2 * WIN
SPAN = P + 2 * WIN
WCH = SPAN // 2
EXPERTS, FFN = 8, 512
FC = FFN // P
BLK = 512
NBLK = BATCH * SEQ // BLK
CAPACITY = 2 * 2 * BATCH * SEQ // EXPERTS
PARTS = 3
ROWS = 6 * DH
MAXROW = 32
STACK = ROWS + PARTS
SCALE = float(DH) ** -0.5
EPS = 1e-5
LINE = 6
PHI = LINE * LINE
DECAY = 0.99
PAIRS = [(0, 1), (0, 2), (0, 3), (1, 2), (1, 3), (2, 3)]
JOBS = BATCH * HEADS // 2
Q_PART = [0, 0, 1, 0, 2, 1]
K_PART = [0, 1, 0, 2, 0, 1]

CONST_COLS = {"ident": P, "decay_root": P, "decay_next": P, "rank": EXPERTS, "same_head": HEADS}
MASK_COLS = {"ident": P, "before": P, "ones": P, "later_key": P, "later_query": P, "window_keys": SPAN,
             "window_queries": 2 * P}
VEC = {"f0_b1": 0, "f1_b1": 32, "rb1": 64, "a0_b": 68, "f1_b": 71, "ln1_g": 74, "ln1_b": 75, "ln2_g": 76,
       "ln2_b": 77, "a1_qb": 78, "a1_kb": 79}
ROW = {"a0_vb": (0, 128), "f1_vb": (128, 128), "a1_vb": (256, 128), "a0_ob": (384, 128), "f1_ob": (512, 128),
       "a1_ob": (640, 128), "memv_b": (768, 128), "memg_b": (896, 16), "mem_scale": (912, 16), "coef_b": (928, 2)}


def offsets(cols):
    out, at = {}, 0
    for name, n in cols.items():
        out[name] = (at, n)
        at += n
    return out, at


def schedule(steps, maxes, with_b, with_a):
    slots = {}
    if with_a:
        for a in range(maxes):
            slots.setdefault(a * 3 // 2 if with_b else a, []).append(("max", a))
        end = maxes * 3 // 2 if with_b else maxes
        slots.setdefault(end, []).append(("split", 0))
        slots.setdefault(min(end + 2, 2 * steps - 1) if with_b else end, []).append(("rows", 0))
    out = []
    if not with_b:
        for k in sorted(slots):
            out += slots[k]
        return out
    for s in range(steps):
        out.append(("scores", s))
        out += slots.get(2 * s, [])
        if s:
            out.append(("values", s - 1))
        out += slots.get(2 * s + 1, [])
    out.append(("values", steps - 1))
    return out


class Mode:
    def __init__(self, kind):
        self.kind = kind
        self.steps = 4 if kind == "window" else 2 * TB
        self.maxes = self.steps
        self.per_head = self.steps // 2
        self.items = self.maxes + 1


class Count:

    v = s = a = g = o = u = w0 = w1 = xn = xt = coef = coefT = picks = vp = aot = jobs = 0
    stored = parts = s_in = step = var = std = gate = gexp = bias1 = 0


def build(nc, d, out, LAYERS=6):
    co, nconst = offsets(CONST_COLS)
    mo, nmask = offsets(MASK_COLS)
    MODES = [Mode("causal"), Mode("full"), Mode("window")]
    CAUSAL, FULL, WINDOW = MODES

    with ExitStack() as ctx:
        def sb(name, shape, dt=F32):
            return ctx.enter_context(nc.sbuf_tensor(name, shape, dt))

        def ps(name, shape):
            return ctx.enter_context(nc.psum_tensor(name, shape, F32))

        def sem(name):
            return ctx.enter_context(nc.semaphore(name))

        q_dram = nc.dram_tensor("q_stack_dram", (BATCH, HEADS, ROWS, SEQ), BF16, kind="Internal").ap()
        k_dram = nc.dram_tensor("k_stack_dram", (BATCH, HEADS, ROWS, PADDED), BF16, kind="Internal").ap()
        q_heads = q_dram.rearrange("b h r t -> (b h) r t")
        k_heads = k_dram.rearrange("b h r t -> (b h) r t")

        X = sb("X", [P, NT, DIM])
        LX = sb("LX", [P, NT, DIM])
        XN = sb("XN", [P, NT, DIM])
        XT = sb("XT", [P, BATCH, PADDED])
        stats = sb("stats", [P, NT, 6])
        mv = sb("mv", [P, NT, 2])
        std = sb("std", [P, NT])
        rstd = sb("rstd", [P, NT])

        const = sb("const", [P, nconst])
        masks = sb("masks", [P, nmask], BF16)
        mask_in = LX[:, :, :].rearrange("p t c -> p (t c)")[:, 0:nmask]
        valid = sb("valid", [1, PADDED])
        vec_rows = sb("vec_rows", [P, P])
        vec = sb("vec", [P, P])
        row = sb("row", [1, 930])
        b2_0 = sb("b2_0", [EXPERTS, DIM])
        b2_1 = sb("b2_1", [EXPERTS + 1, DIM])

        def C(name):
            return const[:, co[name][0]:co[name][0] + co[name][1]]

        def M(name):
            return masks[:, mo[name][0]:mo[name][0] + mo[name][1]]

        def R(name):
            return row[0:1, ROW[name][0]:ROW[name][0] + ROW[name][1]]

        ident, identb = C("ident"), M("ident")

        a0_qkv = sb("a0_qkv", [P, 3 * DIM])
        a0_out = sb("a0_out", [P, DIM])
        lines_w = sb("lines_w", [P, 4, 4 * HEADS])
        memv_w = sb("memv_w", [P, DIM])
        memg_w = sb("memg_w", [P, HEADS])
        f0_gate = sb("f0_gate", [P, EXPERTS])
        f1_qkv = sb("f1_qkv", [P, 3 * DIM])
        f1_out = sb("f1_out", [P, DIM])
        f1_gate = sb("f1_gate", [P, EXPERTS])
        coef_w = sb("coef_w", [P, 2])
        a1_raw = sb("a1_raw", [P, 4, DIM])
        a1_w = sb("a1_w", [P, 4, DIM])

        W1 = [sb(f"W1_{k}", [P, FFN]) for k in range(2)]
        W2 = [sb(f"W2_{k}", [P, FC, DIM]) for k in range(2)]
        bias1 = [sb(f"bias1_{k}", [P, FC]) for k in range(2)]
        hidden_all = sb("hidden", [P, 2, FC, BLK])
        hidden = [hidden_all[:, k] for k in range(2)]

        logits = sb("logits", [P, NT, EXPERTS])
        g = [sb(f"gate_{k}", [P, NT, EXPERTS]) for k in range(4)]
        pick1 = sb("pick1", [P, NT, EXPERTS])
        pick2 = sb("pick2", [P, NT, EXPERTS])
        pick1b = sb("pick1b", [P, NT, EXPERTS], BF16)
        pick2b = sb("pick2b", [P, NT, EXPERTS], BF16)
        s1 = sb("s1", [P, 12, NT])
        coef2 = sb("coef2", [P, NT, 2])
        coefe = sb("coefe", [P, NT, 2])
        coef = sb("coef", [P, EXPERTS + 1, NT])
        memval = sb("memval", [P, NT, DIM])
        coefT = memval[0:EXPERTS + 1].rearrange("e t c -> e (t c)")

        Qp = [sb(f"Qp_{k}", [P, BATCH, SEQ], BF16) for k in range(PARTS)]
        Kp = [sb(f"Kp_{k}", [P, BATCH, PADDED], BF16) for k in range(PARTS)]
        rest = sb("rest", [P, BLK])
        QS = [sb(f"QS_{k}", [P, SEQ], BF16) for k in range(2)]
        KS = [sb(f"KS_{k}", [P, PADDED], BF16) for k in range(2)]
        V = sb("V", [P, BATCH * HEADS, TB, DH + 1])
        VW_all = sb("VW", [P, BATCH * HEADS * TB * 2 * (DH + 1)])
        VW = VW_all[0:WCH, :].rearrange("p (b t c d) -> p b t c d", b=BATCH * HEADS, t=TB, c=2)
        PT_all = sb("PT", [P, 2, SEQ])
        PT = [PT_all[:, k, :] for k in range(2)]
        negmax = sb("negmax", [P, 2 * TB])
        negrest = sb("negrest", [P, 2 * TB])
        negparts = sb("negparts", [P, 2 * TB, PARTS], BF16)
        rden = sb("rden", [P, TB])
        AO = sb("AO", [P, TB, BATCH * HEADS, DH])
        AOT = sb("AOT", [P, NT * P])

        pts = hidden_all[:, :, :, :].rearrange("p k c b -> p (k c b)")\
            .rearrange("p (t g h c) -> p t g h c", t=NT, g=4, h=HEADS)
        n_line = NT * HEADS * LINE
        Lw, Lr, sq = (VW_all[:, k * n_line:(k + 1) * n_line].rearrange("p (t h c) -> p t h c", t=NT, h=HEADS)
                      for k in range(3))
        prod = [sb(f"prod_{k}", [P, NT, HEADS]) for k in range(2)]
        norm = sb("norm", [P, NT, HEADS])
        rnorm = [sb(f"rnorm_{k}", [P, NT, HEADS]) for k in range(2)]
        LT = [sb(f"LT_{k}", [HEADS * LINE, 2, P]) for k in range(2)]
        JM = [LX[0:HEADS * LINE, :, :], AOT[0:HEADS * LINE, :].rearrange("p (h s) -> p h s", h=HEADS)]
        phiR = [sb(f"phiR_{k}", [P, HEADS, PHI]) for k in range(2)]
        phiJ = [sb(f"phiJ_{k}", [P, HEADS, PHI]) for k in range(2)]
        far = sb("far", [P, HEADS, PHI])
        farp = sb("farp", [P, HEADS // 2, PHI])
        near = [PT[0][:, k * BLK:(k + 1) * BLK].rearrange("p (h s) -> p h s", h=4) for k in range(2)]
        near2 = [PT[1][:, k * BLK:(k + 1) * BLK].rearrange("p (h s) -> p h s", h=4) for k in range(2)]
        score_in = sb("score_in", [P, NT, HEADS])
        score_far = sb("score_far", [P, NT, HEADS])
        gates = sb("gates", [P, NT, HEADS])
        scale16 = sb("scale16", [P, HEADS])
        gated = sb("gated", [P, NT])

        pA = ps("pA", [P, 2 * BLK])
        pS = [ps(f"pS_{k}", [P, 2 * BLK]) for k in range(2)]
        pO = [ps(f"pO_{k}", [P, BLK]) for k in range(2)]

        loaded = sem("loaded")
        x_loaded = sem("x_loaded")
        set_up = sem("set_up")
        consts_done = sem("consts_done")
        vec_done = sem("vec_done")
        v_ready, v_free = sem("v_ready"), sem("v_free")
        s_ready, s_free = sem("s_ready"), sem("s_free")
        dve_step, pool_step = sem("dve_step"), sem("pool_step")
        var_ready, std_ready = sem("var_ready"), sem("std_ready")
        xn_ready, xt_ready = sem("xn_ready"), sem("xt_ready")
        gate_in, gate_exp = sem("gate_in"), sem("gate_exp")
        picks_ready, coef_ready, coefT_ready = sem("picks_ready"), sem("coef_ready"), sem("coefT_ready")
        w_in = [sem(f"w_in_{k}") for k in range(2)]
        h_ready, gelu_done = sem("h_ready"), sem("gelu_done")
        y_done, y_free = sem("y_done"), sem("y_free")
        bias1_ready = sem("bias1_ready")
        parts_ready, stack_stored = sem("parts_ready"), sem("stack_stored")
        stack_in = [sem(f"stack_in_{k}") for k in range(2)]
        rows_clear = sem("rows_clear")
        a_ready, a_free = sem("a_ready"), sem("a_free")
        negparts_ready = sem("negparts_ready")
        st_ready, exp_done, pt_free = sem("st_ready"), sem("exp_done"), sem("pt_free")
        o_free = sem("o_free")
        v_in_place = sem("v_in_place")
        ao_ready, aot_ready = sem("ao_ready"), sem("aot_ready")
        pts_ready, lines_ready = sem("pts_ready"), sem("lines_ready")
        sq_ready, norm_in, norm_out, rnorm_ready = sem("sq_ready"), sem("norm_in"), sem("norm_out"), sem("rnorm_ready")
        lt_ready, jm_ready, phi_ready, phi_used = sem("lt_ready"), sem("jm_ready"), sem("phi_ready"), sem("phi_used")
        near2_ready = sem("near2_ready")
        sig_in, sig_out = sem("sig_in"), sem("sig_out")
        x_final, out_stored = sem("x_final"), sem("out_stored")

        x_tok = d["L0_attn_x"].rearrange("b (i p) c -> p (b i) c", p=P)
        out_tok = out.rearrange("b (i p) c -> p (b i) c", p=P)

        SYNC_LOADS = [
            (const[:, :], d["consts"][:, 0:nconst]),
            (mask_in[:, :], d["mask_consts"]),
            (valid[:, :], d["valid"]),
            (f0_gate[:, :], d["L0_ffn_Wg"]),
            (vec_rows[0:32, :], d["L0_ffn_b1"].rearrange("e (c p) -> (e c) p", p=P)),
            (vec_rows[32:64, :], d["L1_ffn_b1"].rearrange("e (c p) -> (e c) p", p=P)),
            (vec_rows[64:68, :], d["L1_ffn_rb1"].rearrange("(c p) -> c p", p=P)),
            (vec_rows[68:71, :], d["L0_attn_qkv_b"].rearrange("(c p) -> c p", p=P)),
            (vec_rows[71:74, :], d["L1_ffn_bqkv"].rearrange("(c p) -> c p", p=P)),
            (vec_rows[74:75, :], d["L1_ffn_ln1_g"].unsqueeze(0)),
            (vec_rows[75:76, :], d["L1_ffn_ln1_b"].unsqueeze(0)),
            (vec_rows[76:77, :], d["L1_ffn_ln2_g"].unsqueeze(0)),
            (vec_rows[77:78, :], d["L1_ffn_ln2_b"].unsqueeze(0)),
            (vec_rows[78:79, :], d["L1_attn_q_b"].unsqueeze(0)),
            (vec_rows[79:80, :], d["L1_attn_k_b"].unsqueeze(0)),
            (b2_0[:, :], d["L0_ffn_b2"]),
            (b2_1[0:EXPERTS, :], d["L1_ffn_b2"]),
            (b2_1[EXPERTS:EXPERTS + 1, :], d["L1_ffn_rb2"].unsqueeze(0)),
            (R("a0_vb"), d["L0_attn_qkv_b"].unsqueeze(0)[:, 2 * DIM:3 * DIM]),
            (R("f1_vb"), d["L1_ffn_bqkv"].unsqueeze(0)[:, 2 * DIM:3 * DIM]),
            (R("a1_vb"), d["L1_attn_v_b"].unsqueeze(0)),
            (R("a0_ob"), d["L0_attn_out_b"].unsqueeze(0)),
            (R("f1_ob"), d["L1_ffn_bo"].unsqueeze(0)),
            (R("a1_ob"), d["L1_attn_o_b"].unsqueeze(0)),
            (R("memv_b"), d["L0_attn_memv_b"].unsqueeze(0)),
            (R("memg_b"), d["L0_attn_memg_b"].unsqueeze(0)),
            (R("mem_scale"), d["L0_attn_mem_scale"].unsqueeze(0)),
            (R("coef_b"), d["L1_ffn_coef_b"].unsqueeze(0)),
            (a0_qkv[:, :], d["L0_attn_qkv_w"]),
            (a0_out[:, :], d["L0_attn_out_w"]),
            (lines_w[:, 0, :], d["L0_attn_w2w"]),
            (lines_w[:, 1, :], d["L0_attn_r1w"]),
            (lines_w[:, 2, :], d["L0_attn_r2w"]),
            (lines_w[:, 3, :], d["L0_attn_w1w"]),
            (memv_w[:, :], d["L0_attn_memv_w"]),
            (memg_w[:, :], d["L0_attn_memg_w"]),
            (f1_qkv[:, :], d["L1_ffn_Wqkv"]),
            (f1_out[:, :], d["L1_ffn_Wo"]),
            (f1_gate[:, :], d["L1_ffn_gate_w"]),
            (coef_w[:, :], d["L1_ffn_coef_w"]),
            (a1_raw[:, 0, :], d["L1_attn_q_w"]),
            (a1_raw[:, 1, :], d["L1_attn_k_w"]),
            (a1_raw[:, 2, :], d["L1_attn_v_w"]),
            (a1_raw[:, 3, :], d["L1_attn_o_w"]),
        ]
        ALL_LOADED = 16 * len(SYNC_LOADS)

        PLAN = [("moe", 0), ("attn", CAUSAL), ("moe", 0), ("l1", FULL), ("attn", WINDOW), ("l1", FULL)][:LAYERS]
        ATTN_OF = {
            "causal": dict(w=a0_qkv[:, :], wo=a0_out[:, :], qb=VEC["a0_b"], kb=VEC["a0_b"] + 1, vb="a0_vb", ob="a0_ob"),
            "full": dict(w=f1_qkv[:, :], wo=f1_out[:, :], qb=VEC["f1_b"], kb=VEC["f1_b"] + 1, vb="f1_vb", ob="f1_ob"),
            "window": dict(w=a1_w[:, 0:3, :].rearrange("p a b -> p (a b)"), wo=a1_w[:, 3, :], qb=VEC["a1_qb"],
                           kb=VEC["a1_kb"], vb="a1_vb", ob="a1_ob"),
        }

        def tile_cols(t, shift=0):
            at = WIN + t % TB * P + shift
            return XT[:, t // TB, at:at + P]

        def heads_of(t):
            return AO[:, t % TB, t // TB * HEADS:(t // TB + 1) * HEADS, :]

        def block_cols(k):
            at = WIN + k % 2 * BLK
            return XT[:, k // 2, at:at + BLK]

        WINDOW_S0 = 2 + 4 + 4 + (4 + 4 + NT // 2 + 4 + NT + 4)

        MEM_V0 = 1 + 7 + 2 * NBLK + 1

        def far_items(t):
            return 2 * sum(1 for u in range(t + 1) if u % TB)

        block = ctx.enter_context(nc.Block())

        @block.sync
        def _(sp):
            n = Count()
            sp.dma_start(X[:, :, :], x_tok).then_inc(x_loaded, 16)
            sp.wait_ge(set_up, 1)
            for dst, src in SYNC_LOADS:
                sp.dma_start(dst, src).then_inc(loaded, 16)

            def load_expert(w1, w2, k):
                sp.dma_start(W1[k][:, :], w1).then_inc(w_in[k], 16)
                sp.dma_start(W2[k][:, :, :], w2).then_inc(w_in[k], 16)

            def experts(layer):
                w1, w2 = d[f"L{layer}_ffn_W1"], d[f"L{layer}_ffn_W2"]

                def load(e, k):
                    load_expert(w1[bass.ds(e, 1)].rearrange("e c f -> (e c) f"),
                                w2[bass.ds(e, 1)].rearrange("e (c p) o -> (e p) c o", p=P), k)

                if n.u:
                    sp.wait_ge(y_done, n.u + 2)
                load(0, 0)
                load(1, 1)
                with sp.Fori(1, EXPERTS // 2) as i:
                    for k in range(2):
                        sp.wait_ge(y_done, n.u + 2 + NBLK * (2 * i + (k - 1)))
                        load(2 * i + k, k)
                n.u += NBLK * EXPERTS
                if layer:
                    sp.wait_ge(y_done, n.u + 2 - NBLK)
                    load_expert(d["L1_ffn_rW1"], d["L1_ffn_rW2"].rearrange("(c p) o -> p c o", p=P), 0)
                    n.u += NBLK

            def stacks(mode):
                S = mode.steps
                sp.wait_ge(parts_ready, n.parts + 1)
                for grp in range(6):
                    for b in range(BATCH):
                        sp.dma_start(q_dram[b, :, grp * DH:(grp + 1) * DH, :], Qp[Q_PART[grp]][:, b, :])\
                          .then_inc(stack_stored, 16)
                sp.wait_ge(parts_ready, n.parts + 2)
                for grp in range(6):
                    for b in range(BATCH):
                        sp.dma_start(k_dram[b, :, grp * DH:(grp + 1) * DH, :], Kp[K_PART[grp]][:, b, :])\
                          .then_inc(stack_stored, 16)
                n.parts += 2
                n.stored += 16 * 24
                sp.wait_ge(stack_stored, n.stored)

                def load(j, k):
                    for hh in range(2):
                        bh = 2 * j + hh
                        for dst, src in ((QS[k], q_heads), (KS[k], k_heads)):
                            for r0, r1, at in ((0, MAXROW, 0), (MAXROW, ROWS, MAXROW + PARTS)):
                                sp.dma_start(dst[64 * hh + at:64 * hh + at + r1 - r0, :],
                                             src[bass.ds(bh, 1), r0:r1, :].rearrange("a r t -> (a r) t"))\
                                  .then_inc(stack_in[k], 16)

                load(0, 0)
                load(1, 1)
                with sp.Fori(0, JOBS // 2 - 1) as i:
                    for k in range(2):
                        sp.wait_ge(pt_free, n.g + 2 + S * (2 * i + (k + 1)))
                        load(2 * i + (k + 2), k)
                n.g += S * JOBS
                n.s_in += 64 * JOBS
                sp.wait_ge(stack_in[0], n.s_in)
                sp.wait_ge(stack_in[1], n.s_in)

            for kind, arg in PLAN:
                if kind == "moe":
                    experts(0)
                elif kind == "attn":
                    stacks(arg)
                else:
                    stacks(arg)
                    experts(1)
            sp.wait_ge(x_final, 1)
            sp.dma_start(out_tok, X[:, :, :]).then_inc(out_stored, 16)
            sp.wait_ge(out_stored, 16)

        @block.gpsimd
        def _(pool):
            n = Count()

            def link(ins):
                n.step += 1
                ins.then_inc(pool_step, 1)
                pool.wait_ge(pool_step, n.step)

            pool.memset(vec_rows[:, :], 0.0).then_inc(set_up, 1)
            pool.memset(XT[:, :, 0:WIN], 0.0)
            pool.memset(XT[:, :, WIN + SEQ:PADDED], 0.0)
            for k in range(PARTS):
                pool.memset(Kp[k][:, :, 0:WIN], 0.0)
                pool.memset(Kp[k][:, :, WIN + SEQ:PADDED], 0.0)
            link(pool.memset(V[:, :, :, DH:DH + 1].rearrange("p b t d -> p (b t d)"), 1.0))
            for k in range(2):
                for hh in range(2):
                    at = 64 * hh + MAXROW
                    link(pool.memset(KS[k][at:at + PARTS, :], 1.0))
            pool.sem_inc(set_up, 1)

            def memory():
                pool.wait_ge(pts_ready, NT // 2)
                for which, (dst, i1, i2) in enumerate(((Lw, 3, 0), (Lr, 1, 2))):
                    for c, (a, b) in enumerate(PAIRS):
                        if which == 0 and c in (1, 4):
                            a, b = b, a
                        link(pool.tensor_tensor(prod[0][:, :, :], pts[:, :, i1, :, a], pts[:, :, i2, :, b], ALU.mult))
                        link(pool.tensor_tensor(prod[1][:, :, :], pts[:, :, i1, :, b], pts[:, :, i2, :, a], ALU.mult))
                        at = c if which else LINE - 1 - c
                        link(pool.tensor_tensor(dst[:, :, :, at], prod[0][:, :, :], prod[1][:, :, :], ALU.subtract))
                    if which:
                        pool.wait_ge(norm_in, 1)
                    pool.tensor_tensor(sq[:, :, :, :], dst[:, :, :, :], dst[:, :, :, :], ALU.mult).then_inc(sq_ready, 1)
                for which, dst in enumerate((Lw, Lr)):
                    pool.wait_ge(rnorm_ready, which + 1)
                    for half in range(2):
                        ts = slice(half * TB, (half + 1) * TB)
                        ins = pool.tensor_tensor(
                            dst[:, ts, :, :].rearrange("p t h c -> p (t h) c"),
                            dst[:, ts, :, :].rearrange("p t h c -> p (t h) c"),
                            rnorm[which][:, ts, :].rearrange("p t h -> p (t h)").unsqueeze(2)
                            .broadcast_to([P, TB * HEADS, LINE]), ALU.mult)
                    ins.then_inc(lines_ready, 1)
                pool.wait_ge(lines_ready, 2)
                used = 0
                for t in range(NT):
                    k = t % 2
                    if t % TB:
                        if used >= 2:
                            pool.wait_ge(phi_used, used - 1)
                        for src, dst, tt in ((Lr, phiR[used % 2], t), (Lw, phiJ[used % 2], t - 1)):
                            line = src[:, tt, :, :]
                            for half in range(2):
                                hs = slice(half * HEADS // 2, (half + 1) * HEADS // 2)
                                ins = pool.tensor_tensor(
                                    dst[:, hs, :].rearrange("p h (a b) -> p h a b", a=LINE),
                                    line[:, hs, :].unsqueeze(3).broadcast_to([P, HEADS // 2, LINE, LINE]),
                                    line[:, hs, :].unsqueeze(2).broadcast_to([P, HEADS // 2, LINE, LINE]), ALU.mult)
                        ins.then_inc(phi_ready, 1)
                        used += 1
                        pool.wait_ge(phi_ready, used)
                    pool.wait_ge(lt_ready, t + 1)
                    if t >= 2:
                        pool.wait_ge(v_ready, MEM_V0 + (t - 2) * 4 + far_items(t - 2) + 4)
                    nl = HEADS * LINE
                    pool.tensor_tensor(JM[k][:, :, :], LT[k][:, 1, :].unsqueeze(1).broadcast_to([nl, HEADS, P]),
                                       C("same_head")[0:nl, :].unsqueeze(2).broadcast_to([nl, HEADS, P]), ALU.mult)\
                        .then_inc(jm_ready, 1)
                    pool.wait_ge(jm_ready, t + 1)

            for kind, arg in PLAN:
                if kind == "attn" and arg is CAUSAL:
                    memory()
                if arg is WINDOW:
                    pool.wait_ge(s_ready, WINDOW_S0)
                    pool.memset(VW[:, :, :, :, DH:DH + 1].rearrange("p b t c d -> p (b t c d)"), 1.0).then_inc(set_up, 1)

        @block.tensor
        def _(pe):
            n = Count()

            def v_bank():
                k = n.v
                n.v += 1
                pe.wait_ge(v_free, k + 1)
                return pA[:, k % 2 * BLK:(k % 2 + 1) * BLK]

            def s_bank():
                k = n.s
                n.s += 1
                pe.wait_ge(s_free, k + 1)
                return pO[k % 2][:, :]

            def turn4(src, ready=None):
                bank = s_bank()
                for q, a in enumerate(src):
                    ins = pe.transpose(bank[:, q * P:(q + 1) * P], a, ident)
                ins.then_inc(s_ready, 1)

            def norm_turn():
                for q in range(4):
                    pe.wait_ge(xn_ready, n.xn + q + 1)
                    turn4([XN[:, 4 * q + r, :] for r in range(4)])
                n.xn += 4
                n.xt += 4

            def wait_xt():
                pe.wait_ge(xt_ready, n.xt)

            def gate(layer):
                wait_xt()
                bank = v_bank()
                wg = f1_gate if layer else f0_gate
                for t in range(NT):
                    ins = pe.matmul(bank[:, t * EXPERTS:(t + 1) * EXPERTS], tile_cols(t), wg[:, :], start=True, stop=True)
                if layer:
                    for t in range(NT):
                        o = bank[:, P + 2 * t:P + 2 * t + 2]
                        pe.matmul(o, tile_cols(t), coef_w[:, :], start=True, stop=False)
                        ins = pe.matmul(o, valid[0:1, WIN:WIN + P], R("coef_b"), start=False, stop=True)
                ins.then_inc(v_ready, 1)
                if not layer:
                    pe.wait_ge(picks_ready, n.picks + 1)
                    n.picks += 1
                    for which, pick in enumerate((pick1b, pick2b)):
                        bank = v_bank()
                        ins = pe.matmul(bank[:, 0:NT * EXPERTS], M("before"), pick[:, :, :].rearrange("p t e -> p (t e)"),
                                        start=True, stop=False, skip_group_check=True)
                        for t in range(NT - 1):
                            k = NT - 1 - t
                            ins = pe.matmul(bank[:, (t + 1) * EXPERTS:NT * EXPERTS].rearrange("p (t e) -> p t e", t=k),
                                            M("ones"), pick[:, t, :].unsqueeze(1).broadcast_to([P, k, EXPERTS]),
                                            start=False, stop=(which == 0 and t == NT - 2), skip_group_check=True)
                        if which:
                            for t in range(NT):
                                ins = pe.matmul(bank[:, 0:NT * EXPERTS].rearrange("p (t e) -> p t e", t=NT), M("ones"),
                                                pick1b[:, t, :].unsqueeze(1).broadcast_to([P, NT, EXPERTS]),
                                                start=False, stop=(t == NT - 1), skip_group_check=True)
                        ins.then_inc(v_ready, 1)
                ne = EXPERTS + (1 if layer else 0)
                pe.wait_ge(coef_ready, n.coef + 1)
                n.coef += 1
                for q in range(4):
                    bank = s_bank()
                    for r in range(4):
                        ins = pe.matmul(bank[0:ne, r * P:(r + 1) * P], coef[:, 0:ne, 4 * q + r], ident, start=True, stop=True)
                    ins.then_inc(s_ready, 1)
                b2 = b2_1 if layer else b2_0
                for q in range(4):
                    n.coefT += 1
                    pe.wait_ge(coefT_ready, n.coefT)
                    bank = v_bank()
                    for r in range(4):
                        t = 4 * q + r
                        ins = pe.matmul(bank[:, r * P:(r + 1) * P], coefT[0:ne, t * P:(t + 1) * P], b2[0:ne, :],
                                        start=True, stop=True)
                    ins.then_inc(v_ready, 1)

            def up(k, u, blk):
                for c in range(FC):
                    pe.wait_ge(gelu_done, FC * u + (c + 1))
                    pe.matmul(pS[c // 2][:, c % 2 * BLK:(c % 2 + 1) * BLK], W1[k][:, c * P:(c + 1) * P],
                              block_cols(blk), start=True, stop=True).then_inc(h_ready, 1)

            def down(k, u, blk):
                pe.wait_ge(gelu_done, FC * u + 2 * FC)
                pe.wait_ge(y_free, u + 1)
                y = pO[blk % 2]
                for r in range(4):
                    for c in range(FC):
                        ins = pe.matmul(y[:, r * P:(r + 1) * P], hidden[blk % 2][:, c, r * P:(r + 1) * P], W2[k][:, c, :],
                                        start=(c == 0), stop=(c == FC - 1))
                ins.then_inc(y_done, 1)

            def expert_units(uses, u0):
                units = [(k, b) for k in range(len(uses)) for b in range(NBLK)]
                for m, (k, b) in enumerate(units):
                    if b == 0:
                        pe.wait_ge(w_in[k], 32 * uses[k] + 32)
                    up(k, u0 + m, b)
                    if m:
                        down(units[m - 1][0], u0 + (m - 1), units[m - 1][1])
                down(units[-1][0], u0 + (len(units) - 1), units[-1][1])

            def experts(layer):
                pe.wait_ge(s_free, n.s + 2)
                with pe.Fori(0, EXPERTS // 2) as i:
                    expert_units([n.w0 + i, n.w1 + i], n.u + 2 * NBLK * i)
                n.u += NBLK * EXPERTS
                n.w0 += EXPERTS // 2
                n.w1 += EXPERTS // 2
                if layer:
                    expert_units([n.w0], n.u)
                    n.u += NBLK
                    n.w0 += 1
                pe.wait_ge(y_free, n.u + 2)

            def project(mode):
                a = ATTN_OF[mode.kind]
                w = a["w"]
                wait_xt()
                for which in range(2):
                    for b in range(NBLK):
                        bank = v_bank()
                        pe.matmul(bank, w[:, which * DIM:(which + 1) * DIM], block_cols(b), start=True, stop=True)\
                          .then_inc(v_ready, 1)
                wv = w[:, 2 * DIM:3 * DIM]
                if mode.kind == "window":
                    pe.wait_ge(set_up, 3)
                    for bi in range(0, NT, 2):
                        bank = s_bank()
                        for q in range(4):
                            b, at = bi // TB, (bi % TB + q // 2) * P + q % 2 * WCH
                            o = bank[0:WCH, q * P:(q + 1) * P]
                            pe.matmul(o, XT[:, b, at:at + WCH], wv, start=True, stop=False)
                            ins = pe.matmul(o, valid[0:1, at:at + WCH], R(a["vb"]), start=False, stop=True)
                        ins.then_inc(s_ready, 1)
                        n.vp += 1
                else:
                    for q in range(4):
                        bank = s_bank()
                        for r in range(4):
                            o = bank[:, r * P:(r + 1) * P]
                            pe.matmul(o, tile_cols(4 * q + r), wv, start=True, stop=False)
                            ins = pe.matmul(o, valid[0:1, WIN:WIN + P], R(a["vb"]), start=False, stop=True)
                        ins.then_inc(s_ready, 1)
                        n.vp += 1

            def max_part(mode, k, a):
                hh, q = divmod(a, mode.per_head)
                r = slice(64 * hh, 64 * hh + STACK)
                if mode.kind == "window":
                    for half in range(2):
                        for m in range(2):
                            t = 4 * q + 2 * half + m
                            o = pA[:, half * BLK + m * SPAN:half * BLK + (m + 1) * SPAN]
                            pe.matmul(o, QS[k][r, t * P:(t + 1) * P], KS[k][r, t * P:t * P + SPAN],
                                      start=(m == 0), stop=False, skip_group_check=True)
                        o = pA[:, half * BLK:half * BLK + 2 * SPAN].rearrange("p (m s) -> p m s", m=2)
                        ins = pe.matmul(o, identb, M("window_keys").unsqueeze(1).broadcast_to([P, 2, SPAN]),
                                        start=False, stop=True, skip_group_check=True)
                    return ins
                width = (q + 1) * P if mode.kind == "causal" else SEQ
                for at in range(0, width, BLK):
                    w = min(BLK, width - at)
                    ins = pe.matmul(pA[:, at:at + w], QS[k][r, q * P:(q + 1) * P], KS[k][r, WIN + at:WIN + at + w],
                                    start=True, stop=(mode.kind == "full"), skip_group_check=True)
                if mode.kind == "causal":
                    ins = pe.matmul(pA[:, width - P:width], identb, M("later_key"), start=False, stop=True,
                                    skip_group_check=True)
                return ins

            def score_part(mode, k, s):
                hh, q = divmod(s, mode.per_head)
                r = slice(64 * hh, 64 * hh + STACK)
                o = pS[s % 2]
                if mode.kind == "window":
                    for c in range(2):
                        for m in range(4):
                            t = 4 * q + m
                            pe.matmul(o[0:WCH, c * BLK + m * P:c * BLK + (m + 1) * P],
                                      KS[k][r, t * P + c * WCH:t * P + (c + 1) * WCH], QS[k][r, t * P:(t + 1) * P],
                                      start=(m == 0), stop=False, skip_group_check=True)
                        wm = M("window_queries")[0:WCH, c * P:(c + 1) * P]
                        ins = pe.matmul(o[0:WCH, c * BLK:(c + 1) * BLK].rearrange("p (m t) -> p m t", m=4),
                                        identb[0:WCH, 0:WCH], wm.unsqueeze(1).broadcast_to([WCH, 4, P]),
                                        start=False, stop=True, skip_group_check=True)
                    return ins
                first = q * P if mode.kind == "causal" else 0
                width = SEQ - first
                for at in range(0, width, BLK):
                    w = min(BLK, width - at)
                    ins = pe.matmul(o[:, at:at + w], KS[k][r, WIN + q * P:WIN + (q + 1) * P],
                                    QS[k][r, first + at:first + at + w],
                                    start=True, stop=(mode.kind == "full"), skip_group_check=True)
                if mode.kind == "causal":
                    ins = pe.matmul(o[:, 0:P], identb, M("later_query"), start=False, stop=True, skip_group_check=True)
                return ins

            def value_part(mode, k, j, s):
                hh, q = divmod(s, mode.per_head)
                o = pO[hh]
                bh = bass.ds(2 * j + hh, 1)
                if mode.kind == "window":
                    for m in range(4):
                        t = 4 * q + m
                        for c in range(2):
                            ins = pe.matmul(o[:, t * (DH + 1):(t + 1) * (DH + 1)],
                                            PT[s % 2][0:WCH, c * BLK + m * P:c * BLK + (m + 1) * P],
                                            VW[:, bh, t, c, :].rearrange("p a b -> p (a b)"),
                                            start=(t == 0 and c == 0), stop=(t == TB - 1 and c == 1),
                                            skip_group_check=True)
                    return ins
                first = q if mode.kind == "causal" else 0
                for t in range(first, TB):
                    ins = pe.matmul(o[:, t * (DH + 1):(t + 1) * (DH + 1)], PT[s % 2][:, (t - first) * P:(t - first + 1) * P],
                                    V[:, bh, q, :].rearrange("p a b -> p (a b)"),
                                    start=(q == 0 and t == 0), stop=(q == TB - 1 and t == TB - 1), skip_group_check=True)
                return ins

            def job(mode, j, k, with_b, with_a):
                S, I = mode.steps, mode.items
                ja, ka = j + 1, 1 - k
                for what, s in schedule(S, mode.maxes, with_b, with_a):
                    if what == "scores":
                        if s == 0:
                            pe.wait_ge(a_free, n.a + 1 + I * j + I)
                        score_part(mode, k, s).then_inc(st_ready, 1)
                    elif what == "values":
                        pe.wait_ge(exp_done, n.g + S * j + (s + 1))
                        if s % mode.per_head == 0:
                            pe.wait_ge(o_free, n.o + 2 * j + (s // mode.per_head + 1))
                        value_part(mode, k, j, s).then_inc(pt_free, 1)
                    elif what == "max":
                        if s == 0:
                            pe.wait_ge(rows_clear, n.jobs + ja + 1)
                            pe.wait_ge(stack_in[ka], n.jobs * 64 + (ja + (2 - ka)) * 64)
                        pe.wait_ge(a_free, n.a + I * ja + (s + 1))
                        max_part(mode, ka, s).then_inc(a_ready, 1)
                    elif what == "rows":
                        pe.wait_ge(negparts_ready, n.jobs + ja + 1)
                        pe.wait_ge(a_free, n.a + I * ja + I)
                        for hh in range(2):
                            for t in range(TB):
                                at = 64 * hh + MAXROW
                                ins = pe.matmul(pA[at:at + PARTS, t * P:(t + 1) * P], negparts[:, hh * TB + t, :], identb,
                                                start=True, stop=True)
                        ins.then_inc(a_ready, 1)

            def attention(mode):
                pe.wait_ge(v_free, n.v + 2)
                pe.wait_ge(s_free, n.s + 2)
                pe.wait_ge(v_in_place, n.vp)
                job(mode, -1, 1, False, True)
                with pe.Fori(0, JOBS // 2 - 1) as i:
                    job(mode, 2 * i, 0, True, True)
                    job(mode, 2 * i + 1, 1, True, True)
                job(mode, JOBS - 2, 0, True, True)
                job(mode, JOBS - 1, 1, True, False)
                n.a += mode.items * JOBS
                n.g += mode.steps * JOBS
                n.o += 2 * JOBS
                n.jobs += JOBS
                pe.wait_ge(a_free, n.a + 1)
                pe.wait_ge(o_free, n.o + 2)

            def out_proj(mode):
                a = ATTN_OF[mode.kind]
                if mode.kind == "causal":
                    pe.wait_ge(ao_ready, 1)
                for q in range(4):
                    turn4([heads_of(4 * q + r).rearrange("p h d -> p (h d)") for r in range(4)])
                for q in range(4):
                    n.aot += 1
                    pe.wait_ge(aot_ready, n.aot)
                    bank = v_bank()
                    for r in range(4):
                        t = 4 * q + r
                        o = bank[:, r * P:(r + 1) * P]
                        pe.matmul(o, AOT[:, t * P:(t + 1) * P], a["wo"], start=True, stop=False)
                        ins = pe.matmul(o, valid[0:1, WIN:WIN + P], R(a["ob"]), start=False, stop=True)
                    ins.then_inc(v_ready, 1)

            def memory():
                wait_xt()
                for q in range(NT // 2):
                    bank = s_bank()
                    for r in range(2):
                        t = 2 * q + r
                        pe.matmul(bank[:, r * 256:r * 256 + 192], tile_cols(t),
                                  lines_w[:, 0:3, :].rearrange("p a b -> p (a b)"), start=True, stop=True)
                        ins = pe.matmul(bank[:, r * 256 + 192:(r + 1) * 256], tile_cols(t, -1), lines_w[:, 3, :],
                                        start=True, stop=True)
                    ins.then_inc(s_ready, 1)
                for q in range(4):
                    bank = s_bank()
                    for r in range(4):
                        o = bank[:, r * P:(r + 1) * P]
                        pe.matmul(o, tile_cols(4 * q + r), memv_w[:, :], start=True, stop=False)
                        ins = pe.matmul(o, valid[0:1, WIN:WIN + P], R("memv_b"), start=False, stop=True)
                    ins.then_inc(s_ready, 1)
                bank = v_bank()
                for t in range(NT):
                    o = bank[:, t * HEADS:(t + 1) * HEADS]
                    pe.matmul(o, tile_cols(t), memg_w[:, :], start=True, stop=False)
                    ins = pe.matmul(o, valid[0:1, WIN:WIN + P], R("memg_b"), start=False, stop=True)
                ins.then_inc(v_ready, 1)

            def memory_scores():
                pe.wait_ge(lines_ready, 2)
                assert n.v == MEM_V0, n.v
                nl = HEADS * LINE
                used = 0

                def turn(t):
                    bank = s_bank()
                    for m, src in enumerate((Lr, Lw)):
                        ins = pe.transpose(bank[0:nl, m * P:(m + 1) * P],
                                           src[:, t, :, :].rearrange("p h c -> p (h c)"), ident)
                    ins.then_inc(s_ready, 1)

                turn(0)
                for t in range(NT):
                    if t + 1 < NT:
                        turn(t + 1)
                    if t % TB:
                        pe.wait_ge(phi_ready, used + 1)
                        for half in range(2):
                            bank = v_bank()
                            hs = slice(half * HEADS // 2, (half + 1) * HEADS // 2)
                            pe.matmul(bank[:, 0:HEADS // 2 * PHI], C("decay_next"),
                                      phiJ[used % 2][:, hs, :].rearrange("p h c -> p (h c)"), start=True, stop=True)\
                              .then_inc(v_ready, 1)
                        used += 1
                    pe.wait_ge(jm_ready, t + 1)
                    for q in range(4):
                        bank = v_bank()
                        pe.matmul(bank, LT[t % 2][:, 0, :],
                                  JM[t % 2][:, 4 * q:4 * q + 4, :].rearrange("p h s -> p (h s)"), start=True, stop=True)\
                          .then_inc(v_ready, 1)

            pe.wait_ge(loaded, ALL_LOADED)
            bank = s_bank()
            pe.transpose(bank[:, 0:P], vec_rows[:, :], ident).then_inc(s_ready, 1)
            turn4([a1_raw[:, q, :] for q in range(4)])
            bank = v_bank()
            pe.matmul(bank[:, 0:HEADS], valid[0:1, WIN:WIN + P], R("mem_scale"), start=True, stop=True).then_inc(v_ready, 1)
            pe.wait_ge(set_up, 2)
            pe.wait_ge(vec_done, 2)
            pe.wait_ge(consts_done, 1)
            for kind, arg in PLAN:
                norm_turn()
                if kind == "moe":
                    gate(0)
                    experts(0)
                elif kind == "attn":
                    project(arg)
                    if arg is CAUSAL:
                        memory()
                        memory_scores()
                    attention(arg)
                    out_proj(arg)
                else:
                    project(arg)
                    attention(arg)
                    out_proj(arg)
                    norm_turn()
                    gate(1)
                    experts(1)

        @block.scalar
        def _(act):
            n = Count()
            act.sem_inc(s_free, 2)
            act.sem_inc(gelu_done, FC)

            def s_take():
                k = n.s
                n.s += 1
                act.wait_ge(s_ready, k + 1)
                return pO[k % 2][:, :]

            def norm_turn(gb=None):
                n.var += 1
                act.wait_ge(var_ready, n.var)
                act.activation(std[:, :], mv[:, :, 1], ACT.Sqrt).then_inc(std_ready, 1)
                for q in range(4):
                    bank = s_take()
                    b, at = q // 2, WIN + q % 2 * BLK
                    dst = XT[:, b, at:at + BLK]
                    if gb is None:
                        ins = act.activation(dst, bank[:, :], ACT.Copy)
                    else:
                        ins = act.activation(dst, bank[:, :], ACT.Identity, scale=vec[:, gb:gb + 1], bias=vec[:, gb + 1:gb + 2])
                    ins.then_inc(s_free, 1)
                    act.wait_ge(s_free, n.s + 2)
                    act.sem_inc(xt_ready, 1)

            def gate(layer):
                ne = EXPERTS + (1 if layer else 0)
                n.gate += 1
                act.wait_ge(gate_in, n.gate)
                act.activation(g[1][:, :, :], g[0][:, :, :], ACT.Exp).then_inc(gate_exp, 1)
                if layer:
                    n.gate += 1
                    act.wait_ge(gate_in, n.gate)
                    act.activation(coefe[:, :, :], coef2[:, :, :], ACT.Exp).then_inc(gate_exp, 1)
                for q in range(4):
                    bank = s_take()
                    act.activation(coefT[0:ne, q * BLK:(q + 1) * BLK], bank[0:ne, :], ACT.Copy).then_inc(s_free, 1)
                    act.wait_ge(s_free, n.s + 2)
                    act.sem_inc(coefT_ready, 1)

            def gelus(u, blk, k):
                act.wait_ge(y_done, u + 1)
                for c in range(FC):
                    act.wait_ge(h_ready, FC * u + (c + 1))
                    act.activation(hidden[blk % 2][:, c, :], pS[c // 2][:, c % 2 * BLK:(c % 2 + 1) * BLK], ACT.Gelu,
                                   bias=bias1[k][:, c:c + 1]).then_inc(gelu_done, 1)

            def experts(layer):
                act.preload_act_table(ACT.Gelu)
                with act.Fori(0, EXPERTS // 2) as i:
                    for k in range(2):
                        act.wait_ge(bias1_ready, n.bias1 + 2 * i + (k + 1))
                        for b in range(NBLK):
                            gelus(n.u + 2 * NBLK * i + (NBLK * k + b), b, k)
                n.u += NBLK * EXPERTS
                if layer:
                    act.wait_ge(bias1_ready, n.bias1 + EXPERTS + 1)
                    for b in range(NBLK):
                        gelus(n.u + b, b, 0)
                    n.u += NBLK
                n.bias1 += EXPERTS + 1

            def project(mode):
                if mode.kind == "window":
                    for bi in range(0, NT, 2):
                        bank = s_take()
                        b, t = bi // TB, bi % TB
                        for tt in range(2):
                            dst = VW[:, b * HEADS:(b + 1) * HEADS, t + tt, :, 0:DH].rearrange("p h c d -> p c h d")
                            src = bank[0:WCH, 2 * tt * P:2 * (tt + 1) * P].rearrange("p (c h d) -> p c h d", c=2, h=HEADS)
                            ins = act.activation(dst, src, ACT.Copy)
                        ins.then_inc(s_free, 1)
                        act.wait_ge(s_free, n.s + 2)
                        act.sem_inc(v_in_place, 1)
                else:
                    for q in range(4):
                        bank = s_take()
                        b, t = 4 * q // TB, 4 * q % TB
                        dst = V[:, b * HEADS:(b + 1) * HEADS, t:t + 4, 0:DH].rearrange("p h t d -> p t h d")
                        act.activation(dst, bank[:, :].rearrange("p (t h d) -> p t h d", t=4, h=HEADS), ACT.Copy)\
                           .then_inc(s_free, 1)
                        act.wait_ge(s_free, n.s + 2)
                        act.sem_inc(v_in_place, 1)

            def job(mode, j, with_b):
                S = mode.steps
                for what, s in schedule(S, mode.maxes, with_b, False):
                    if what == "scores":
                        act.wait_ge(st_ready, n.g + S * j + (s + 1))
                        act.wait_ge(pt_free, n.g + S * j + (s + 1))
                        if mode.kind == "window":
                            dst, src = PT[s % 2][0:WCH, :], pS[s % 2][0:WCH, :]
                        else:
                            w = SEQ - (s % mode.per_head * P if mode.kind == "causal" else 0)
                            dst, src = PT[s % 2][:, 0:w], pS[s % 2][:, 0:w]
                        act.activation(dst, src, ACT.Exp, scale=SCALE).then_inc(exp_done, 1)

            def attention(mode):
                with act.Fori(0, JOBS // 2 - 1) as i:
                    job(mode, 2 * i, True)
                    job(mode, 2 * i + 1, True)
                job(mode, JOBS - 2, True)
                job(mode, JOBS - 1, True)
                n.g += mode.steps * JOBS

            def out_proj(mode):
                for q in range(4):
                    bank = s_take()
                    act.activation(AOT[:, q * BLK:(q + 1) * BLK], bank[:, :], ACT.Copy).then_inc(s_free, 1)
                    act.wait_ge(s_free, n.s + 2)
                    act.sem_inc(aot_ready, 1)

            def memory():
                for q in range(NT // 2):
                    bank = s_take()
                    act.activation(pts[:, 2 * q:2 * q + 2, :, :, :].rearrange("p t g h c -> p (t g h c)"), bank[:, :], ACT.Copy)\
                       .then_inc(s_free, 1)
                    act.wait_ge(s_free, n.s + 2)
                    act.sem_inc(pts_ready, 1)
                for q in range(4):
                    bank = s_take()
                    act.activation(memval[:, 4 * q:4 * q + 4, :].rearrange("p t c -> p (t c)"), bank[:, :], ACT.Copy)\
                       .then_inc(s_free, 1)
                act.wait_ge(sig_in, 1)
                act.activation(gates[:, :, :], gates[:, :, :], ACT.Sigmoid).then_inc(sig_out, 1)
                for which in range(2):
                    act.wait_ge(norm_in, which + 1)
                    act.activation(norm[:, :, :], norm[:, :, :], ACT.Sqrt).then_inc(norm_out, 1)

            def memory_scores():
                def take(t):
                    bank = s_take()
                    if t >= 2:
                        act.wait_ge(v_ready, MEM_V0 + (t - 2) * 4 + far_items(t - 2) + 4)
                        act.wait_ge(jm_ready, t - 1)
                    act.activation(LT[t % 2][:, :, :].rearrange("p a b -> p (a b)"), bank[0:HEADS * LINE, 0:2 * P], ACT.Copy)\
                       .then_inc(s_free, 1)
                    act.wait_ge(s_free, n.s + 2)
                    act.sem_inc(lt_ready, 1)

                take(0)
                m = 0
                for t in range(NT):
                    if t + 1 < NT:
                        take(t + 1)
                    for q in range(4):
                        act.wait_ge(v_free, MEM_V0 + 4 * t + far_items(t) + q + 3)
                        act.activation(near2[m % 2][:, :, :], near[m % 2][:, :, :], ACT.Square).then_inc(near2_ready, 1)
                        m += 1
                act.wait_ge(sig_in, 2)
                act.activation(score_in[:, :, :], score_in[:, :, :], ACT.Sigmoid).then_inc(sig_out, 1)

            bank = s_take()
            act.activation(vec[:, :], bank[:, 0:P], ACT.Copy).then_inc(s_free, 1)
            bank = s_take()
            act.activation(a1_w[:, :, :].rearrange("p a b -> p (a b)"), bank[:, :], ACT.Copy).then_inc(s_free, 1)
            act.wait_ge(s_free, n.s + 2)
            act.sem_inc(vec_done, 2)
            for kind, arg in PLAN:
                if kind == "moe":
                    norm_turn()
                    gate(0)
                    experts(0)
                elif kind == "attn":
                    norm_turn()
                    project(arg)
                    if arg is CAUSAL:
                        memory()
                        memory_scores()
                    attention(arg)
                    out_proj(arg)
                else:
                    n.var += 1
                    act.wait_ge(var_ready, n.var)
                    act.activation(std[:, :], mv[:, :, 1], ACT.Sqrt).then_inc(std_ready, 1)
                    norm_turn(VEC["ln1_g"])
                    project(arg)
                    attention(arg)
                    out_proj(arg)
                    norm_turn(VEC["ln2_g"])
                    gate(1)
                    experts(1)

        @block.vector
        def _(dve):
            n = Count()

            def link(ins):
                n.step += 1
                ins.then_inc(dve_step, 1)
                dve.wait_ge(dve_step, n.step)

            def v_take():
                k = n.v
                n.v += 1
                dve.wait_ge(v_ready, k + 1)
                return pA[:, k % 2 * BLK:(k % 2 + 1) * BLK]

            def layer_norm(src, dst, signal=True):
                for t in range(NT):
                    ins = dve.bn_stats(stats[:, t, :], src[:, t, :])
                link(ins)
                for t in range(NT):
                    ins = dve.bn_aggr(mv[:, t, :], stats[:, t, :])
                link(ins)
                dve.tensor_scalar(mv[:, :, 1], mv[:, :, 1], EPS, None, ALU.add).then_inc(var_ready, 1)
                n.std += 1
                dve.wait_ge(std_ready, n.std)
                link(dve.reciprocal(rstd[:, :], std[:, :]))
                for t in range(NT):
                    ins = dve.tensor_scalar(dst[:, t, :], src[:, t, :], mv[:, t, 0:1], rstd[:, t:t + 1], ALU.subtract, ALU.mult)
                    if signal and t % 4 == 3:
                        ins.then_inc(xn_ready, 1)
                if not signal:
                    link(ins)

            def bc(ap, k):
                return ap.unsqueeze(2).broadcast_to([P, NT, k])

            def pick_largest(src, dst, m):
                link(dve.tensor_reduce(m, src, AX_X, ALU.max))
                link(dve.tensor_tensor(g[2][:, :, :], src, bc(m, EXPERTS), ALU.is_equal))
                link(dve.tensor_tensor(g[2][:, :, :], g[2][:, :, :], C("rank").unsqueeze(1).broadcast_to([P, NT, EXPERTS]),
                                       ALU.mult))
                link(dve.tensor_reduce(s1[:, 11, :], g[2][:, :, :], AX_X, ALU.max))
                link(dve.tensor_tensor(dst[:, :, :], g[2][:, :, :], bc(s1[:, 11, :], EXPERTS), ALU.is_equal))

            def gate(layer):
                bank = v_take()
                m1, m2, z, rz, e2, g2, den, rden2, w1, w2 = (s1[:, q, :] for q in range(10))
                ins = dve.tensor_copy(logits[:, :, :].rearrange("p t e -> p (t e)"), bank[:, 0:NT * EXPERTS])
                if layer:
                    ins = dve.tensor_copy(coef2[:, :, :].rearrange("p t e -> p (t e)"), bank[:, P:P + 2 * NT])
                ins.then_inc(v_free, 1)
                dve.wait_ge(v_free, n.v + 2)
                pick_largest(logits[:, :, :], pick1, m1)
                dve.tensor_tensor(g[0][:, :, :], logits[:, :, :], bc(m1, EXPERTS), ALU.subtract).then_inc(gate_in, 1)
                if layer:
                    link(dve.tensor_reduce(m2, coef2[:, :, :], AX_X, ALU.max))
                    dve.tensor_tensor(coef2[:, :, :], coef2[:, :, :], bc(m2, 2), ALU.subtract).then_inc(gate_in, 1)
                    n.gexp += 2
                    dve.wait_ge(gate_exp, n.gexp)
                    link(dve.tensor_reduce(z, g[1][:, :, :], AX_X, ALU.add))
                    link(dve.tensor_reduce(e2, coefe[:, :, :], AX_X, ALU.add))
                    link(dve.reciprocal(rz, z))
                    link(dve.reciprocal(g2, e2))
                    link(dve.tensor_scalar(g2, g2, 0.5, None, ALU.mult))
                    link(dve.tensor_tensor(w1, coefe[:, :, 0], g2, ALU.mult))
                    link(dve.tensor_tensor(w1, w1, rz, ALU.mult))
                    dve.tensor_tensor(coef[:, EXPERTS, :], coefe[:, :, 1], g2, ALU.mult)
                    dve.tensor_tensor(coef[:, 0:EXPERTS, :].rearrange("p e t -> p t e"), pick1[:, :, :], bc(w1, EXPERTS),
                                      ALU.mult).then_inc(coef_ready, 1)
                else:
                    link(dve.scalar_tensor_tensor(g[3][:, :, :], pick1[:, :, :], -3e38, logits[:, :, :], ALU.mult, ALU.add))
                    pick_largest(g[3][:, :, :], pick2, m2)
                    dve.tensor_copy(pick1b[:, :, :], pick1[:, :, :])
                    dve.tensor_copy(pick2b[:, :, :], pick2[:, :, :]).then_inc(picks_ready, 1)
                    n.gexp += 1
                    dve.wait_ge(gate_exp, n.gexp)
                    link(dve.tensor_reduce(z, g[1][:, :, :], AX_X, ALU.add))
                    link(dve.reciprocal(rz, z))
                    link(dve.tensor_tensor(g[2][:, :, :], pick2[:, :, :], g[1][:, :, :], ALU.mult))
                    link(dve.tensor_reduce(e2, g[2][:, :, :], AX_X, ALU.add))
                    link(dve.tensor_tensor(g2, e2, rz, ALU.mult))
                    link(dve.scalar_tensor_tensor(den, rz, 1e-9, g2, ALU.add, ALU.add))
                    link(dve.reciprocal(rden2, den))
                    link(dve.scalar_tensor_tensor(w1, rz, 0.5, rden2, ALU.mult, ALU.mult))
                    link(dve.scalar_tensor_tensor(w2, g2, 0.5, rden2, ALU.mult, ALU.mult))
                    for which, (pick, w) in enumerate(((pick1, w1), (pick2, w2))):
                        bank = v_take()
                        dve.scalar_tensor_tensor(g[2 + which][:, :, :].rearrange("p t e -> p (t e)"), bank[:, 0:NT * EXPERTS],
                                                 float(CAPACITY), pick[:, :, :].rearrange("p t e -> p (t e)"),
                                                 ALU.is_lt, ALU.mult).then_inc(v_free, 1)
                        dve.wait_ge(v_free, n.v + 2)
                        link(dve.tensor_tensor(g[2 + which][:, :, :], g[2 + which][:, :, :], bc(w, EXPERTS), ALU.mult))
                    dve.tensor_tensor(coef[:, 0:EXPERTS, :].rearrange("p e t -> p t e"), g[2][:, :, :], g[3][:, :, :],
                                      ALU.add).then_inc(coef_ready, 1)
                for q in range(4):
                    bank = v_take()
                    x4 = X[:, 4 * q:4 * q + 4, :].rearrange("p t c -> p (t c)")
                    dve.tensor_tensor(x4, bank, x4, ALU.add).then_inc(v_free, 1)
                dve.wait_ge(v_free, n.v + 2)

            def add_unit(u, blk, e):
                dve.wait_ge(y_done, u + 3)
                dve.wait_ge(y_free, u + 2)
                for r in range(4):
                    t = 4 * blk + r
                    ins = dve.scalar_tensor_tensor(X[:, t, :], pO[blk % 2][:, r * P:(r + 1) * P], coef[:, bass.ds(e, 1), t]
                                                   , X[:, t, :], ALU.mult, ALU.add)
                ins.then_inc(y_free, 1)

            def take_bias(k, at):
                dve.tensor_scalar(bias1[k][:, :], vec[:, bass.ds(at, FC)], 1.0, None, ALU.mult).then_inc(bias1_ready, 1)

            def experts(layer):
                base = VEC["f1_b1" if layer else "f0_b1"]
                take_bias(0, base)
                with dve.Fori(0, EXPERTS // 2) as i:
                    take_bias(1, base + 2 * FC * i + FC)
                    for m in range(2 * NBLK):
                        add_unit(n.u + 2 * NBLK * i + m, m % NBLK, 2 * i + m // NBLK)
                        if m == NBLK - 1:
                            take_bias(0, base + 2 * FC * i + 2 * FC)
                n.u += NBLK * EXPERTS
                if layer:
                    for m in range(NBLK):
                        add_unit(n.u + m, m, EXPERTS)
                    n.u += NBLK
                dve.wait_ge(y_free, n.u + 2)

            def project(mode):
                a = ATTN_OF[mode.kind]
                if n.stored:
                    dve.wait_ge(stack_stored, n.stored)
                n.stored += 16 * 24
                for which, (dst, off, bias) in enumerate(((Qp, 0, a["qb"]), (Kp, WIN, a["kb"]))):
                    for b in range(NBLK):
                        bank = v_take()
                        cols = [p[:, b // 2, off + b % 2 * BLK:off + (b % 2 + 1) * BLK] for p in dst]
                        bcol = vec[:, bias:bias + 1]
                        link(dve.tensor_scalar(cols[0], bank, bcol, None, ALU.add))
                        dve.scalar_tensor_tensor(rest[:, :], bank, bcol, cols[0], ALU.add, ALU.subtract).then_inc(v_free, 1)
                        dve.wait_ge(v_free, n.v + 2)
                        link(dve.tensor_copy(cols[1], rest[:, :]))
                        link(dve.tensor_tensor(cols[2], rest[:, :], cols[1], ALU.subtract))
                    dve.sem_inc(parts_ready, 1)

            def clear_rows(k):
                for hh in range(2):
                    ins = dve.memset(QS[k][64 * hh + MAXROW:64 * hh + MAXROW + PARTS, :], 0.0)
                ins.then_inc(rows_clear, 1)

            def job(mode, j, k, with_b, with_a, clear=False):
                S, I = mode.steps, mode.items
                ja, ka = j + 1, 1 - k
                c = 0
                base = n.step + 5 * ja - (2 if with_b else 0)
                for what, s in schedule(S, mode.maxes, with_b, with_a):
                    if what == "max":
                        dve.wait_ge(a_ready, n.a + I * ja + (s + 1))
                        hh, q = divmod(s, mode.per_head)
                        if mode.kind == "window":
                            src = pA[:, :].rearrange("p (b f) -> p b f", b=2)[:, :, 0:2 * SPAN]\
                                .rearrange("p b (m s) -> p b m s", m=2)
                            at = hh * TB + 4 * q
                            dst = negmax[:, at:at + 4].rearrange("p (b m) -> p b m", b=2)
                        else:
                            src = pA[:, 0:(q + 1) * P if mode.kind == "causal" else SEQ]
                            dst = negmax[:, hh * TB + q:hh * TB + q + 1]
                        dve.tensor_reduce(dst, src, AX_X, ALU.max, negate=True).then_inc(a_free, 1)
                    elif what == "split":
                        dve.wait_ge(a_free, n.a + 1 + I * ja + mode.maxes)
                        for m in range(PARTS):
                            if m == 0:
                                ins = dve.tensor_copy(negparts[:, :, 0], negmax[:, :])
                            elif m == 1:
                                c += 1
                                dve.tensor_tensor(negrest[:, :], negmax[:, :], negparts[:, :, 0], ALU.subtract)\
                                    .then_inc(dve_step, 1)
                                dve.wait_ge(dve_step, base + c)
                                ins = dve.tensor_copy(negparts[:, :, 1], negrest[:, :])
                            else:
                                dve.tensor_tensor(negparts[:, :, 2], negrest[:, :], negparts[:, :, 1], ALU.subtract)\
                                    .then_inc(negparts_ready, 1)
                            if m < 2:
                                c += 1
                                ins.then_inc(dve_step, 1)
                                dve.wait_ge(dve_step, base + c)
                    elif what == "rows":
                        dve.wait_ge(a_ready, n.a + I * ja + I)
                        for hh in range(2):
                            at = 64 * hh + MAXROW
                            ins = dve.tensor_copy(QS[ka][at:at + PARTS, :], pA[at:at + PARTS, 0:SEQ])
                        ins.then_inc(a_free, 1)
                    elif what == "values" and s % mode.per_head == mode.per_head - 1:
                        hh = s // mode.per_head
                        dve.wait_ge(o_free, n.o + 2 * j + (hh + 2))
                        dve.wait_ge(pt_free, n.g + S * j + (s + 3))
                        o = pO[hh][:, 0:TB * (DH + 1)].rearrange("p (t d) -> p t d", d=DH + 1)
                        c += 1
                        dve.reciprocal(rden[:, :], o[:, :, DH]).then_inc(dve_step, 1)
                        dve.wait_ge(dve_step, base + c)
                        dve.tensor_tensor(AO[:, :, bass.ds(2 * j + hh, 1), :].rearrange("p t a d -> p t (a d)"),
                                          o[:, :, 0:DH], rden[:, :].unsqueeze(2).broadcast_to([P, TB, DH]), ALU.mult)\
                            .then_inc(o_free, 1)
                if clear:
                    clear_rows(k)

            def attention(mode):
                clear_rows(0)
                clear_rows(1)
                job(mode, -1, 1, False, True)
                with dve.Fori(0, JOBS // 2 - 1) as i:
                    job(mode, 2 * i, 0, True, True, True)
                    job(mode, 2 * i + 1, 1, True, True, True)
                job(mode, JOBS - 2, 0, True, True)
                job(mode, JOBS - 1, 1, True, False)
                n.step += 3 + 5 * (JOBS - 1) + 2
                n.a += mode.items * JOBS
                n.g += mode.steps * JOBS
                n.o += 2 * JOBS
                dve.wait_ge(o_free, n.o + 2)

            def out_proj(mode):
                for q in range(4):
                    bank = v_take()
                    ts = slice(4 * q, 4 * q + 4)
                    x4, lx4, x1 = (a[:, ts, :].rearrange("p t c -> p (t c)") for a in (X, LX, XN))
                    if mode.kind == "full":
                        dve.tensor_tensor(x1, bank, lx4, ALU.add).then_inc(v_free, 1)
                        dve.wait_ge(v_free, n.v + 2)
                        link(dve.scalar_tensor_tensor(x4, x1, 0.5, x4, ALU.mult, ALU.add))
                    else:
                        dve.tensor_tensor(x4, bank, x4, ALU.add).then_inc(v_free, 1)
                dve.wait_ge(v_free, n.v + 2)

            def memory():
                bank = v_take()
                dve.tensor_copy(gates[:, :, :].rearrange("p t h -> p (t h)"), bank[:, 0:NT * HEADS]).then_inc(v_free, 1)
                dve.wait_ge(v_free, n.v + 2)
                dve.sem_inc(sig_in, 1)
                for which in range(2):
                    dve.wait_ge(sq_ready, which + 1)
                    link(dve.tensor_reduce(norm[:, :, :].rearrange("p t h -> p (t h)"),
                                           sq[:, :, :, :].rearrange("p t h c -> p (t h) c"), AX_X, ALU.add))
                    dve.tensor_scalar(norm[:, :, :], norm[:, :, :], 1e-24, None, ALU.max).then_inc(norm_in, 1)
                    dve.wait_ge(norm_out, which + 1)
                    dve.reciprocal(rnorm[which][:, :, :], norm[:, :, :]).then_inc(rnorm_ready, 1)
                    dve.wait_ge(rnorm_ready, which + 1)

            def memory_scores():
                assert n.v == MEM_V0, n.v
                m, used = 0, 0

                def near_sum(m):
                    dve.wait_ge(near2_ready, m + 1)
                    return dve.tensor_reduce(score_in[:, m // 4, m % 4 * 4:m % 4 * 4 + 4], near2[m % 2][:, :, :], AX_X, ALU.add)

                for t in range(NT):
                    if t % TB:
                        dve.wait_ge(phi_ready, used + 1)
                        for half in range(2):
                            bank = v_take()
                            hs = slice(half * HEADS // 2, (half + 1) * HEADS // 2)
                            f = far[:, hs, :].rearrange("p h c -> p (h c)")
                            if t % TB == 1:
                                dve.tensor_copy(f, bank[:, 0:HEADS // 2 * PHI]).then_inc(v_free, 1)
                            else:
                                dve.scalar_tensor_tensor(f, f, DECAY ** P, bank[:, 0:HEADS // 2 * PHI], ALU.mult, ALU.add)\
                                    .then_inc(v_free, 1)
                            dve.wait_ge(v_free, n.v + 2)
                            link(dve.tensor_tensor(farp[:, :, :], far[:, hs, :], phiR[used % 2][:, hs, :], ALU.mult))
                            link(dve.tensor_reduce(score_far[:, t, hs], farp[:, :, :], AX_X, ALU.add))
                        used += 1
                        dve.sem_inc(phi_used, 1)
                    for q in range(4):
                        bank = v_take()
                        dve.tensor_tensor(near[m % 2][:, :, :], bank.rearrange("p (h s) -> p h s", h=4),
                                          C("decay_root").unsqueeze(1).broadcast_to([P, 4, P]), ALU.mult)\
                            .then_inc(v_free, 1)
                        dve.wait_ge(v_free, n.v + 2)
                        if m:
                            near_sum(m - 1)
                        m += 1
                link(near_sum(m - 1))
                for b in range(BATCH):
                    ts = slice(b * TB + 1, (b + 1) * TB)
                    link(dve.tensor_tensor(score_in[:, ts, :], score_in[:, ts, :], score_far[:, ts, :], ALU.add))
                dve.tensor_tensor(score_in[:, :, :], score_in[:, :, :], scale16[:, :].unsqueeze(1)
                                  .broadcast_to([P, NT, HEADS]), ALU.mult).then_inc(sig_in, 1)
                dve.wait_ge(sig_out, 2)
                link(dve.tensor_tensor(score_in[:, :, :], score_in[:, :, :], gates[:, :, :], ALU.mult))
                link(dve.tensor_reduce(gated[:, :], score_in[:, :, :], AX_X, ALU.add))
                link(dve.tensor_scalar(gated[:, :], gated[:, :], 1.0 / HEADS, None, ALU.mult))

            def add_memory():
                for t in range(NT):
                    a = heads_of(t)
                    ins = dve.scalar_tensor_tensor(a, memval[:, t, :].rearrange("p (h d) -> p h d", h=HEADS),
                                                   gated[:, t:t + 1], a, ALU.mult, ALU.add)
                link(ins)
                dve.sem_inc(ao_ready, 1)

            dve.sem_inc(v_free, 2)
            dve.sem_inc(y_free, 2)
            dve.sem_inc(y_done, 2)
            dve.sem_inc(a_free, 1)
            dve.sem_inc(o_free, 2)
            dve.sem_inc(pt_free, 2)
            dve.wait_ge(loaded, ALL_LOADED)
            dve.tensor_copy(masks[:, :], mask_in[:, :]).then_inc(consts_done, 1)
            bank = v_take()
            dve.tensor_copy(scale16[:, :], bank[:, 0:HEADS]).then_inc(v_free, 1)
            dve.wait_ge(v_free, n.v + 2)
            dve.wait_ge(x_loaded, 16)
            dve.wait_ge(vec_done, 2)
            for kind, arg in PLAN:
                if kind == "moe":
                    layer_norm(X, XN)
                    gate(0)
                    experts(0)
                elif kind == "attn":
                    layer_norm(X, XN)
                    project(arg)
                    if arg is CAUSAL:
                        memory()
                        memory_scores()
                    attention(arg)
                    if arg is CAUSAL:
                        add_memory()
                    out_proj(arg)
                else:
                    layer_norm(X, LX, False)
                    layer_norm(LX, XN)
                    project(arg)
                    attention(arg)
                    out_proj(arg)
                    layer_norm(XN, XN)
                    gate(1)
                    experts(1)
            dve.sem_inc(x_final, 1)


_INS = ['L0_attn_x', 'L0_attn_qkv_w', 'L0_attn_qkv_b', 'L0_attn_w1w', 'L0_attn_w2w', 'L0_attn_r1w', 'L0_attn_r2w',
        'L0_attn_memv_w', 'L0_attn_memv_b', 'L0_attn_memg_w', 'L0_attn_memg_b', 'L0_attn_mem_scale', 'L0_attn_out_w',
        'L0_attn_out_b', 'L0_ffn_Wg', 'L0_ffn_W1', 'L0_ffn_b1', 'L0_ffn_W2', 'L0_ffn_b2', 'L1_attn_q_w', 'L1_attn_q_b',
        'L1_attn_k_w', 'L1_attn_k_b', 'L1_attn_v_w', 'L1_attn_v_b', 'L1_attn_o_w', 'L1_attn_o_b', 'L1_ffn_ln1_g',
        'L1_ffn_ln1_b', 'L1_ffn_Wqkv', 'L1_ffn_bqkv', 'L1_ffn_Wo', 'L1_ffn_bo', 'L1_ffn_ln2_g', 'L1_ffn_ln2_b',
        'L1_ffn_gate_w', 'L1_ffn_W1', 'L1_ffn_b1', 'L1_ffn_W2', 'L1_ffn_b2', 'L1_ffn_rW1', 'L1_ffn_rb1', 'L1_ffn_rW2',
        'L1_ffn_rb2', 'L1_ffn_coef_w', 'L1_ffn_coef_b']


def constants():
    at = np.arange(P)
    row_, col = at[:, None], at[None, :]
    co, nconst = offsets(CONST_COLS)
    mo, nmask = offsets(MASK_COLS)
    const = np.zeros((P, nconst), np.float32)
    mask = np.zeros((P, nmask), np.float32)

    def put(where, cols, name, value):
        where[:, cols[name][0]:cols[name][0] + cols[name][1]] = value

    far_off = -1e30
    put(const, co, "ident", row_ == col)
    put(const, co, "decay_root", np.where(col < row_, DECAY ** ((row_ - col) / 2.0), 0.0))
    put(const, co, "decay_next", DECAY ** (P + col - row_ + 0.0))
    put(const, co, "rank", EXPERTS - np.arange(EXPERTS)[None, :])
    put(const, co, "same_head", row_ // LINE == np.arange(HEADS)[None, :])
    put(mask, mo, "ident", row_ == col)
    put(mask, mo, "before", row_ < col)
    put(mask, mo, "ones", 1.0)
    put(mask, mo, "later_key", np.where(col > row_, far_off, 0.0))
    put(mask, mo, "later_query", np.where(row_ > col, far_off, 0.0))
    key = np.arange(SPAN)[None, :]
    put(mask, mo, "window_keys", np.where((key >= row_) & (key <= row_ + 2 * WIN), 0.0, far_off))
    key = np.concatenate([row_, row_ + WCH], 1)[:, :, None]
    query = at[None, None, :]
    put(mask, mo, "window_queries",
        np.where((key >= query) & (key <= query + 2 * WIN), 0.0, far_off).reshape(P, 2 * P))
    valid = np.zeros((1, PADDED), np.float32)
    valid[:, WIN:WIN + SEQ] = 1.0
    return {"consts": const, "mask_consts": mask, "valid": valid}


def kernel(**inputs):
    import concourse.bacc as _bacc
    from concourse.bass_utils import run_bass_kernel_spmd as _run

    nc = _bacc.Bacc("TRN2", target_bir_lowering=False, num_devices=1)
    arrays, d = {}, {}
    given = {name: np.ascontiguousarray(inputs[name]) for name in _INS}
    for name, a in {**given, **constants()}.items():
        arrays[f"in_{name}_dram"] = a
        d[name] = nc.dram_tensor(f"in_{name}_dram", a.shape, mybir.dt.from_np(a.dtype), kind="ExternalInput").ap()
    out = nc.dram_tensor("out_0_dram", (BATCH, SEQ, DIM), F32, kind="ExternalOutput").ap()
    build(nc, d, out)
    r = _run(nc, [arrays], core_ids=[0])
    return r.results[0]["out_0_dram"]
```

```python
from contextlib import ExitStack

import numpy as np

import concourse.bass as bass
from concourse import mybir

ALU = mybir.AluOpType
ACT = mybir.ActivationFunctionType
AX_X = mybir.AxisListType.X
F32 = mybir.dt.float32
BF16 = mybir.dt.bfloat16

P = 128
BATCH, SEQ, DIM = 2, 1024, 128
TB = SEQ // P
NT = BATCH * TB
HEADS, DH = 16, DIM // 16
WIN = 32
PADDED = SEQ + 2 * WIN
SPAN = P + 2 * WIN
WCH = SPAN // 2
EXPERTS, FFN = 8, 512
FC = FFN // P
BLK = 512
NBLK = BATCH * SEQ // BLK
CAPACITY = 2 * 2 * BATCH * SEQ // EXPERTS
PARTS = 3
ROWS = 6 * DH
MAXROW = 64
STACK = 96
QUAD = 32
SCALE = float(DH) ** -0.5
EPS = 1e-5
LINE = 6
PHI = LINE * LINE
DECAY = 0.99
PAIRS = [(0, 1), (0, 2), (0, 3), (1, 2), (1, 3), (2, 3)]
JOBS = BATCH * HEADS // 2
Q_PART = [0, 0, 1, 0, 2, 1]
K_PART = [0, 1, 0, 2, 0, 1]

CONST_COLS = {"ident": P, "decay_root": P, "decay_next": P, "rank": EXPERTS, "same_head": HEADS, "gather": 2 * (DH + 1)}
MASK_COLS = {"ident": P, "before": P, "ones": P, "later_key": P, "never": P, "later_query": P, "window_keys": SPAN,
             "window_queries": 2 * P}
VEC = {"f0_b1": 0, "f1_b1": 32, "rb1": 64, "a0_b": 68, "f1_b": 71, "ln1_g": 74, "ln1_b": 75, "ln2_g": 76,
       "ln2_b": 77, "a1_qb": 78, "a1_kb": 79}
ROW = {"a0_vb": (0, 128), "f1_vb": (128, 128), "a1_vb": (256, 128), "a0_ob": (384, 128), "f1_ob": (512, 128),
       "a1_ob": (640, 128), "memv_b": (768, 128), "memg_b": (896, 16), "mem_scale": (912, 16), "coef_b": (928, 2)}


def offsets(cols):
    out, at = {}, 0
    for name, n in cols.items():
        out[name] = (at, n)
        at += n
    return out, at


def schedule(mode, with_b, with_a, carry=False):
    if not with_b:
        out = [("max", a, False) for a in range(mode.maxes)]
        return out + [("split", 0, False), ("rows", 0, False)]
    S, pairs = mode.steps, mode.steps // 2
    slots = S * 3 // 4 if S > 4 else 2
    out, behind = [], []
    for s in range(S):
        out.append(("scores", s, False))
        if s % 2 == 0:
            out += behind
            behind = []
        elif s > 1 or carry:
            p = (s // 2 - 1) % pairs
            out.append(("values", p, s == 1))
            if p % (pairs // 2) == pairs // 2 - 1:
                out.append(("take", p // (pairs // 2), s == 1))
                behind = [("gather", p // (pairs // 2), s == 1)]
        if with_a:
            first, last = (min(mode.maxes, -(-mode.maxes * k // slots)) for k in (s, s + 1))
            out += [("max", a, False) for a in range(first, last)]
            if s == slots:
                out.append(("split", 0, False))
            if s == slots + (1 if S > 4 else 0):
                out.append(("rows", 0, False))
    return out + behind


def last_values(mode):
    return [("values", mode.steps // 2 - 1, True), ("take", 1, True), ("gather", 1, True)]


class Mode:
    def __init__(self, kind):
        self.kind = kind
        self.steps = 4 if kind == "window" else 2 * TB
        self.maxes = self.steps
        self.per_head = self.steps // 2
        self.pairs = self.steps // 2
        self.items = self.maxes + 1


class Count:

    v = s = a = g = o = p = u = w0 = w1 = xn = xt = coef = coefT = picks = vp = aot = jobs = c0 = 0
    stored = parts = s_in = step = var = std = gate = gexp = bias1 = 0


def build(nc, d, out, LAYERS=6):
    co, nconst = offsets(CONST_COLS)
    mo, nmask = offsets(MASK_COLS)
    MODES = [Mode("causal"), Mode("full"), Mode("window")]
    CAUSAL, FULL, WINDOW = MODES

    with ExitStack() as ctx:
        def sb(name, shape, dt=F32):
            return ctx.enter_context(nc.sbuf_tensor(name, shape, dt))

        def ps(name, shape):
            return ctx.enter_context(nc.psum_tensor(name, shape, F32))

        def sem(name):
            return ctx.enter_context(nc.semaphore(name))

        q_dram = nc.dram_tensor("q_stack_dram", (BATCH, HEADS, ROWS, SEQ), BF16, kind="Internal").ap()
        k_dram = nc.dram_tensor("k_stack_dram", (BATCH, HEADS, ROWS, PADDED), BF16, kind="Internal").ap()
        q_heads = q_dram.rearrange("b h r t -> (b h) r t")
        k_heads = k_dram.rearrange("b h r t -> (b h) r t")

        X = sb("X", [P, NT, DIM])
        LX = sb("LX", [P, NT, DIM])
        XN = sb("XN", [P, NT, DIM])
        XT = sb("XT", [P, BATCH, PADDED])
        stats = sb("stats", [P, NT, 6])
        mv = sb("mv", [P, NT, 2])
        std = sb("std", [P, NT])
        rstd = sb("rstd", [P, NT])

        const = sb("const", [P, nconst])
        masks = sb("masks", [P, nmask], BF16)
        mask_in = LX[:, :, :].rearrange("p t c -> p (t c)")[:, 0:nmask]
        assert nmask <= 1536
        valid = sb("valid", [1, PADDED])
        vec_rows = sb("vec_rows", [P, P])
        vec = sb("vec", [P, P])
        row = sb("row", [1, 930])
        b2_0 = sb("b2_0", [EXPERTS, DIM])
        b2_1 = sb("b2_1", [EXPERTS + 1, DIM])

        def C(name):
            return const[:, co[name][0]:co[name][0] + co[name][1]]

        def M(name):
            return masks[:, mo[name][0]:mo[name][0] + mo[name][1]]

        def R(name):
            return row[0:1, ROW[name][0]:ROW[name][0] + ROW[name][1]]

        ident, identb = C("ident"), M("ident")

        a0_qkv = sb("a0_qkv", [P, 3 * DIM])
        a0_out = sb("a0_out", [P, DIM])
        lines_w = sb("lines_w", [P, 4, 4 * HEADS])
        memv_w = sb("memv_w", [P, DIM])
        memg_w = sb("memg_w", [P, HEADS])
        f0_gate = sb("f0_gate", [P, EXPERTS])
        f1_qkv = sb("f1_qkv", [P, 3 * DIM])
        f1_out = sb("f1_out", [P, DIM])
        f1_gate = sb("f1_gate", [P, EXPERTS])
        coef_w = sb("coef_w", [P, 2])
        LX_all = LX[:, :, :].rearrange("p t c -> p (t c)")
        a1_raw = LX_all[:, 1536:2048].rearrange("p (a b) -> p a b", a=4)
        a1_w = sb("a1_w", [P, 4, DIM])

        W1 = [sb(f"W1_{k}", [P, FFN]) for k in range(2)]
        W2 = [sb(f"W2_{k}", [P, FC, DIM]) for k in range(2)]
        bias1 = [sb(f"bias1_{k}", [P, FC]) for k in range(2)]
        hidden_all = sb("hidden", [P, 2, FC, BLK])
        hidden = [hidden_all[:, k] for k in range(2)]

        logits = sb("logits", [P, NT, EXPERTS])
        g = [sb(f"gate_{k}", [P, NT, EXPERTS]) for k in range(4)]
        pick1 = sb("pick1", [P, NT, EXPERTS])
        pick2 = sb("pick2", [P, NT, EXPERTS])
        pick1b = sb("pick1b", [P, NT, EXPERTS], BF16)
        pick2b = sb("pick2b", [P, NT, EXPERTS], BF16)
        s1 = sb("s1", [P, 12, NT])
        coef2 = sb("coef2", [P, NT, 2])
        coefe = sb("coefe", [P, NT, 2])
        coef = sb("coef", [P, EXPERTS + 1, NT])
        memval = sb("memval", [P, NT, DIM])
        coefT = memval[0:EXPERTS + 1].rearrange("e t c -> e (t c)")

        Qp = [sb(f"Qp_{k}", [P, BATCH, SEQ], BF16) for k in range(PARTS)]
        Kp = [sb(f"Kp_{k}", [P, BATCH, PADDED], BF16) for k in range(PARTS)]
        rest = sb("rest", [P, BLK])
        QS = [[sb(f"QS_{k}_{hh}", [STACK, SEQ], BF16) for hh in range(2)] for k in range(2)]
        KS = [[sb(f"KS_{k}_{hh}", [STACK, PADDED], BF16) for hh in range(2)] for k in range(2)]
        V = sb("V", [P, BATCH * HEADS, TB, DH])
        VW_all = sb("VW", [P, 3 * NT * HEADS * LINE])
        VW = VW_all[0:WCH, 0:BATCH * HEADS * TB * 2 * DH]\
            .rearrange("p (b t c d) -> p b t c d", b=BATCH * HEADS, t=TB, c=2)
        VJ = [sb(f"VJ_{k}", [P, 2, 2 * TB, QUAD]) for k in range(2)]
        PT = [Qp[k][:, :, :].rearrange("p b t -> p (b t)").bitcast(F32) for k in range(PARTS)] + [sb("PT", [P, SEQ])[:, :]]
        OT = [sb(f"OT_{k}", [P, BLK]) for k in range(2)]
        negmax = sb("negmax", [P, 2 * TB])
        negrest = sb("negrest", [P, 2 * TB])
        negparts = sb("negparts", [P, 2 * TB, PARTS], BF16)
        rden = sb("rden", [P, 4, 2])
        AO = sb("AO", [P, TB, BATCH * HEADS, DH])
        AOT = sb("AOT", [P, NT * P])

        pts = hidden_all[:, :, :, :].rearrange("p k c b -> p (k c b)")\
            .rearrange("p (t g h c) -> p t g h c", t=NT, g=4, h=HEADS)
        n_line = NT * HEADS * LINE
        Lw, Lr, sq = (VW_all[:, k * n_line:(k + 1) * n_line].rearrange("p (t h c) -> p t h c", t=NT, h=HEADS)
                      for k in range(3))
        prod = [sb(f"prod_{k}", [P, NT, HEADS]) for k in range(2)]
        norm = sb("norm", [P, NT, HEADS])
        rnorm = [sb(f"rnorm_{k}", [P, NT, HEADS]) for k in range(2)]
        LT = [sb(f"LT_{k}", [HEADS * LINE, 2, P]) for k in range(2)]
        JM = [LX[0:HEADS * LINE, :, :], AOT[0:HEADS * LINE, :].rearrange("p (h s) -> p h s", h=HEADS)]
        AO_all = AO[:, :, :, :].rearrange("p t b d -> p (t b d)")
        hid = hidden_all[:, :, :, :].rearrange("p k c b -> p (k c b)")
        HP = HEADS * PHI
        phiR = [AO_all[:, k * HP:(k + 1) * HP].rearrange("p (h c) -> p h c", h=HEADS) for k in range(2)]
        phiJ = [a.rearrange("p (h c) -> p h c", h=HEADS) for a in (AO_all[:, 2 * HP:3 * HP], hid[:, 4 * BLK:4 * BLK + HP])]
        far = hid[:, 4 * BLK + HP:4 * BLK + 2 * HP].rearrange("p (h c) -> p h c", h=HEADS)
        farp = hid[:, 4 * BLK + 2 * HP:4 * BLK + 2 * HP + HP // 2].rearrange("p (h c) -> p h c", h=HEADS // 2)
        near = [hid[:, k * BLK:(k + 1) * BLK].rearrange("p (h s) -> p h s", h=4) for k in range(2)]
        near2 = [hid[:, k * BLK:(k + 1) * BLK].rearrange("p (h s) -> p h s", h=4) for k in range(2, 4)]
        score_in = sb("score_in", [P, NT, HEADS])
        score_far = sb("score_far", [P, NT, HEADS])
        gates = sb("gates", [P, NT, HEADS])
        scale16 = sb("scale16", [P, HEADS])
        gated = sb("gated", [P, NT])

        pA = ps("pA", [P, 2 * BLK])
        pS = [ps(f"pS_{k}", [P, 2 * BLK]) for k in range(2)]
        pO = [ps(f"pO_{k}", [P, BLK]) for k in range(2)]

        loaded = sem("loaded")
        x_loaded = sem("x_loaded")
        set_up = sem("set_up")
        consts_done = sem("consts_done")
        vec_done = sem("vec_done")
        v_ready, v_free = sem("v_ready"), sem("v_free")
        s_ready, s_free = sem("s_ready"), sem("s_free")
        dve_step, pool_step = sem("dve_step"), sem("pool_step")
        var_ready, std_ready = sem("var_ready"), sem("std_ready")
        xn_ready, xt_ready = sem("xn_ready"), sem("xt_ready")
        gate_in, gate_exp = sem("gate_in"), sem("gate_exp")
        picks_ready, coef_ready, coefT_ready = sem("picks_ready"), sem("coef_ready"), sem("coefT_ready")
        w_in = [sem(f"w_in_{k}") for k in range(2)]
        h_ready, gelu_done = sem("h_ready"), sem("gelu_done")
        y_done, y_free = sem("y_done"), sem("y_free")
        bias1_ready = sem("bias1_ready")
        parts_ready, stack_stored = sem("parts_ready"), sem("stack_stored")
        stack_in = [[sem(f"stack_in_{k}_{hh}") for hh in range(2)] for k in range(2)]
        rows_clear = [sem(f"rows_clear_{hh}") for hh in range(2)]
        vj_ready = sem("vj_ready")
        a_ready, a_free = sem("a_ready"), sem("a_free")
        negparts_ready = sem("negparts_ready")
        st_ready, exp_done, values_done = sem("st_ready"), sem("exp_done"), sem("values_done")
        ot_ready, gathered, o_free = sem("ot_ready"), sem("gathered"), sem("o_free")
        v_in_place = sem("v_in_place")
        ao_ready, aot_ready = sem("ao_ready"), sem("aot_ready")
        pts_ready, lines_ready = sem("pts_ready"), sem("lines_ready")
        sq_ready, norm_in, norm_out, rnorm_ready = sem("sq_ready"), sem("norm_in"), sem("norm_out"), sem("rnorm_ready")
        lt_ready, jm_ready, phi_ready, phi_used = sem("lt_ready"), sem("jm_ready"), sem("phi_ready"), sem("phi_used")
        near2_ready = sem("near2_ready")
        sig_in, sig_out = sem("sig_in"), sem("sig_out")
        x_final, out_stored = sem("x_final"), sem("out_stored")

        x_tok = d["L0_attn_x"].rearrange("b (i p) c -> p (b i) c", p=P)
        out_tok = out.rearrange("b (i p) c -> p (b i) c", p=P)

        SYNC_LOADS = [
            (const[:, :], d["consts"][:, 0:nconst]),
            (mask_in[:, :], d["mask_consts"]),
            (valid[:, :], d["valid"]),
            (f0_gate[:, :], d["L0_ffn_Wg"]),
            (vec_rows[0:32, :], d["L0_ffn_b1"].rearrange("e (c p) -> (e c) p", p=P)),
            (vec_rows[32:64, :], d["L1_ffn_b1"].rearrange("e (c p) -> (e c) p", p=P)),
            (vec_rows[64:68, :], d["L1_ffn_rb1"].rearrange("(c p) -> c p", p=P)),
            (vec_rows[68:71, :], d["L0_attn_qkv_b"].rearrange("(c p) -> c p", p=P)),
            (vec_rows[71:74, :], d["L1_ffn_bqkv"].rearrange("(c p) -> c p", p=P)),
            (vec_rows[74:75, :], d["L1_ffn_ln1_g"].unsqueeze(0)),
            (vec_rows[75:76, :], d["L1_ffn_ln1_b"].unsqueeze(0)),
            (vec_rows[76:77, :], d["L1_ffn_ln2_g"].unsqueeze(0)),
            (vec_rows[77:78, :], d["L1_ffn_ln2_b"].unsqueeze(0)),
            (vec_rows[78:79, :], d["L1_attn_q_b"].unsqueeze(0)),
            (vec_rows[79:80, :], d["L1_attn_k_b"].unsqueeze(0)),
            (b2_0[:, :], d["L0_ffn_b2"]),
            (b2_1[0:EXPERTS, :], d["L1_ffn_b2"]),
            (b2_1[EXPERTS:EXPERTS + 1, :], d["L1_ffn_rb2"].unsqueeze(0)),
            (R("a0_vb"), d["L0_attn_qkv_b"].unsqueeze(0)[:, 2 * DIM:3 * DIM]),
            (R("f1_vb"), d["L1_ffn_bqkv"].unsqueeze(0)[:, 2 * DIM:3 * DIM]),
            (R("a1_vb"), d["L1_attn_v_b"].unsqueeze(0)),
            (R("a0_ob"), d["L0_attn_out_b"].unsqueeze(0)),
            (R("f1_ob"), d["L1_ffn_bo"].unsqueeze(0)),
            (R("a1_ob"), d["L1_attn_o_b"].unsqueeze(0)),
            (R("memv_b"), d["L0_attn_memv_b"].unsqueeze(0)),
            (R("memg_b"), d["L0_attn_memg_b"].unsqueeze(0)),
            (R("mem_scale"), d["L0_attn_mem_scale"].unsqueeze(0)),
            (R("coef_b"), d["L1_ffn_coef_b"].unsqueeze(0)),
            (a0_qkv[:, :], d["L0_attn_qkv_w"]),
            (a0_out[:, :], d["L0_attn_out_w"]),
            (lines_w[:, 0, :], d["L0_attn_w2w"]),
            (lines_w[:, 1, :], d["L0_attn_r1w"]),
            (lines_w[:, 2, :], d["L0_attn_r2w"]),
            (lines_w[:, 3, :], d["L0_attn_w1w"]),
            (memv_w[:, :], d["L0_attn_memv_w"]),
            (memg_w[:, :], d["L0_attn_memg_w"]),
            (f1_qkv[:, :], d["L1_ffn_Wqkv"]),
            (f1_out[:, :], d["L1_ffn_Wo"]),
            (f1_gate[:, :], d["L1_ffn_gate_w"]),
            (coef_w[:, :], d["L1_ffn_coef_w"]),
            (a1_raw[:, 0, :], d["L1_attn_q_w"]),
            (a1_raw[:, 1, :], d["L1_attn_k_w"]),
            (a1_raw[:, 2, :], d["L1_attn_v_w"]),
            (a1_raw[:, 3, :], d["L1_attn_o_w"]),
        ]
        ALL_LOADED = 16 * len(SYNC_LOADS)

        PLAN = [("moe", 0), ("attn", CAUSAL), ("moe", 0), ("l1", FULL), ("attn", WINDOW), ("l1", FULL)][:LAYERS]
        ATTN_OF = {
            "causal": dict(w=a0_qkv[:, :], wo=a0_out[:, :], qb=VEC["a0_b"], kb=VEC["a0_b"] + 1, vb="a0_vb", ob="a0_ob"),
            "full": dict(w=f1_qkv[:, :], wo=f1_out[:, :], qb=VEC["f1_b"], kb=VEC["f1_b"] + 1, vb="f1_vb", ob="f1_ob"),
            "window": dict(w=a1_w[:, 0:3, :].rearrange("p a b -> p (a b)"), wo=a1_w[:, 3, :], qb=VEC["a1_qb"],
                           kb=VEC["a1_kb"], vb="a1_vb", ob="a1_ob"),
        }

        def tile_cols(t, shift=0):
            at = WIN + t % TB * P + shift
            return XT[:, t // TB, at:at + P]

        def first_query(mode, kt):
            return kt * P if mode.kind == "causal" and kt > 1 else 0

        def heads_of(t):
            return AO[:, t % TB, t // TB * HEADS:(t // TB + 1) * HEADS, :]

        def block_cols(k):
            at = WIN + k % 2 * BLK
            return XT[:, k // 2, at:at + BLK]

        MEM_V0 = 1 + 7 + 2 * NBLK + 1

        def far_items(t):
            return 2 * sum(1 for u in range(t + 1) if u % TB)

        block = ctx.enter_context(nc.Block())

        @block.sync
        def _(sp):
            n = Count()
            sp.dma_start(X[:, :, :], x_tok).then_inc(x_loaded, 16)
            sp.wait_ge(set_up, 1)
            for dst, src in SYNC_LOADS:
                sp.dma_start(dst, src).then_inc(loaded, 16)

            def load_expert(w1, w2, k):
                sp.dma_start(W1[k][:, :], w1).then_inc(w_in[k], 16)
                sp.dma_start(W2[k][:, :, :], w2).then_inc(w_in[k], 16)

            def experts(layer):
                w1, w2 = d[f"L{layer}_ffn_W1"], d[f"L{layer}_ffn_W2"]

                def load(e, k):
                    load_expert(w1[bass.ds(e, 1)].rearrange("e c f -> (e c) f"),
                                w2[bass.ds(e, 1)].rearrange("e (c p) o -> (e p) c o", p=P), k)

                if n.u:
                    sp.wait_ge(y_done, n.u + 2)
                load(0, 0)
                load(1, 1)
                with sp.Fori(1, EXPERTS // 2) as i:
                    for k in range(2):
                        sp.wait_ge(y_done, n.u + 2 + NBLK * (2 * i + (k - 1)))
                        load(2 * i + k, k)
                n.u += NBLK * EXPERTS
                if layer:
                    sp.wait_ge(y_done, n.u + 2 - NBLK)
                    load_expert(d["L1_ffn_rW1"], d["L1_ffn_rW2"].rearrange("(c p) o -> p c o", p=P), 0)
                    n.u += NBLK

            def stacks(mode):
                S = mode.steps
                sp.wait_ge(parts_ready, n.parts + 1)
                for grp in range(6):
                    for b in range(BATCH):
                        sp.dma_start(q_dram[b, :, grp * DH:(grp + 1) * DH, :], Qp[Q_PART[grp]][:, b, :])\
                          .then_inc(stack_stored, 16)
                sp.wait_ge(parts_ready, n.parts + 2)
                for grp in range(6):
                    for b in range(BATCH):
                        sp.dma_start(k_dram[b, :, grp * DH:(grp + 1) * DH, :], Kp[K_PART[grp]][:, b, :])\
                          .then_inc(stack_stored, 16)
                n.parts += 2
                n.stored += 16 * 24
                sp.wait_ge(stack_stored, n.stored)

                def load(j, k, hh):
                    for dst, src in ((QS, q_heads), (KS, k_heads)):
                        sp.dma_start(dst[k][hh][0:ROWS, :],
                                     src[bass.ds(2 * j + hh, 1)].rearrange("a r t -> (a r) t"))\
                          .then_inc(stack_in[k][hh], 16)

                for j in range(2):
                    for hh in range(2):
                        load(j, j, hh)
                with sp.Fori(0, JOBS // 2 - 1) as i:
                    for k in range(2):
                        for hh in range(2):
                            sp.wait_ge(st_ready, n.g + S * (2 * i + k) + (S // 2 * (hh + 1)))
                            load(2 * i + (k + 2), k, hh)
                n.g += S * JOBS
                n.s_in += 16 * JOBS
                for k in range(2):
                    for hh in range(2):
                        sp.wait_ge(stack_in[k][hh], n.s_in)

            for kind, arg in PLAN:
                if kind == "moe":
                    experts(0)
                elif kind == "attn":
                    stacks(arg)
                else:
                    stacks(arg)
                    experts(1)
            sp.wait_ge(x_final, 1)
            sp.dma_start(out_tok, X[:, :, :]).then_inc(out_stored, 16)
            sp.wait_ge(out_stored, 16)

        @block.gpsimd
        def _(pool):
            n = Count()

            def link(ins):
                n.step += 1
                ins.then_inc(pool_step, 1)
                pool.wait_ge(pool_step, n.step)

            pool.memset(vec_rows[:, :], 0.0).then_inc(set_up, 1)
            pool.memset(XT[:, :, 0:WIN], 0.0)
            pool.memset(XT[:, :, WIN + SEQ:PADDED], 0.0)
            for k in range(PARTS):
                pool.memset(Kp[k][:, :, 0:WIN], 0.0)
                pool.memset(Kp[k][:, :, WIN + SEQ:PADDED], 0.0)
            for k in range(2):
                link(pool.memset(VJ[k][:, :, :, :], 0.0))
                link(pool.memset(VJ[k][:, :, :, DH:DH + 1].rearrange("p h t d -> p (h t d)"), 1.0))
            for k in range(2):
                for hh in range(2):
                    link(pool.memset(QS[k][hh][:, :], 0.0))
                    link(pool.memset(KS[k][hh][:, :], 0.0))
                    link(pool.memset(KS[k][hh][MAXROW:MAXROW + PARTS, :], 1.0))
            pool.sem_inc(set_up, 1)

            def memory():
                pool.wait_ge(pts_ready, NT // 2)
                for which, (dst, i1, i2) in enumerate(((Lw, 3, 0), (Lr, 1, 2))):
                    for c, (a, b) in enumerate(PAIRS):
                        if which == 0 and c in (1, 4):
                            a, b = b, a
                        link(pool.tensor_tensor(prod[0][:, :, :], pts[:, :, i1, :, a], pts[:, :, i2, :, b], ALU.mult))
                        link(pool.tensor_tensor(prod[1][:, :, :], pts[:, :, i1, :, b], pts[:, :, i2, :, a], ALU.mult))
                        at = c if which else LINE - 1 - c
                        link(pool.tensor_tensor(dst[:, :, :, at], prod[0][:, :, :], prod[1][:, :, :], ALU.subtract))
                    if which:
                        pool.wait_ge(norm_in, 1)
                    pool.tensor_tensor(sq[:, :, :, :], dst[:, :, :, :], dst[:, :, :, :], ALU.mult).then_inc(sq_ready, 1)
                for which, dst in enumerate((Lw, Lr)):
                    pool.wait_ge(rnorm_ready, which + 1)
                    for half in range(2):
                        ts = slice(half * TB, (half + 1) * TB)
                        ins = pool.tensor_tensor(
                            dst[:, ts, :, :].rearrange("p t h c -> p (t h) c"),
                            dst[:, ts, :, :].rearrange("p t h c -> p (t h) c"),
                            rnorm[which][:, ts, :].rearrange("p t h -> p (t h)").unsqueeze(2)
                            .broadcast_to([P, TB * HEADS, LINE]), ALU.mult)
                    ins.then_inc(lines_ready, 1)
                pool.wait_ge(lines_ready, 2)
                used = 0
                for t in range(NT):
                    k = t % 2
                    if t % TB:
                        if used >= 2:
                            pool.wait_ge(phi_used, used - 1)
                        for src, dst, tt in ((Lr, phiR[used % 2], t), (Lw, phiJ[used % 2], t - 1)):
                            line = src[:, tt, :, :]
                            for half in range(2):
                                hs = slice(half * HEADS // 2, (half + 1) * HEADS // 2)
                                ins = pool.tensor_tensor(
                                    dst[:, hs, :].rearrange("p h (a b) -> p h a b", a=LINE),
                                    line[:, hs, :].unsqueeze(3).broadcast_to([P, HEADS // 2, LINE, LINE]),
                                    line[:, hs, :].unsqueeze(2).broadcast_to([P, HEADS // 2, LINE, LINE]), ALU.mult)
                        ins.then_inc(phi_ready, 1)
                        used += 1
                        pool.wait_ge(phi_ready, used)
                    pool.wait_ge(lt_ready, t + 1)
                    if t >= 2:
                        pool.wait_ge(v_ready, MEM_V0 + (t - 2) * 4 + far_items(t - 2) + 4)
                    nl = HEADS * LINE
                    pool.tensor_tensor(JM[k][:, :, :], LT[k][:, 1, :].unsqueeze(1).broadcast_to([nl, HEADS, P]),
                                       C("same_head")[0:nl, :].unsqueeze(2).broadcast_to([nl, HEADS, P]), ALU.mult)\
                        .then_inc(jm_ready, 1)
                    pool.wait_ge(jm_ready, t + 1)

            for kind, arg in PLAN:
                if kind == "attn" and arg is CAUSAL:
                    memory()

        @block.tensor
        def _(pe):
            n = Count()

            def v_bank():
                k = n.v
                n.v += 1
                pe.wait_ge(v_free, k + 1)
                return pA[:, k % 2 * BLK:(k % 2 + 1) * BLK]

            def s_bank():
                k = n.s
                n.s += 1
                pe.wait_ge(s_free, k + 1)
                return pO[k % 2][:, :]

            def turn4(src, ready=None):
                bank = s_bank()
                for q, a in enumerate(src):
                    ins = pe.transpose(bank[:, q * P:(q + 1) * P], a, ident)
                ins.then_inc(s_ready, 1)

            def norm_turn():
                for q in range(4):
                    pe.wait_ge(xn_ready, n.xn + q + 1)
                    turn4([XN[:, 4 * q + r, :] for r in range(4)])
                n.xn += 4
                n.xt += 4

            def wait_xt():
                pe.wait_ge(xt_ready, n.xt)

            def gate(layer):
                wait_xt()
                bank = v_bank()
                wg = f1_gate if layer else f0_gate
                for t in range(NT):
                    ins = pe.matmul(bank[:, t * EXPERTS:(t + 1) * EXPERTS], tile_cols(t), wg[:, :], start=True, stop=True)
                if layer:
                    for t in range(NT):
                        o = bank[:, P + 2 * t:P + 2 * t + 2]
                        pe.matmul(o, tile_cols(t), coef_w[:, :], start=True, stop=False)
                        ins = pe.matmul(o, valid[0:1, WIN:WIN + P], R("coef_b"), start=False, stop=True)
                ins.then_inc(v_ready, 1)
                if not layer:
                    pe.wait_ge(picks_ready, n.picks + 1)
                    n.picks += 1
                    for which, pick in enumerate((pick1b, pick2b)):
                        bank = v_bank()
                        ins = pe.matmul(bank[:, 0:NT * EXPERTS], M("before"), pick[:, :, :].rearrange("p t e -> p (t e)"),
                                        start=True, stop=False, skip_group_check=True)
                        for t in range(NT - 1):
                            k = NT - 1 - t
                            ins = pe.matmul(bank[:, (t + 1) * EXPERTS:NT * EXPERTS].rearrange("p (t e) -> p t e", t=k),
                                            M("ones"), pick[:, t, :].unsqueeze(1).broadcast_to([P, k, EXPERTS]),
                                            start=False, stop=(which == 0 and t == NT - 2), skip_group_check=True)
                        if which:
                            for t in range(NT):
                                ins = pe.matmul(bank[:, 0:NT * EXPERTS].rearrange("p (t e) -> p t e", t=NT), M("ones"),
                                                pick1b[:, t, :].unsqueeze(1).broadcast_to([P, NT, EXPERTS]),
                                                start=False, stop=(t == NT - 1), skip_group_check=True)
                        ins.then_inc(v_ready, 1)
                ne = EXPERTS + (1 if layer else 0)
                pe.wait_ge(coef_ready, n.coef + 1)
                n.coef += 1
                for q in range(4):
                    bank = s_bank()
                    for r in range(4):
                        ins = pe.matmul(bank[0:ne, r * P:(r + 1) * P], coef[:, 0:ne, 4 * q + r], ident, start=True, stop=True)
                    ins.then_inc(s_ready, 1)
                b2 = b2_1 if layer else b2_0
                for q in range(4):
                    n.coefT += 1
                    pe.wait_ge(coefT_ready, n.coefT)
                    bank = v_bank()
                    for r in range(4):
                        t = 4 * q + r
                        ins = pe.matmul(bank[:, r * P:(r + 1) * P], coefT[0:ne, t * P:(t + 1) * P], b2[0:ne, :],
                                        start=True, stop=True)
                    ins.then_inc(v_ready, 1)

            def up(k, u, blk):
                for c in range(FC):
                    pe.wait_ge(gelu_done, FC * u + (c + 1))
                    pe.matmul(pS[c // 2][:, c % 2 * BLK:(c % 2 + 1) * BLK], W1[k][:, c * P:(c + 1) * P],
                              block_cols(blk), start=True, stop=True).then_inc(h_ready, 1)

            def down(k, u, blk):
                pe.wait_ge(gelu_done, FC * u + 2 * FC)
                pe.wait_ge(y_free, u + 1)
                y = pO[blk % 2]
                for r in range(4):
                    for c in range(FC):
                        ins = pe.matmul(y[:, r * P:(r + 1) * P], hidden[blk % 2][:, c, r * P:(r + 1) * P], W2[k][:, c, :],
                                        start=(c == 0), stop=(c == FC - 1))
                ins.then_inc(y_done, 1)

            def expert_units(uses, u0):
                units = [(k, b) for k in range(len(uses)) for b in range(NBLK)]
                for m, (k, b) in enumerate(units):
                    if b == 0:
                        pe.wait_ge(w_in[k], 32 * uses[k] + 32)
                    up(k, u0 + m, b)
                    if m:
                        down(units[m - 1][0], u0 + (m - 1), units[m - 1][1])
                down(units[-1][0], u0 + (len(units) - 1), units[-1][1])

            def experts(layer):
                pe.wait_ge(s_free, n.s + 2)
                with pe.Fori(0, EXPERTS // 2) as i:
                    expert_units([n.w0 + i, n.w1 + i], n.u + 2 * NBLK * i)
                n.u += NBLK * EXPERTS
                n.w0 += EXPERTS // 2
                n.w1 += EXPERTS // 2
                if layer:
                    expert_units([n.w0], n.u)
                    n.u += NBLK
                    n.w0 += 1
                pe.wait_ge(y_free, n.u + 2)

            def project(mode):
                a = ATTN_OF[mode.kind]
                w = a["w"]
                wait_xt()
                for which in range(2):
                    for b in range(NBLK):
                        bank = v_bank()
                        pe.matmul(bank, w[:, which * DIM:(which + 1) * DIM], block_cols(b), start=True, stop=True)\
                          .then_inc(v_ready, 1)
                wv = w[:, 2 * DIM:3 * DIM]
                if mode.kind == "window":
                    for bi in range(0, NT, 2):
                        bank = s_bank()
                        for q in range(4):
                            b, at = bi // TB, (bi % TB + q // 2) * P + q % 2 * WCH
                            o = bank[0:WCH, q * P:(q + 1) * P]
                            pe.matmul(o, XT[:, b, at:at + WCH], wv, start=True, stop=False)
                            ins = pe.matmul(o, valid[0:1, at:at + WCH], R(a["vb"]), start=False, stop=True)
                        ins.then_inc(s_ready, 1)
                        n.vp += 1
                else:
                    for q in range(4):
                        bank = s_bank()
                        for r in range(4):
                            o = bank[:, r * P:(r + 1) * P]
                            pe.matmul(o, tile_cols(4 * q + r), wv, start=True, stop=False)
                            ins = pe.matmul(o, valid[0:1, WIN:WIN + P], R(a["vb"]), start=False, stop=True)
                        ins.then_inc(s_ready, 1)
                        n.vp += 1

            def max_part(mode, k, a):
                hh, q = divmod(a, mode.per_head)
                Q, K = QS[k][hh], KS[k][hh]
                if mode.kind == "window":
                    for half in range(2):
                        for m in range(2):
                            t = 4 * q + 2 * half + m
                            o = pA[:, half * BLK + m * SPAN:half * BLK + (m + 1) * SPAN]
                            pe.matmul(o, Q[:, t * P:(t + 1) * P], K[:, t * P:t * P + SPAN],
                                      start=(m == 0), stop=False, skip_group_check=True)
                        o = pA[:, half * BLK:half * BLK + 2 * SPAN].rearrange("p (m s) -> p m s", m=2)
                        ins = pe.matmul(o, identb, M("window_keys").unsqueeze(1).broadcast_to([P, 2, SPAN]),
                                        start=False, stop=True, skip_group_check=True)
                    return ins
                width = (q + 1) * P if mode.kind == "causal" else SEQ
                for at in range(0, width, BLK):
                    w = min(BLK, width - at)
                    ins = pe.matmul(pA[:, at:at + w], Q[:, q * P:(q + 1) * P], K[:, WIN + at:WIN + at + w],
                                    start=True, stop=(mode.kind == "full"), skip_group_check=True)
                if mode.kind == "causal":
                    ins = pe.matmul(pA[:, width - P:width], identb, M("later_key"), start=False, stop=True,
                                    skip_group_check=True)
                return ins

            def score_part(mode, k, s):
                hh, q = divmod(s, mode.per_head)
                Q, K = QS[k][hh], KS[k][hh]
                o = pS[s % 2]
                if mode.kind == "window":
                    for c in range(2):
                        for m in range(4):
                            t = 4 * q + m
                            pe.matmul(o[0:WCH, c * BLK + m * P:c * BLK + (m + 1) * P],
                                      K[:, t * P + c * WCH:t * P + (c + 1) * WCH], Q[:, t * P:(t + 1) * P],
                                      start=(m == 0), stop=False, skip_group_check=True)
                        wm = M("window_queries")[0:WCH, c * P:(c + 1) * P]
                        ins = pe.matmul(o[0:WCH, c * BLK:(c + 1) * BLK].rearrange("p (m t) -> p m t", m=4),
                                        identb[0:WCH, 0:WCH], wm.unsqueeze(1).broadcast_to([WCH, 4, P]),
                                        start=False, stop=True, skip_group_check=True)
                    return ins
                first = first_query(mode, q)
                width = SEQ - first
                for at in range(0, width, BLK):
                    w = min(BLK, width - at)
                    ins = pe.matmul(o[:, at:at + w], K[:, WIN + q * P:WIN + (q + 1) * P],
                                    Q[:, first + at:first + at + w],
                                    start=True, stop=(mode.kind == "full"), skip_group_check=True)
                if mode.kind == "causal":
                    m0, m1 = (mo["never"][0] if q == 1 else mo["later_query"][0]), mo["later_query"][0] + P
                    ins = pe.matmul(o[:, 0:m1 - m0], identb, masks[:, m0:m1], start=False, stop=True, skip_group_check=True)
                return ins

            def value_part(mode, k, p):
                hh, q = divmod(p, mode.pairs // 2)
                v = VJ[k]
                if mode.kind == "window":
                    for m in range(4):
                        for half in range(2):
                            for c in range(2):
                                at = QUAD * (2 * c + half)
                                ins = pe.matmul(pO[hh][at:at + QUAD, m * P:(m + 1) * P],
                                                v[0:WCH, hh, 2 * (4 * half + m) + c, :],
                                                PT[(2 * p + half) % 4][0:WCH, c * BLK + m * P:c * BLK + (m + 1) * P],
                                                start=True, stop=True, skip_group_check=True)
                    return ins
                for c in range(2):
                    kt = 2 * q + c
                    first = first_query(mode, kt)
                    for half in range(2):
                        lo, hi = max(first, half * BLK), (half + 1) * BLK
                        if lo < hi:
                            at = QUAD * (2 * c + half)
                            ins = pe.matmul(pO[hh][at:at + QUAD, lo - half * BLK:BLK], v[:, hh, kt, :],
                                            PT[(2 * p + c) % 4][:, lo - first:hi - first],
                                            start=(q == 0), stop=(q == TB // 2 - 1), skip_group_check=True)
                return ins

            def run(mode, j, k, events):
                S, I, pairs = mode.steps, mode.items, mode.pairs
                ja, ka = j + 1, 1 - k
                for what, s, prev in events:
                    jj, kk = (j - 1, 1 - k) if prev else (j, k)
                    if what == "scores":
                        if s == 0:
                            pe.wait_ge(a_free, n.a + 1 + I * j + I)
                        pe.wait_ge(exp_done, n.g + S * j + (s + 1))
                        score_part(mode, k, s).then_inc(st_ready, 1)
                    elif what == "values":
                        pe.wait_ge(exp_done, n.g + S * jj + (2 * s + 4))
                        if s == 0:
                            pe.wait_ge(vj_ready, n.jobs + jj + 1)
                        if s % (pairs // 2) == 0:
                            pe.wait_ge(o_free, n.o + 2 * jj + (s // (pairs // 2) + 1))
                        value_part(mode, kk, s).then_inc(values_done, 1)
                    elif what == "gather":
                        pe.wait_ge(ot_ready, n.o + 2 * jj + (s + 1))
                        for b in range(4):
                            ins = pe.matmul(pO[s][:, b * 2 * (DH + 1):(b + 1) * 2 * (DH + 1)],
                                            OT[s][:, b * P:(b + 1) * P], C("gather"), start=True, stop=True)
                        ins.then_inc(gathered, 1)
                    elif what == "max":
                        if s % mode.per_head == 0:
                            hh = s // mode.per_head
                            pe.wait_ge(rows_clear[hh], (n.c0 if hh == 0 else n.jobs) + ja + 1)
                            pe.wait_ge(stack_in[ka][hh], n.jobs * 16 + (ja + (2 - ka)) * 16)
                        pe.wait_ge(a_free, n.a + I * ja + (s + 1))
                        max_part(mode, ka, s).then_inc(a_ready, 1)
                    elif what == "rows":
                        pe.wait_ge(negparts_ready, n.jobs + ja + 1)
                        pe.wait_ge(a_free, n.a + I * ja + I)
                        for hh in range(2):
                            at = MAXROW + QUAD * hh
                            for t in range(TB):
                                ins = pe.matmul(pA[at:at + PARTS, t * P:(t + 1) * P], negparts[:, hh * TB + t, :], identb,
                                                start=True, stop=True)
                        ins.then_inc(a_ready, 1)

            def attention(mode):
                pe.wait_ge(v_free, n.v + 2)
                pe.wait_ge(s_free, n.s + 2)
                pe.wait_ge(v_in_place, n.vp)
                run(mode, -1, 1, schedule(mode, False, True))
                run(mode, 0, 0, schedule(mode, True, True))
                with pe.Fori(0, JOBS // 2 - 1) as i:
                    run(mode, 2 * i + 1, 1, schedule(mode, True, True, True))
                    run(mode, 2 * i + 2, 0, schedule(mode, True, True, True))
                run(mode, JOBS - 1, 1, schedule(mode, True, False, True))
                run(mode, JOBS, 0, last_values(mode))
                n.a += mode.items * JOBS
                n.g += mode.steps * JOBS
                n.o += 2 * JOBS
                n.jobs += JOBS
                n.c0 += JOBS + 1
                pe.wait_ge(a_free, n.a + 1)
                pe.wait_ge(o_free, n.o + 2)

            def out_proj(mode):
                a = ATTN_OF[mode.kind]
                if mode.kind == "causal":
                    pe.wait_ge(ao_ready, 1)
                for q in range(4):
                    turn4([heads_of(4 * q + r).rearrange("p h d -> p (h d)") for r in range(4)])
                for q in range(4):
                    n.aot += 1
                    pe.wait_ge(aot_ready, n.aot)
                    bank = v_bank()
                    for r in range(4):
                        t = 4 * q + r
                        o = bank[:, r * P:(r + 1) * P]
                        pe.matmul(o, AOT[:, t * P:(t + 1) * P], a["wo"], start=True, stop=False)
                        ins = pe.matmul(o, valid[0:1, WIN:WIN + P], R(a["ob"]), start=False, stop=True)
                    ins.then_inc(v_ready, 1)

            def memory():
                wait_xt()
                for q in range(NT // 2):
                    bank = s_bank()
                    for r in range(2):
                        t = 2 * q + r
                        pe.matmul(bank[:, r * 256:r * 256 + 192], tile_cols(t),
                                  lines_w[:, 0:3, :].rearrange("p a b -> p (a b)"), start=True, stop=True)
                        ins = pe.matmul(bank[:, r * 256 + 192:(r + 1) * 256], tile_cols(t, -1), lines_w[:, 3, :],
                                        start=True, stop=True)
                    ins.then_inc(s_ready, 1)
                for q in range(4):
                    bank = s_bank()
                    for r in range(4):
                        o = bank[:, r * P:(r + 1) * P]
                        pe.matmul(o, tile_cols(4 * q + r), memv_w[:, :], start=True, stop=False)
                        ins = pe.matmul(o, valid[0:1, WIN:WIN + P], R("memv_b"), start=False, stop=True)
                    ins.then_inc(s_ready, 1)
                bank = v_bank()
                for t in range(NT):
                    o = bank[:, t * HEADS:(t + 1) * HEADS]
                    pe.matmul(o, tile_cols(t), memg_w[:, :], start=True, stop=False)
                    ins = pe.matmul(o, valid[0:1, WIN:WIN + P], R("memg_b"), start=False, stop=True)
                ins.then_inc(v_ready, 1)

            def memory_scores():
                pe.wait_ge(lines_ready, 2)
                assert n.v == MEM_V0, n.v
                nl = HEADS * LINE
                used = 0

                def turn(t):
                    bank = s_bank()
                    for m, src in enumerate((Lr, Lw)):
                        ins = pe.transpose(bank[0:nl, m * P:(m + 1) * P],
                                           src[:, t, :, :].rearrange("p h c -> p (h c)"), ident)
                    ins.then_inc(s_ready, 1)

                turn(0)
                for t in range(NT):
                    if t + 1 < NT:
                        turn(t + 1)
                    if t % TB:
                        pe.wait_ge(phi_ready, used + 1)
                        for half in range(2):
                            bank = v_bank()
                            hs = slice(half * HEADS // 2, (half + 1) * HEADS // 2)
                            pe.matmul(bank[:, 0:HEADS // 2 * PHI], C("decay_next"),
                                      phiJ[used % 2][:, hs, :].rearrange("p h c -> p (h c)"), start=True, stop=True)\
                              .then_inc(v_ready, 1)
                        used += 1
                    pe.wait_ge(jm_ready, t + 1)
                    for q in range(4):
                        bank = v_bank()
                        pe.matmul(bank, LT[t % 2][:, 0, :],
                                  JM[t % 2][:, 4 * q:4 * q + 4, :].rearrange("p h s -> p (h s)"), start=True, stop=True)\
                          .then_inc(v_ready, 1)

            pe.wait_ge(loaded, ALL_LOADED)
            bank = s_bank()
            pe.transpose(bank[:, 0:P], vec_rows[:, :], ident).then_inc(s_ready, 1)
            turn4([a1_raw[:, q, :] for q in range(4)])
            bank = v_bank()
            pe.matmul(bank[:, 0:HEADS], valid[0:1, WIN:WIN + P], R("mem_scale"), start=True, stop=True).then_inc(v_ready, 1)
            pe.wait_ge(set_up, 2)
            pe.wait_ge(vec_done, 2)
            pe.wait_ge(consts_done, 1)
            for kind, arg in PLAN:
                norm_turn()
                if kind == "moe":
                    gate(0)
                    experts(0)
                elif kind == "attn":
                    project(arg)
                    if arg is CAUSAL:
                        memory()
                        memory_scores()
                    attention(arg)
                    out_proj(arg)
                else:
                    project(arg)
                    attention(arg)
                    out_proj(arg)
                    norm_turn()
                    gate(1)
                    experts(1)

        @block.scalar
        def _(act):
            n = Count()
            act.sem_inc(s_free, 2)
            act.sem_inc(gelu_done, FC)
            act.sem_inc(exp_done, 2)

            def s_take():
                k = n.s
                n.s += 1
                act.wait_ge(s_ready, k + 1)
                return pO[k % 2][:, :]

            def norm_turn(gb=None):
                n.var += 1
                act.wait_ge(var_ready, n.var)
                act.activation(std[:, :], mv[:, :, 1], ACT.Sqrt).then_inc(std_ready, 1)
                for q in range(4):
                    bank = s_take()
                    b, at = q // 2, WIN + q % 2 * BLK
                    dst = XT[:, b, at:at + BLK]
                    if gb is None:
                        ins = act.activation(dst, bank[:, :], ACT.Copy)
                    else:
                        ins = act.activation(dst, bank[:, :], ACT.Identity, scale=vec[:, gb:gb + 1], bias=vec[:, gb + 1:gb + 2])
                    ins.then_inc(s_free, 1)
                    act.wait_ge(s_free, n.s + 2)
                    act.sem_inc(xt_ready, 1)

            def gate(layer):
                ne = EXPERTS + (1 if layer else 0)
                n.gate += 1
                act.wait_ge(gate_in, n.gate)
                act.activation(g[1][:, :, :], g[0][:, :, :], ACT.Exp).then_inc(gate_exp, 1)
                if layer:
                    n.gate += 1
                    act.wait_ge(gate_in, n.gate)
                    act.activation(coefe[:, :, :], coef2[:, :, :], ACT.Exp).then_inc(gate_exp, 1)
                for q in range(4):
                    bank = s_take()
                    act.activation(coefT[0:ne, q * BLK:(q + 1) * BLK], bank[0:ne, :], ACT.Copy).then_inc(s_free, 1)
                    act.wait_ge(s_free, n.s + 2)
                    act.sem_inc(coefT_ready, 1)

            def gelus(u, blk, k):
                act.wait_ge(y_done, u + 1)
                for c in range(FC):
                    act.wait_ge(h_ready, FC * u + (c + 1))
                    act.activation(hidden[blk % 2][:, c, :], pS[c // 2][:, c % 2 * BLK:(c % 2 + 1) * BLK], ACT.Gelu,
                                   bias=bias1[k][:, c:c + 1]).then_inc(gelu_done, 1)

            def experts(layer):
                act.preload_act_table(ACT.Gelu)
                with act.Fori(0, EXPERTS // 2) as i:
                    for k in range(2):
                        act.wait_ge(bias1_ready, n.bias1 + 2 * i + (k + 1))
                        for b in range(NBLK):
                            gelus(n.u + 2 * NBLK * i + (NBLK * k + b), b, k)
                n.u += NBLK * EXPERTS
                if layer:
                    act.wait_ge(bias1_ready, n.bias1 + EXPERTS + 1)
                    for b in range(NBLK):
                        gelus(n.u + b, b, 0)
                    n.u += NBLK
                n.bias1 += EXPERTS + 1

            def project(mode):
                if mode.kind == "window":
                    for bi in range(0, NT, 2):
                        bank = s_take()
                        b, t = bi // TB, bi % TB
                        for tt in range(2):
                            dst = VW[:, b * HEADS:(b + 1) * HEADS, t + tt, :, 0:DH].rearrange("p h c d -> p c h d")
                            src = bank[0:WCH, 2 * tt * P:2 * (tt + 1) * P].rearrange("p (c h d) -> p c h d", c=2, h=HEADS)
                            ins = act.activation(dst, src, ACT.Copy)
                        ins.then_inc(s_free, 1)
                        act.wait_ge(s_free, n.s + 2)
                        act.sem_inc(v_in_place, 1)
                else:
                    for q in range(4):
                        bank = s_take()
                        b, t = 4 * q // TB, 4 * q % TB
                        dst = V[:, b * HEADS:(b + 1) * HEADS, t:t + 4, 0:DH].rearrange("p h t d -> p t h d")
                        act.activation(dst, bank[:, :].rearrange("p (t h d) -> p t h d", t=4, h=HEADS), ACT.Copy)\
                           .then_inc(s_free, 1)
                        act.wait_ge(s_free, n.s + 2)
                        act.sem_inc(v_in_place, 1)

            def run(mode, j, k, events):
                S, I, pairs = mode.steps, mode.items, mode.pairs
                for what, s, prev in events:
                    jj = j - 1 if prev else j
                    if what == "scores":
                        act.wait_ge(st_ready, n.g + S * j + (s + 1))
                        act.wait_ge(values_done, n.p + pairs * j + (s // 2 + 1))
                        w = SEQ if mode.kind == "window" else SEQ - first_query(mode, s % mode.per_head)
                        rows = WCH if mode.kind == "window" else P
                        act.activation(PT[s % 4][0:rows, 0:w], pS[s % 2][0:rows, 0:w], ACT.Exp, scale=SCALE)\
                           .then_inc(exp_done, 1)
                    elif what == "take":
                        act.wait_ge(values_done, n.p + pairs * jj + (pairs // 2 * (s + 1) + 2))
                        act.activation(OT[s][:, :], pO[s][:, :], ACT.Copy).then_inc(ot_ready, 1)
                    elif what == "rows":
                        act.wait_ge(a_ready, n.a + I * (j + 1) + I)
                        for hh in range(2):
                            at = MAXROW + QUAD * hh
                            ins = act.activation(QS[1 - k][hh][MAXROW:MAXROW + PARTS, :], pA[at:at + PARTS, 0:SEQ], ACT.Copy)
                        ins.then_inc(a_free, 1)

            def attention(mode):
                run(mode, -1, 1, schedule(mode, False, True))
                run(mode, 0, 0, schedule(mode, True, True))
                with act.Fori(0, JOBS // 2 - 1) as i:
                    run(mode, 2 * i + 1, 1, schedule(mode, True, True, True))
                    run(mode, 2 * i + 2, 0, schedule(mode, True, True, True))
                run(mode, JOBS - 1, 1, schedule(mode, True, False, True))
                run(mode, JOBS, 0, last_values(mode))
                n.a += mode.items * JOBS
                n.g += mode.steps * JOBS
                n.p += mode.pairs * JOBS

            def out_proj(mode):
                for q in range(4):
                    bank = s_take()
                    act.activation(AOT[:, q * BLK:(q + 1) * BLK], bank[:, :], ACT.Copy).then_inc(s_free, 1)
                    act.wait_ge(s_free, n.s + 2)
                    act.sem_inc(aot_ready, 1)

            def memory():
                for q in range(NT // 2):
                    bank = s_take()
                    act.activation(pts[:, 2 * q:2 * q + 2, :, :, :].rearrange("p t g h c -> p (t g h c)"), bank[:, :], ACT.Copy)\
                       .then_inc(s_free, 1)
                    act.wait_ge(s_free, n.s + 2)
                    act.sem_inc(pts_ready, 1)
                for q in range(4):
                    bank = s_take()
                    act.activation(memval[:, 4 * q:4 * q + 4, :].rearrange("p t c -> p (t c)"), bank[:, :], ACT.Copy)\
                       .then_inc(s_free, 1)
                act.wait_ge(sig_in, 1)
                act.activation(gates[:, :, :], gates[:, :, :], ACT.Sigmoid).then_inc(sig_out, 1)
                for which in range(2):
                    act.wait_ge(norm_in, which + 1)
                    act.activation(norm[:, :, :], norm[:, :, :], ACT.Sqrt).then_inc(norm_out, 1)

            def memory_scores():
                def take(t):
                    bank = s_take()
                    if t >= 2:
                        act.wait_ge(v_ready, MEM_V0 + (t - 2) * 4 + far_items(t - 2) + 4)
                        act.wait_ge(jm_ready, t - 1)
                    act.activation(LT[t % 2][:, :, :].rearrange("p a b -> p (a b)"), bank[0:HEADS * LINE, 0:2 * P], ACT.Copy)\
                       .then_inc(s_free, 1)
                    act.wait_ge(s_free, n.s + 2)
                    act.sem_inc(lt_ready, 1)

                take(0)
                m = 0
                for t in range(NT):
                    if t + 1 < NT:
                        take(t + 1)
                    for q in range(4):
                        act.wait_ge(v_free, MEM_V0 + 4 * t + far_items(t) + q + 3)
                        act.activation(near2[m % 2][:, :, :], near[m % 2][:, :, :], ACT.Square).then_inc(near2_ready, 1)
                        m += 1
                act.wait_ge(sig_in, 2)
                act.activation(score_in[:, :, :], score_in[:, :, :], ACT.Sigmoid).then_inc(sig_out, 1)

            bank = s_take()
            act.activation(vec[:, :], bank[:, 0:P], ACT.Copy).then_inc(s_free, 1)
            bank = s_take()
            act.activation(a1_w[:, :, :].rearrange("p a b -> p (a b)"), bank[:, :], ACT.Copy).then_inc(s_free, 1)
            act.wait_ge(s_free, n.s + 2)
            act.sem_inc(vec_done, 2)
            for kind, arg in PLAN:
                if kind == "moe":
                    norm_turn()
                    gate(0)
                    experts(0)
                elif kind == "attn":
                    norm_turn()
                    project(arg)
                    if arg is CAUSAL:
                        memory()
                        memory_scores()
                    attention(arg)
                    out_proj(arg)
                else:
                    n.var += 1
                    act.wait_ge(var_ready, n.var)
                    act.activation(std[:, :], mv[:, :, 1], ACT.Sqrt).then_inc(std_ready, 1)
                    norm_turn(VEC["ln1_g"])
                    project(arg)
                    attention(arg)
                    out_proj(arg)
                    norm_turn(VEC["ln2_g"])
                    gate(1)
                    experts(1)

        @block.vector
        def _(dve):
            n = Count()

            def link(ins):
                n.step += 1
                ins.then_inc(dve_step, 1)
                dve.wait_ge(dve_step, n.step)

            def v_take():
                k = n.v
                n.v += 1
                dve.wait_ge(v_ready, k + 1)
                return pA[:, k % 2 * BLK:(k % 2 + 1) * BLK]

            def layer_norm(src, dst, signal=True):
                for t in range(NT):
                    ins = dve.bn_stats(stats[:, t, :], src[:, t, :])
                link(ins)
                for t in range(NT):
                    ins = dve.bn_aggr(mv[:, t, :], stats[:, t, :])
                link(ins)
                dve.tensor_scalar(mv[:, :, 1], mv[:, :, 1], EPS, None, ALU.add).then_inc(var_ready, 1)
                n.std += 1
                dve.wait_ge(std_ready, n.std)
                link(dve.reciprocal(rstd[:, :], std[:, :]))
                for t in range(NT):
                    ins = dve.tensor_scalar(dst[:, t, :], src[:, t, :], mv[:, t, 0:1], rstd[:, t:t + 1], ALU.subtract, ALU.mult)
                    if signal and t % 4 == 3:
                        ins.then_inc(xn_ready, 1)
                if not signal:
                    link(ins)

            def bc(ap, k):
                return ap.unsqueeze(2).broadcast_to([P, NT, k])

            def pick_largest(src, dst, m):
                link(dve.tensor_reduce(m, src, AX_X, ALU.max))
                link(dve.tensor_tensor(g[2][:, :, :], src, bc(m, EXPERTS), ALU.is_equal))
                link(dve.tensor_tensor(g[2][:, :, :], g[2][:, :, :], C("rank").unsqueeze(1).broadcast_to([P, NT, EXPERTS]),
                                       ALU.mult))
                link(dve.tensor_reduce(s1[:, 11, :], g[2][:, :, :], AX_X, ALU.max))
                link(dve.tensor_tensor(dst[:, :, :], g[2][:, :, :], bc(s1[:, 11, :], EXPERTS), ALU.is_equal))

            def gate(layer):
                bank = v_take()
                m1, m2, z, rz, e2, g2, den, rden2, w1, w2 = (s1[:, q, :] for q in range(10))
                ins = dve.tensor_copy(logits[:, :, :].rearrange("p t e -> p (t e)"), bank[:, 0:NT * EXPERTS])
                if layer:
                    ins = dve.tensor_copy(coef2[:, :, :].rearrange("p t e -> p (t e)"), bank[:, P:P + 2 * NT])
                ins.then_inc(v_free, 1)
                dve.wait_ge(v_free, n.v + 2)
                pick_largest(logits[:, :, :], pick1, m1)
                dve.tensor_tensor(g[0][:, :, :], logits[:, :, :], bc(m1, EXPERTS), ALU.subtract).then_inc(gate_in, 1)
                if layer:
                    link(dve.tensor_reduce(m2, coef2[:, :, :], AX_X, ALU.max))
                    dve.tensor_tensor(coef2[:, :, :], coef2[:, :, :], bc(m2, 2), ALU.subtract).then_inc(gate_in, 1)
                    n.gexp += 2
                    dve.wait_ge(gate_exp, n.gexp)
                    link(dve.tensor_reduce(z, g[1][:, :, :], AX_X, ALU.add))
                    link(dve.tensor_reduce(e2, coefe[:, :, :], AX_X, ALU.add))
                    link(dve.reciprocal(rz, z))
                    link(dve.reciprocal(g2, e2))
                    link(dve.tensor_scalar(g2, g2, 0.5, None, ALU.mult))
                    link(dve.tensor_tensor(w1, coefe[:, :, 0], g2, ALU.mult))
                    link(dve.tensor_tensor(w1, w1, rz, ALU.mult))
                    dve.tensor_tensor(coef[:, EXPERTS, :], coefe[:, :, 1], g2, ALU.mult)
                    dve.tensor_tensor(coef[:, 0:EXPERTS, :].rearrange("p e t -> p t e"), pick1[:, :, :], bc(w1, EXPERTS),
                                      ALU.mult).then_inc(coef_ready, 1)
                else:
                    link(dve.scalar_tensor_tensor(g[3][:, :, :], pick1[:, :, :], -3e38, logits[:, :, :], ALU.mult, ALU.add))
                    pick_largest(g[3][:, :, :], pick2, m2)
                    dve.tensor_copy(pick1b[:, :, :], pick1[:, :, :])
                    dve.tensor_copy(pick2b[:, :, :], pick2[:, :, :]).then_inc(picks_ready, 1)
                    n.gexp += 1
                    dve.wait_ge(gate_exp, n.gexp)
                    link(dve.tensor_reduce(z, g[1][:, :, :], AX_X, ALU.add))
                    link(dve.reciprocal(rz, z))
                    link(dve.tensor_tensor(g[2][:, :, :], pick2[:, :, :], g[1][:, :, :], ALU.mult))
                    link(dve.tensor_reduce(e2, g[2][:, :, :], AX_X, ALU.add))
                    link(dve.tensor_tensor(g2, e2, rz, ALU.mult))
                    link(dve.scalar_tensor_tensor(den, rz, 1e-9, g2, ALU.add, ALU.add))
                    link(dve.reciprocal(rden2, den))
                    link(dve.scalar_tensor_tensor(w1, rz, 0.5, rden2, ALU.mult, ALU.mult))
                    link(dve.scalar_tensor_tensor(w2, g2, 0.5, rden2, ALU.mult, ALU.mult))
                    for which, (pick, w) in enumerate(((pick1, w1), (pick2, w2))):
                        bank = v_take()
                        dve.scalar_tensor_tensor(g[2 + which][:, :, :].rearrange("p t e -> p (t e)"), bank[:, 0:NT * EXPERTS],
                                                 float(CAPACITY), pick[:, :, :].rearrange("p t e -> p (t e)"),
                                                 ALU.is_lt, ALU.mult).then_inc(v_free, 1)
                        dve.wait_ge(v_free, n.v + 2)
                        link(dve.tensor_tensor(g[2 + which][:, :, :], g[2 + which][:, :, :], bc(w, EXPERTS), ALU.mult))
                    dve.tensor_tensor(coef[:, 0:EXPERTS, :].rearrange("p e t -> p t e"), g[2][:, :, :], g[3][:, :, :],
                                      ALU.add).then_inc(coef_ready, 1)
                for q in range(4):
                    bank = v_take()
                    x4 = X[:, 4 * q:4 * q + 4, :].rearrange("p t c -> p (t c)")
                    dve.tensor_tensor(x4, bank, x4, ALU.add).then_inc(v_free, 1)
                dve.wait_ge(v_free, n.v + 2)

            def add_unit(u, blk, e):
                dve.wait_ge(y_done, u + 3)
                dve.wait_ge(y_free, u + 2)
                for r in range(4):
                    t = 4 * blk + r
                    ins = dve.scalar_tensor_tensor(X[:, t, :], pO[blk % 2][:, r * P:(r + 1) * P], coef[:, bass.ds(e, 1), t]
                                                   , X[:, t, :], ALU.mult, ALU.add)
                ins.then_inc(y_free, 1)

            def take_bias(k, at):
                dve.tensor_scalar(bias1[k][:, :], vec[:, bass.ds(at, FC)], 1.0, None, ALU.mult).then_inc(bias1_ready, 1)

            def experts(layer):
                base = VEC["f1_b1" if layer else "f0_b1"]
                take_bias(0, base)
                with dve.Fori(0, EXPERTS // 2) as i:
                    take_bias(1, base + 2 * FC * i + FC)
                    for m in range(2 * NBLK):
                        add_unit(n.u + 2 * NBLK * i + m, m % NBLK, 2 * i + m // NBLK)
                        if m == NBLK - 1:
                            take_bias(0, base + 2 * FC * i + 2 * FC)
                n.u += NBLK * EXPERTS
                if layer:
                    for m in range(NBLK):
                        add_unit(n.u + m, m, EXPERTS)
                    n.u += NBLK
                dve.wait_ge(y_free, n.u + 2)

            def project(mode):
                a = ATTN_OF[mode.kind]
                if n.stored:
                    dve.wait_ge(stack_stored, n.stored)
                n.stored += 16 * 24
                for which, (dst, off, bias) in enumerate(((Qp, 0, a["qb"]), (Kp, WIN, a["kb"]))):
                    for b in range(NBLK):
                        bank = v_take()
                        cols = [p[:, b // 2, off + b % 2 * BLK:off + (b % 2 + 1) * BLK] for p in dst]
                        bcol = vec[:, bias:bias + 1]
                        link(dve.tensor_scalar(cols[0], bank, bcol, None, ALU.add))
                        dve.scalar_tensor_tensor(rest[:, :], bank, bcol, cols[0], ALU.add, ALU.subtract).then_inc(v_free, 1)
                        dve.wait_ge(v_free, n.v + 2)
                        link(dve.tensor_copy(cols[1], rest[:, :]))
                        link(dve.tensor_tensor(cols[2], rest[:, :], cols[1], ALU.subtract))
                    dve.sem_inc(parts_ready, 1)

            def clear_rows(k, hh):
                dve.memset(QS[k][hh][MAXROW:MAXROW + PARTS, :], 0.0).then_inc(rows_clear[hh], 1)

            def copy_v(mode, j, k):
                if mode.kind == "window":
                    for hh in range(2):
                        ins = dve.tensor_scalar(VJ[k][0:WCH, hh, :, 0:DH],
                                                VW[:, bass.ds(2 * j + hh, 1), :, :, :].rearrange("p a t c d -> p (a t c) d"),
                                                1.0, None, ALU.mult)
                else:
                    ins = dve.tensor_scalar(VJ[k][:, :, 0:TB, 0:DH], V[:, bass.ds(2 * j, 2), :, :], 1.0, None, ALU.mult)
                ins.then_inc(vj_ready, 1)

            def run(mode, j, k, events, base):
                S, I, pairs = mode.steps, mode.items, mode.pairs
                ja, ka = j + 1, 1 - k
                with_a = ("split", 0, False) in events
                c = 0
                for what, s, prev in events:
                    jj = j - 1 if prev else j
                    if what == "scores" and s == S // 2 and with_a:
                        dve.wait_ge(st_ready, n.g + S * j + S // 2)
                        clear_rows(k, 0)
                    elif what == "values" and prev and s == pairs - 1 and with_a:
                        dve.wait_ge(st_ready, n.g + S * j)
                        clear_rows(ka, 1)
                    elif what == "max":
                        dve.wait_ge(a_ready, n.a + I * ja + (s + 1))
                        hh, q = divmod(s, mode.per_head)
                        if mode.kind == "window":
                            src = pA[:, :].rearrange("p (b f) -> p b f", b=2)[:, :, 0:2 * SPAN]\
                                .rearrange("p b (m s) -> p b m s", m=2)
                            at = hh * TB + 4 * q
                            dst = negmax[:, at:at + 4].rearrange("p (b m) -> p b m", b=2)
                        else:
                            src = pA[:, 0:(q + 1) * P if mode.kind == "causal" else SEQ]
                            dst = negmax[:, hh * TB + q:hh * TB + q + 1]
                        dve.tensor_reduce(dst, src, AX_X, ALU.max, negate=True).then_inc(a_free, 1)
                    elif what == "split":
                        dve.wait_ge(a_free, n.a + 1 + I * ja + mode.maxes)
                        dve.tensor_copy(negparts[:, :, 0], negmax[:, :]).then_inc(dve_step, 1)
                        dve.wait_ge(dve_step, base + (c + 1))
                        dve.tensor_tensor(negrest[:, :], negmax[:, :], negparts[:, :, 0], ALU.subtract).then_inc(dve_step, 1)
                        dve.wait_ge(dve_step, base + (c + 2))
                        dve.tensor_copy(negparts[:, :, 1], negrest[:, :]).then_inc(dve_step, 1)
                        dve.wait_ge(dve_step, base + (c + 3))
                        dve.tensor_tensor(negparts[:, :, 2], negrest[:, :], negparts[:, :, 1], ALU.subtract)\
                            .then_inc(negparts_ready, 1)
                        c += 3
                    elif what == "gather":
                        dve.wait_ge(o_free, n.o + 2 * jj + (s + 2))
                        dve.wait_ge(gathered, n.o + 2 * jj + (s + 1))
                        o = pO[s][:, 0:TB * (DH + 1)].rearrange("p (b h d) -> p b h d", b=4, h=2)
                        c += 1
                        dve.reciprocal(rden[:, :, :], o[:, :, :, DH]).then_inc(dve_step, 1)
                        dve.wait_ge(dve_step, base + c)
                        dve.tensor_tensor(AO[:, :, bass.ds(2 * jj + s, 1), :].rearrange("p (h b) a d -> p b h (a d)", h=2),
                                          o[:, :, :, 0:DH], rden[:, :, :].unsqueeze(3).broadcast_to([P, 4, 2, DH]), ALU.mult)\
                            .then_inc(o_free, 1)
                        if s == 1 and with_a:
                            copy_v(mode, ja, ka)
                return c

            def attention(mode):
                for k in range(2):
                    for hh in range(2):
                        clear_rows(k, hh)
                n.vp += NT // 2 if mode.kind == "window" else NT // 4
                dve.wait_ge(v_in_place, n.vp)
                copy_v(mode, 0, 0)
                copy_v(mode, 1, 1)
                n.step += run(mode, -1, 1, schedule(mode, False, True), n.step)
                n.step += run(mode, 0, 0, schedule(mode, True, True), n.step)
                with dve.Fori(0, JOBS // 2 - 1) as i:
                    c = run(mode, 2 * i + 1, 1, schedule(mode, True, True, True), n.step + 10 * i)
                    c += run(mode, 2 * i + 2, 0, schedule(mode, True, True, True), n.step + 5 + 10 * i)
                assert c == 10
                n.step += c * (JOBS // 2 - 1)
                n.step += run(mode, JOBS - 1, 1, schedule(mode, True, False, True), n.step)
                n.step += run(mode, JOBS, 0, last_values(mode), n.step)
                n.a += mode.items * JOBS
                n.g += mode.steps * JOBS
                n.o += 2 * JOBS
                dve.wait_ge(o_free, n.o + 2)

            def out_proj(mode):
                for q in range(4):
                    bank = v_take()
                    ts = slice(4 * q, 4 * q + 4)
                    x4, lx4, x1 = (a[:, ts, :].rearrange("p t c -> p (t c)") for a in (X, LX, XN))
                    if mode.kind == "full":
                        dve.tensor_tensor(x1, bank, lx4, ALU.add).then_inc(v_free, 1)
                        dve.wait_ge(v_free, n.v + 2)
                        link(dve.scalar_tensor_tensor(x4, x1, 0.5, x4, ALU.mult, ALU.add))
                    else:
                        dve.tensor_tensor(x4, bank, x4, ALU.add).then_inc(v_free, 1)
                dve.wait_ge(v_free, n.v + 2)

            def memory():
                bank = v_take()
                dve.tensor_copy(gates[:, :, :].rearrange("p t h -> p (t h)"), bank[:, 0:NT * HEADS]).then_inc(v_free, 1)
                dve.wait_ge(v_free, n.v + 2)
                dve.sem_inc(sig_in, 1)
                for which in range(2):
                    dve.wait_ge(sq_ready, which + 1)
                    link(dve.tensor_reduce(norm[:, :, :].rearrange("p t h -> p (t h)"),
                                           sq[:, :, :, :].rearrange("p t h c -> p (t h) c"), AX_X, ALU.add))
                    dve.tensor_scalar(norm[:, :, :], norm[:, :, :], 1e-24, None, ALU.max).then_inc(norm_in, 1)
                    dve.wait_ge(norm_out, which + 1)
                    dve.reciprocal(rnorm[which][:, :, :], norm[:, :, :]).then_inc(rnorm_ready, 1)
                    dve.wait_ge(rnorm_ready, which + 1)

            def memory_scores():
                assert n.v == MEM_V0, n.v
                m, used = 0, 0

                def near_sum(m):
                    dve.wait_ge(near2_ready, m + 1)
                    return dve.tensor_reduce(score_in[:, m // 4, m % 4 * 4:m % 4 * 4 + 4], near2[m % 2][:, :, :], AX_X, ALU.add)

                for t in range(NT):
                    if t % TB:
                        dve.wait_ge(phi_ready, used + 1)
                        for half in range(2):
                            bank = v_take()
                            hs = slice(half * HEADS // 2, (half + 1) * HEADS // 2)
                            f = far[:, hs, :].rearrange("p h c -> p (h c)")
                            if t % TB == 1:
                                dve.tensor_copy(f, bank[:, 0:HEADS // 2 * PHI]).then_inc(v_free, 1)
                            else:
                                dve.scalar_tensor_tensor(f, f, DECAY ** P, bank[:, 0:HEADS // 2 * PHI], ALU.mult, ALU.add)\
                                    .then_inc(v_free, 1)
                            dve.wait_ge(v_free, n.v + 2)
                            link(dve.tensor_tensor(farp[:, :, :], far[:, hs, :], phiR[used % 2][:, hs, :], ALU.mult))
                            link(dve.tensor_reduce(score_far[:, t, hs], farp[:, :, :], AX_X, ALU.add))
                        used += 1
                        dve.sem_inc(phi_used, 1)
                    for q in range(4):
                        bank = v_take()
                        dve.tensor_tensor(near[m % 2][:, :, :], bank.rearrange("p (h s) -> p h s", h=4),
                                          C("decay_root").unsqueeze(1).broadcast_to([P, 4, P]), ALU.mult)\
                            .then_inc(v_free, 1)
                        dve.wait_ge(v_free, n.v + 2)
                        if m:
                            near_sum(m - 1)
                        m += 1
                link(near_sum(m - 1))
                for b in range(BATCH):
                    ts = slice(b * TB + 1, (b + 1) * TB)
                    link(dve.tensor_tensor(score_in[:, ts, :], score_in[:, ts, :], score_far[:, ts, :], ALU.add))
                dve.tensor_tensor(score_in[:, :, :], score_in[:, :, :], scale16[:, :].unsqueeze(1)
                                  .broadcast_to([P, NT, HEADS]), ALU.mult).then_inc(sig_in, 1)
                dve.wait_ge(sig_out, 2)
                link(dve.tensor_tensor(score_in[:, :, :], score_in[:, :, :], gates[:, :, :], ALU.mult))
                link(dve.tensor_reduce(gated[:, :], score_in[:, :, :], AX_X, ALU.add))
                link(dve.tensor_scalar(gated[:, :], gated[:, :], 1.0 / HEADS, None, ALU.mult))

            def add_memory():
                for t in range(NT):
                    a = heads_of(t)
                    ins = dve.scalar_tensor_tensor(a, memval[:, t, :].rearrange("p (h d) -> p h d", h=HEADS),
                                                   gated[:, t:t + 1], a, ALU.mult, ALU.add)
                link(ins)
                dve.sem_inc(ao_ready, 1)

            dve.sem_inc(v_free, 2)
            dve.sem_inc(y_free, 2)
            dve.sem_inc(y_done, 2)
            dve.sem_inc(a_free, 1)
            dve.sem_inc(o_free, 2)
            dve.sem_inc(values_done, 2)
            dve.wait_ge(loaded, ALL_LOADED)
            dve.tensor_copy(masks[:, :], mask_in[:, :]).then_inc(consts_done, 1)
            bank = v_take()
            dve.tensor_copy(scale16[:, :], bank[:, 0:HEADS]).then_inc(v_free, 1)
            dve.wait_ge(v_free, n.v + 2)
            dve.wait_ge(x_loaded, 16)
            dve.wait_ge(vec_done, 2)
            for kind, arg in PLAN:
                if kind == "moe":
                    layer_norm(X, XN)
                    gate(0)
                    experts(0)
                elif kind == "attn":
                    layer_norm(X, XN)
                    project(arg)
                    if arg is CAUSAL:
                        memory()
                        memory_scores()
                    attention(arg)
                    if arg is CAUSAL:
                        add_memory()
                    out_proj(arg)
                else:
                    layer_norm(X, LX, False)
                    layer_norm(LX, XN)
                    project(arg)
                    attention(arg)
                    out_proj(arg)
                    layer_norm(XN, XN)
                    gate(1)
                    experts(1)
            dve.sem_inc(x_final, 1)


_INS = ['L0_attn_x', 'L0_attn_qkv_w', 'L0_attn_qkv_b', 'L0_attn_w1w', 'L0_attn_w2w', 'L0_attn_r1w', 'L0_attn_r2w',
        'L0_attn_memv_w', 'L0_attn_memv_b', 'L0_attn_memg_w', 'L0_attn_memg_b', 'L0_attn_mem_scale', 'L0_attn_out_w',
        'L0_attn_out_b', 'L0_ffn_Wg', 'L0_ffn_W1', 'L0_ffn_b1', 'L0_ffn_W2', 'L0_ffn_b2', 'L1_attn_q_w', 'L1_attn_q_b',
        'L1_attn_k_w', 'L1_attn_k_b', 'L1_attn_v_w', 'L1_attn_v_b', 'L1_attn_o_w', 'L1_attn_o_b', 'L1_ffn_ln1_g',
        'L1_ffn_ln1_b', 'L1_ffn_Wqkv', 'L1_ffn_bqkv', 'L1_ffn_Wo', 'L1_ffn_bo', 'L1_ffn_ln2_g', 'L1_ffn_ln2_b',
        'L1_ffn_gate_w', 'L1_ffn_W1', 'L1_ffn_b1', 'L1_ffn_W2', 'L1_ffn_b2', 'L1_ffn_rW1', 'L1_ffn_rb1', 'L1_ffn_rW2',
        'L1_ffn_rb2', 'L1_ffn_coef_w', 'L1_ffn_coef_b']


def constants():
    at = np.arange(P)
    row_, col = at[:, None], at[None, :]
    co, nconst = offsets(CONST_COLS)
    mo, nmask = offsets(MASK_COLS)
    const = np.zeros((P, nconst), np.float32)
    mask = np.zeros((P, nmask), np.float32)

    def put(where, cols, name, value):
        where[:, cols[name][0]:cols[name][0] + cols[name][1]] = value

    far_off = -1e30
    put(const, co, "ident", row_ == col)
    put(const, co, "decay_root", np.where(col < row_, DECAY ** ((row_ - col) / 2.0), 0.0))
    put(const, co, "decay_next", DECAY ** (P + col - row_ + 0.0))
    put(const, co, "rank", EXPERTS - np.arange(EXPERTS)[None, :])
    put(const, co, "same_head", row_ // LINE == np.arange(HEADS)[None, :])
    j = np.arange(2 * (DH + 1))[None, :]
    put(const, co, "gather", (row_ // QUAD % 2 == j // (DH + 1)) & (row_ % QUAD == j % (DH + 1)))
    put(mask, mo, "ident", row_ == col)
    put(mask, mo, "before", row_ < col)
    put(mask, mo, "ones", 1.0)
    put(mask, mo, "later_key", np.where(col > row_, far_off, 0.0))
    put(mask, mo, "never", far_off)
    put(mask, mo, "later_query", np.where(row_ > col, far_off, 0.0))
    key = np.arange(SPAN)[None, :]
    put(mask, mo, "window_keys", np.where((key >= row_) & (key <= row_ + 2 * WIN), 0.0, far_off))
    key = np.concatenate([row_, row_ + WCH], 1)[:, :, None]
    query = at[None, None, :]
    put(mask, mo, "window_queries",
        np.where((key >= query) & (key <= query + 2 * WIN), 0.0, far_off).reshape(P, 2 * P))
    valid = np.zeros((1, PADDED), np.float32)
    valid[:, WIN:WIN + SEQ] = 1.0
    return {"consts": const, "mask_consts": mask, "valid": valid}


def kernel(**inputs):
    import concourse.bacc as _bacc
    from concourse.bass_utils import run_bass_kernel_spmd as _run

    nc = _bacc.Bacc("TRN2", target_bir_lowering=False, num_devices=1)
    arrays, d = {}, {}
    given = {name: np.ascontiguousarray(inputs[name]) for name in _INS}
    for name, a in {**given, **constants()}.items():
        arrays[f"in_{name}_dram"] = a
        d[name] = nc.dram_tensor(f"in_{name}_dram", a.shape, mybir.dt.from_np(a.dtype), kind="ExternalInput").ap()
    out = nc.dram_tensor("out_0_dram", (BATCH, SEQ, DIM), F32, kind="ExternalOutput").ap()
    build(nc, d, out)
    r = _run(nc, [arrays], core_ids=[0])
    return r.results[0]["out_0_dram"]
```

```python
from contextlib import ExitStack

import numpy as np

import concourse.bass as bass
from concourse import mybir

ALU = mybir.AluOpType
ACT = mybir.ActivationFunctionType
AX_X = mybir.AxisListType.X
F32 = mybir.dt.float32
BF16 = mybir.dt.bfloat16
F32R = mybir.dt.float32r

P = 128
BATCH, SEQ, DIM = 2, 1024, 128
TB = SEQ // P
NT = BATCH * TB
HEADS, DH = 16, DIM // 16
WIN = 32
PADDED = SEQ + 2 * WIN
SPAN = P + 2 * WIN
WQ = P - 2 * WIN
EXPERTS, FFN = 8, 512
FC = FFN // P
BLK = 512
NBLK = BATCH * SEQ // BLK
CAPACITY = 2 * 2 * BATCH * SEQ // EXPERTS
PARTS = 3
ROWS = 6 * DH
MAXROW = 32
LOAD_ROWS = ROWS + PARTS
STACK = 96
QUAD = 32
SCALE = float(DH) ** -0.5
EPS = 1e-5
LINE = 6
PHI = LINE * LINE
DECAY = 0.99
PAIRS = [(0, 1), (0, 2), (0, 3), (1, 2), (1, 3), (2, 3)]
JOBS = BATCH * HEADS // 2
Q_PART = [0, 0, 1, 0, 2, 1]
K_PART = [0, 1, 0, 2, 0, 1]

WARM = 96
GATHER = WARM
LOGITS1 = EXPERTS + 2
HEAD_ROWS = [range(g * DH + (PARTS if g * DH >= MAXROW else 0), (g + 1) * DH + (PARTS if g * DH >= MAXROW else 0))
             for g in range(6)]

CONST_COLS = {"ident": P, "decay_root": P, "decay_next": P, "rank": EXPERTS, "same_head": HEADS, "gather": GATHER,
              "gather_window": 2 * GATHER}
MASK_COLS = {"ident": P, "before": P, "ones": P, "later_key": P, "later_query": P, "window_keys": SPAN,
             "window_queries": WQ}
VEC = {"f0_b1": 0, "f1_b1": 32, "rb1": 64, "a0_b": 68, "f1_b": 71, "ln1_g": 74, "ln1_b": 75, "ln2_g": 76,
       "ln2_b": 77, "a1_qb": 78, "a1_kb": 79}
ROW = {"a0_vb": (0, 128), "f1_vb": (128, 128), "a1_vb": (256, 128), "a0_ob": (384, 128), "f1_ob": (512, 128),
       "a1_ob": (640, 128), "memv_b": (768, 128), "memg_b": (896, 16), "mem_scale": (912, 16), "coef_b": (928, 2)}


def offsets(cols):
    out, at = {}, 0
    for name, n in cols.items():
        out[name] = (at, n)
        at += n
    return out, at


class Mode:

    def __init__(self, kind):
        self.kind = kind
        if kind == "full":
            self.steps = [[(kt, 0)] for kt in range(TB)]
            self.groups = [[2 * g, 2 * g + 1] for g in range(TB // 2)]
            self.products = [(g, (z,)) for g in range(TB // 2) for z in range(2)]
            self.units = [(t, at, BLK) for t in range(TB) for at in range(0, SEQ, BLK)]
        elif kind == "causal":
            self.steps = [[(0, 0)]] + [[(kt, 0), (TB - kt, SEQ - kt * P)] for kt in range(1, TB // 2)] + [[(TB // 2, 0)]]
            self.groups = [[0, 1], [2, 3], [4]]
            self.products = [(0, (0,)), (0, (1,)), (1, (0,)), (1, (1,)), (2, (1,))]
            self.units = [(t, at * P, w * P) for t, at, w in (
                (3, 0, 4), (4, 4, 1), (4, 0, 4), (5, 0, 4), (0, 0, 1), (6, 0, 4),
                (7, 0, 4), (1, 0, 2), (6, 4, 3), (7, 4, 4), (5, 4, 2), (2, 0, 3))]
        else:
            self.steps = [[]]
            self.groups = [[0]]
            self.products = [(0, (0, 1))]
            self.units = [(t, 0, SPAN) for t in range(0, TB, 2)]
        self.R, self.S = len(self.steps), 2 * len(self.steps)
        self.V, self.U = len(self.products), len(self.units)
        self.rows_step = min(self.R - 1, 2)
        assert self.U % 2 == 0

    def width(self, r):
        return SEQ // 2 if self.kind == "causal" and r == self.R - 1 else SEQ

    def buffer(self, k, s):
        return (self.S * k + s) % 4

    def schedule(self, with_b, with_a, carry=True):
        at_step = {}
        for hh in range(2):
            for m, (g, _) in enumerate(self.products):
                second = m > 0 and self.products[m - 1][0] == g
                at = self.R * hh + self.groups[g][-1] + (2 if second else 1)
                at_step.setdefault(at, []).append(("values", self.V * hh + m))
            at_step[at].append(("take", hh))
            at_step.setdefault(at + 1, []).insert(0, ("gather", hh))
        if not with_b and not with_a:
            return [(what, x, True) for at in sorted(at_step) if at >= self.S for what, x in at_step[at]]
        if not with_b:
            out = []
            for hh in range(2):
                out += [("max", self.U * hh + u, False) for u in range(self.U)] + [("split", hh, False)]
                if hh == 0:
                    out.append(("rows", 0, False))
            return out
        out = []
        for s in range(self.S):
            hh, r = divmod(s, self.R)
            rows = [("rows", 1 - hh, hh == 0)] if r == self.rows_step and (with_a or hh == 0) else []
            if self.R == 1:
                out += rows
                rows = []
            out.append(("scores", s, False))
            due = [(w, x, True) for w, x in at_step.get(s + self.S, []) if carry]
            due += [(w, x, False) for w, x in at_step.get(s, [])]
            if rows or self.R == 1:
                out += [e for e in due if e[0] == "gather"] + rows
                due = [e for e in due if e[0] != "gather"]
            if self.R == 1:
                first, last, cut = 0, self.U, self.U
            else:
                m = r if r < self.rows_step else r - 1
                first, last = ((0, 0) if r == self.rows_step
                               else (self.U * m // (self.R - 1), self.U * (m + 1) // (self.R - 1)))
                cut = (first + last) // 2
            units = [("max", self.U * hh + u, False) for u in range(first, last)] if with_a else []
            out += units[:cut - first] + due + units[cut - first:]
            if with_a and r == self.R - 1:
                out.append(("split", hh, False))
        return out


class Count:

    v = s = a = g = o = p = u = w0 = w1 = xn = xt = coef = coefT = picks = vp = aot = jobs = rows = xs = projections = first = 0
    stored = parts = s_in = step = var = std = gate = gexp = bias1 = 0


def build(nc, d, out, LAYERS=6):
    co, nconst = offsets(CONST_COLS)
    mo, nmask = offsets(MASK_COLS)
    MODES = [Mode("causal"), Mode("full"), Mode("window")]
    CAUSAL, FULL, WINDOW = MODES

    with ExitStack() as ctx:
        def sb(name, shape, dt=F32):
            return ctx.enter_context(nc.sbuf_tensor(name, shape, dt))

        def ps(name, shape):
            return ctx.enter_context(nc.psum_tensor(name, shape, F32))

        def sem(name):
            return ctx.enter_context(nc.semaphore(name))

        q_dram = nc.dram_tensor("q_stack_dram", (BATCH, HEADS, LOAD_ROWS, SEQ), BF16, kind="Internal").ap()
        k_dram = nc.dram_tensor("k_stack_dram", (BATCH, HEADS, LOAD_ROWS, PADDED), BF16, kind="Internal").ap()
        q_heads = q_dram.rearrange("b h r t -> (b h) r t")
        k_heads = k_dram.rearrange("b h r t -> (b h) r t")

        X = sb("X", [P, NT, DIM])
        LX = sb("LX", [P, NT, DIM])
        XN = sb("XN", [P, NT, DIM])
        XT = sb("XT", [P, BATCH, PADDED])
        stats = sb("stats", [P, NT, 6])
        mv = sb("mv", [P, NT, 2])
        std = sb("std", [P, NT])
        rstd = sb("rstd", [P, NT])

        const = sb("const", [P, nconst])
        masks = sb("masks", [P, nmask], BF16)
        mask_in = LX[:, :, :].rearrange("p t c -> p (t c)")[:, 0:nmask]
        assert nmask <= 1536
        valid = sb("valid", [1, PADDED])
        vec_rows = sb("vec_rows", [P, P])
        vec = sb("vec", [P, P])
        row = sb("row", [1, 930])
        b2_0 = sb("b2_0", [WARM, DIM])
        b2_1 = sb("b2_1", [WARM, DIM])

        def C(name):
            return const[:, co[name][0]:co[name][0] + co[name][1]]

        def M(name):
            return masks[:, mo[name][0]:mo[name][0] + mo[name][1]]

        def R(name):
            return row[0:1, ROW[name][0]:ROW[name][0] + ROW[name][1]]

        ident, identb = C("ident"), M("ident")

        a0_qkv = sb("a0_qkv", [P, 3 * DIM])
        a0_out = sb("a0_out", [P, DIM])
        lines_w = sb("lines_w", [P, 4, 4 * HEADS])
        mem_w = sb("mem_w", [P, HEADS + DIM])
        memg_w, memv_w = mem_w[:, 0:HEADS], mem_w[:, HEADS:HEADS + DIM]
        gate_w = sb("gate_w", [P, EXPERTS + WARM])
        f0_gate, f1_gate = gate_w[:, 0:EXPERTS], gate_w[:, EXPERTS:2 * EXPERTS]
        coef_w = gate_w[:, 2 * EXPERTS:2 * EXPERTS + 2]
        f1_qkv = sb("f1_qkv", [P, 3 * DIM])
        f1_out = sb("f1_out", [P, DIM])
        LX_all = LX[:, :, :].rearrange("p t c -> p (t c)")
        a1_raw = LX_all[:, 1536:2048].rearrange("p (a b) -> p a b", a=4)
        a1_w = sb("a1_w", [P, 4, DIM])

        W1 = [sb(f"W1_{k}", [P, FFN]) for k in range(2)]
        W2 = [sb(f"W2_{k}", [P, FC, DIM]) for k in range(2)]
        bias1 = [sb(f"bias1_{k}", [P, FC]) for k in range(2)]
        hidden_all = sb("hidden", [P, 2, FC, BLK])
        hidden = [hidden_all[:, k] for k in range(2)]

        logits = sb("logits", [P, NT, EXPERTS])
        g = [sb(f"gate_{k}", [P, NT, EXPERTS]) for k in range(4)]
        pick1 = sb("pick1", [P, NT, EXPERTS])
        pick2 = sb("pick2", [P, NT, EXPERTS])
        pick1b = sb("pick1b", [P, NT, EXPERTS], BF16)
        pick2b = sb("pick2b", [P, NT, EXPERTS], BF16)
        s1 = sb("s1", [P, 12, NT])
        coef2 = sb("coef2", [P, NT, 2])
        coefe = sb("coefe", [P, NT, 2])
        coef = sb("coef", [P, EXPERTS + 1, NT])
        memval = sb("memval", [P, NT, DIM])
        memval_rows = memval[0:WARM].rearrange("e t c -> e (t c)")
        coefT = memval_rows[0:EXPERTS + 1, :]

        Qp = [sb(f"Qp_{k}", [P, BATCH, SEQ], BF16) for k in range(PARTS)]
        Kp = [sb(f"Kp_{k}", [P, BATCH, PADDED], BF16) for k in range(PARTS)]
        rest = sb("rest", [P, BLK])
        QS = [[sb(f"QS_{k}_{hh}", [STACK, SEQ], BF16) for hh in range(2)] for k in range(2)]
        KS = [[sb(f"KS_{k}_{hh}", [STACK, PADDED], BF16) for hh in range(2)] for k in range(2)]
        V = sb("V", [P, BATCH * HEADS, TB, DH])
        attention_only = ExitStack()
        VW_all = attention_only.enter_context(nc.sbuf_tensor("VW", [P, 3 * NT * HEADS * LINE], F32))
        AOT = attention_only.enter_context(nc.sbuf_tensor("AOT", [P, NT * P], F32))
        attention_only.close()
        experts_only = ExitStack()
        XS = [experts_only.enter_context(nc.sbuf_tensor(f"XS_{m}", [P, NBLK, BLK], F32R)) for m in range(2)]
        W1S = [[experts_only.enter_context(nc.sbuf_tensor(f"W1S_{k}_{m}", [P, FFN], F32R)) for m in range(2)] for k in range(2)]
        experts_only.close()
        ctx.enter_context(nc.sbuf_tensor("attention_or_experts", [P, 3 * NT * HEADS * LINE + NT * P], F32))
        VW = VW_all[:, 0:BATCH * HEADS * 2 * TB * DH].rearrange("p (b u d) -> p b u d", b=BATCH * HEADS, u=2 * TB)
        VJ = [sb(f"VJ_{k}", [P, 2, 2 * TB, QUAD]) for k in range(2)]
        PT = [Qp[k][:, :, :].rearrange("p b t -> p (b t)").bitcast(F32) for k in range(PARTS)] + [sb("PT", [P, SEQ])[:, :]]
        OT = [sb(f"OT_{k}", [P, BLK]) for k in range(2)]
        zeros = sb("zeros", [P, QUAD])
        negmax2 = sb("negmax2", [P, 2, TB, 2])
        negmax = sb("negmax", [P, 2, TB])
        negrest = sb("negrest", [P, 2, TB])
        negparts = sb("negparts", [P, 2, TB, PARTS], BF16)
        rden = sb("rden", [P, 4, 2])
        AO = sb("AO", [P, TB, BATCH * HEADS, DH])

        pts = hidden_all[:, :, :, :].rearrange("p k c b -> p (k c b)")\
            .rearrange("p (t g h c) -> p t g h c", t=NT, g=4, h=HEADS)
        n_line = NT * HEADS * LINE
        Lw, Lr, sq = (VW_all[:, k * n_line:(k + 1) * n_line].rearrange("p (t h c) -> p t h c", t=NT, h=HEADS)
                      for k in range(3))
        prod = [sb(f"prod_{k}", [P, NT, HEADS]) for k in range(2)]
        norm = sb("norm", [P, NT, HEADS])
        rnorm = [sb(f"rnorm_{k}", [P, NT, HEADS]) for k in range(2)]
        LT = [sb(f"LT_{k}", [HEADS * LINE, 2, P]) for k in range(2)]
        JM = [LX[0:HEADS * LINE, :, :], AOT[0:HEADS * LINE, :].rearrange("p (h s) -> p h s", h=HEADS)]
        AO_all = AO[:, :, :, :].rearrange("p t b d -> p (t b d)")
        hid = hidden_all[:, :, :, :].rearrange("p k c b -> p (k c b)")
        HP = HEADS * PHI
        phiR = [AO_all[:, k * HP:(k + 1) * HP].rearrange("p (h c) -> p h c", h=HEADS) for k in range(2)]
        phiJ = [a.rearrange("p (h c) -> p h c", h=HEADS) for a in (AO_all[:, 2 * HP:3 * HP], hid[:, 4 * BLK:4 * BLK + HP])]
        far = hid[:, 4 * BLK + HP:4 * BLK + 2 * HP].rearrange("p (h c) -> p h c", h=HEADS)
        farp = hid[:, 4 * BLK + 2 * HP:4 * BLK + 2 * HP + HP // 2].rearrange("p (h c) -> p h c", h=HEADS // 2)
        near = [hid[:, k * BLK:(k + 1) * BLK].rearrange("p (h s) -> p h s", h=4) for k in range(2)]
        near2 = [hid[:, k * BLK:(k + 1) * BLK].rearrange("p (h s) -> p h s", h=4) for k in range(2, 4)]
        score_in = sb("score_in", [P, NT, HEADS])
        score_far = sb("score_far", [P, NT, HEADS])
        gates = sb("gates", [P, NT, HEADS])
        row_wide = sb("row_wide", [P, HEADS + 2])
        scale16, coef_b = row_wide[:, 0:HEADS], row_wide[:, HEADS:HEADS + 2]
        gated = sb("gated", [P, NT])

        pA = ps("pA", [P, 2 * BLK])
        pS = [ps(f"pS_{k}", [P, 2 * BLK]) for k in range(2)]
        pO = [ps(f"pO_{k}", [P, BLK]) for k in range(2)]

        first_loaded = sem("first_loaded")
        loaded = sem("loaded")
        x_loaded = sem("x_loaded")
        set_up = sem("set_up")
        consts_done = sem("consts_done")
        vec_done = sem("vec_done")
        v_ready, v_free = sem("v_ready"), sem("v_free")
        s_ready, s_free = sem("s_ready"), sem("s_free")
        dve_step, pool_step = sem("dve_step"), sem("pool_step")
        var_ready, std_ready = sem("var_ready"), sem("std_ready")
        xn_ready, xt_ready = sem("xn_ready"), sem("xt_ready")
        gate_in, gate_exp = sem("gate_in"), sem("gate_exp")
        picks_ready, coef_ready, coefT_ready = sem("picks_ready"), sem("coef_ready"), sem("coefT_ready")
        w_in = [sem(f"w_in_{k}") for k in range(2)]
        h_ready, gelu_done = sem("h_ready"), sem("gelu_done")
        y_done, y_free = sem("y_done"), sem("y_free")
        bias1_ready = sem("bias1_ready")
        x_split = sem("x_split")
        w1_high = [sem(f"w1_high_{k}") for k in range(2)]
        w1_split = [sem(f"w1_split_{k}") for k in range(2)]
        parts_ready, stack_stored = sem("parts_ready"), sem("stack_stored")
        stack_in = [[sem(f"stack_in_{k}_{hh}") for hh in range(2)] for k in range(2)]
        fixed_rows = sem("fixed_rows")
        vj_ready = sem("vj_ready")
        a_ready, a_free = sem("a_ready"), sem("a_free")
        negparts_ready, rows_ready = sem("negparts_ready"), sem("rows_ready")
        rows_out = sem("rows_out")
        st_ready, exp_done, values_done = sem("st_ready"), sem("exp_done"), sem("values_done")
        ot_ready, gathered, o_free = sem("ot_ready"), sem("gathered"), sem("o_free")
        v_in_place = sem("v_in_place")
        first_part = sem("first_part")
        ao_ready, aot_ready = sem("ao_ready"), sem("aot_ready")
        pts_ready, lines_ready = sem("pts_ready"), sem("lines_ready")
        sq_ready, norm_in, norm_out, rnorm_ready = sem("sq_ready"), sem("norm_in"), sem("norm_out"), sem("rnorm_ready")
        lt_ready, jm_ready, phi_ready, phi_used = sem("lt_ready"), sem("jm_ready"), sem("phi_ready"), sem("phi_used")
        near2_ready = sem("near2_ready")
        half_written = sem("half_written")
        sig_in, sig_out = sem("sig_in"), sem("sig_out")
        x_final, out_stored = sem("x_final"), sem("out_stored")

        x_tok = d["L0_attn_x"].rearrange("b (i p) c -> p (b i) c", p=P)
        out_tok = out.rearrange("b (i p) c -> p (b i) c", p=P)

        LOADS = [
            (const[:, :], d["consts"][:, 0:nconst]),
            (mask_in[:, :], d["mask_consts"]),
            (valid[:, :], d["valid"]),
            (f0_gate, d["L0_ffn_Wg"]),
            (f1_gate, d["L1_ffn_gate_w"]),
            (coef_w, d["L1_ffn_coef_w"]),
            (b2_0[0:EXPERTS, :], d["L0_ffn_b2"]),
            (vec_rows[0:32, :], d["L0_ffn_b1"].rearrange("e (c p) -> (e c) p", p=P)),
            (vec_rows[32:64, :], d["L1_ffn_b1"].rearrange("e (c p) -> (e c) p", p=P)),
            (vec_rows[64:68, :], d["L1_ffn_rb1"].rearrange("(c p) -> c p", p=P)),
            (vec_rows[68:71, :], d["L0_attn_qkv_b"].rearrange("(c p) -> c p", p=P)),
            (vec_rows[71:74, :], d["L1_ffn_bqkv"].rearrange("(c p) -> c p", p=P)),
            (vec_rows[74:75, :], d["L1_ffn_ln1_g"].unsqueeze(0)),
            (vec_rows[75:76, :], d["L1_ffn_ln1_b"].unsqueeze(0)),
            (vec_rows[76:77, :], d["L1_ffn_ln2_g"].unsqueeze(0)),
            (vec_rows[77:78, :], d["L1_ffn_ln2_b"].unsqueeze(0)),
            (vec_rows[78:79, :], d["L1_attn_q_b"].unsqueeze(0)),
            (vec_rows[79:80, :], d["L1_attn_k_b"].unsqueeze(0)),
            (b2_1[0:EXPERTS, :], d["L1_ffn_b2"]),
            (b2_1[EXPERTS:EXPERTS + 1, :], d["L1_ffn_rb2"].unsqueeze(0)),
            (R("a0_vb"), d["L0_attn_qkv_b"].unsqueeze(0)[:, 2 * DIM:3 * DIM]),
            (R("f1_vb"), d["L1_ffn_bqkv"].unsqueeze(0)[:, 2 * DIM:3 * DIM]),
            (R("a1_vb"), d["L1_attn_v_b"].unsqueeze(0)),
            (R("a0_ob"), d["L0_attn_out_b"].unsqueeze(0)),
            (R("f1_ob"), d["L1_ffn_bo"].unsqueeze(0)),
            (R("a1_ob"), d["L1_attn_o_b"].unsqueeze(0)),
            (R("memv_b"), d["L0_attn_memv_b"].unsqueeze(0)),
            (R("memg_b"), d["L0_attn_memg_b"].unsqueeze(0)),
            (R("mem_scale"), d["L0_attn_mem_scale"].unsqueeze(0)),
            (R("coef_b"), d["L1_ffn_coef_b"].unsqueeze(0)),
            (a0_qkv[:, :], d["L0_attn_qkv_w"]),
            (a0_out[:, :], d["L0_attn_out_w"]),
            (lines_w[:, 0, :], d["L0_attn_w2w"]),
            (lines_w[:, 1, :], d["L0_attn_r1w"]),
            (lines_w[:, 2, :], d["L0_attn_r2w"]),
            (lines_w[:, 3, :], d["L0_attn_w1w"]),
            (memv_w, d["L0_attn_memv_w"]),
            (memg_w, d["L0_attn_memg_w"]),
            (f1_qkv[:, :], d["L1_ffn_Wqkv"]),
            (f1_out[:, :], d["L1_ffn_Wo"]),
            (a1_raw[:, 0, :], d["L1_attn_q_w"]),
            (a1_raw[:, 1, :], d["L1_attn_k_w"]),
            (a1_raw[:, 2, :], d["L1_attn_v_w"]),
            (a1_raw[:, 3, :], d["L1_attn_o_w"]),
        ]
        FIRST = 7

        PLAN = [("moe", 0), ("attn", CAUSAL), ("moe", 0), ("l1", FULL), ("attn", WINDOW), ("l1", FULL)][:LAYERS]
        ATTN_OF = {
            "causal": dict(w=a0_qkv[:, :], wo=a0_out[:, :], qb=VEC["a0_b"], kb=VEC["a0_b"] + 1, vb="a0_vb", ob="a0_ob"),
            "full": dict(w=f1_qkv[:, :], wo=f1_out[:, :], qb=VEC["f1_b"], kb=VEC["f1_b"] + 1, vb="f1_vb", ob="f1_ob"),
            "window": dict(w=a1_w[:, 0:3, :].rearrange("p a b -> p (a b)"), wo=a1_w[:, 3, :], qb=VEC["a1_qb"],
                           kb=VEC["a1_kb"], vb="a1_vb", ob="a1_ob"),
        }

        def tile_cols(t, shift=0):
            at = WIN + t % TB * P + shift
            return XT[:, t // TB, at:at + P]

        def run_jobs(engine, mode, run):
            run(-1, 1, mode.schedule(False, True), None)
            run(0, 0, mode.schedule(True, True, False), None)
            with engine.Fori(0, JOBS // 2 - 1) as i:
                run(2 * i + 1, 1, mode.schedule(True, True), i)
                run(2 * i + 2, 0, mode.schedule(True, True), i)
            run(JOBS - 1, 1, mode.schedule(True, False), None)
            run(JOBS, 0, mode.schedule(False, False), None)

        def heads_of(t):
            return AO[:, t % TB, t // TB * HEADS:(t // TB + 1) * HEADS, :]

        def block_cols(k):
            at = WIN + k % 2 * BLK
            return XT[:, k // 2, at:at + BLK]

        PROJECTIONS = [(which, 2 * b + half) for b in range(BATCH) for which in range(2) for half in range(2)]
        projection_items = []

        def parts_of(which, blk):
            off = (WIN if which else 0) + blk % 2 * BLK
            return [p[:, blk // 2, off:off + BLK] for p in (Kp if which else Qp)]

        MEM_V0 = 1 + 7 + 2 * NBLK + 1

        def far_items(t):
            return 2 * sum(1 for u in range(t + 1) if u % TB)

        def line_part(engine, link, dst, i1, i2, c, written, prods):
            a, b = PAIRS[c]
            if written and c in (1, 4):
                a, b = b, a
            link(engine.tensor_tensor(prods[0], pts[:, :, i1, :, a], pts[:, :, i2, :, b], ALU.mult))
            link(engine.tensor_tensor(prods[1], pts[:, :, i1, :, b], pts[:, :, i2, :, a], ALU.mult))
            at = LINE - 1 - c if written else c
            link(engine.tensor_tensor(dst[:, :, :, at], prods[0], prods[1], ALU.subtract))

        def scale_lines(engine, dst, which, half):
            ts = slice(half * TB, (half + 1) * TB)
            lines = dst[:, ts, :, :].rearrange("p t h c -> p (t h) c")
            return engine.tensor_tensor(lines, lines, rnorm[which][:, ts, :].rearrange("p t h -> p (t h)").unsqueeze(2)
                                        .broadcast_to([P, TB * HEADS, LINE]), ALU.mult)

        block = ctx.enter_context(nc.Block())

        @block.sync
        def _(sp):
            n = Count()
            sp.dma_start(X[:, :, :], x_tok).then_inc(x_loaded, 16)
            sp.wait_ge(set_up, 1)
            for dst, src in LOADS[:FIRST]:
                sp.dma_start(dst, src).then_inc(first_loaded, 16)
            for dst, src in LOADS[FIRST:]:
                sp.dma_start(dst, src).then_inc(loaded, 16)

            def load_expert(w1, w2, k):
                sp.dma_start(W1[k][:, :], w1).then_inc(w_in[k], 16)
                sp.dma_start(W2[k][:, :, :], w2).then_inc(w_in[k], 16)

            def experts(layer):
                w1, w2 = d[f"L{layer}_ffn_W1"], d[f"L{layer}_ffn_W2"]

                def load(e, k):
                    load_expert(w1[bass.ds(e, 1)].rearrange("e c f -> (e c) f"),
                                w2[bass.ds(e, 1)].rearrange("e (c p) o -> (e p) c o", p=P), k)

                if n.u:
                    sp.wait_ge(y_done, n.u + 2)
                load(0, 0)
                load(1, 1)
                with sp.Fori(1, EXPERTS // 2) as i:
                    for k in range(2):
                        sp.wait_ge(y_done, n.u + 2 + NBLK * (2 * i + (k - 1)))
                        load(2 * i + k, k)
                n.u += NBLK * EXPERTS
                if layer:
                    sp.wait_ge(y_done, n.u + 2 - NBLK)
                    load_expert(d["L1_ffn_rW1"], d["L1_ffn_rW2"].rearrange("(c p) o -> p c o", p=P), 0)
                    n.u += NBLK

            def fix_rows():
                sp.wait_ge(set_up, 3)
                n3 = HEADS * PARTS
                for b in range(BATCH):
                    sp.dma_start(q_dram[b, :, MAXROW:MAXROW + PARTS, :], KS[0][1][0:n3, 0:SEQ]).then_inc(fixed_rows, 16)
                    sp.dma_start(k_dram[b, :, MAXROW:MAXROW + PARTS, :], KS[0][0][0:n3, :]).then_inc(fixed_rows, 16)
                sp.wait_ge(fixed_rows, 64)
                sp.wait_ge(set_up, 4)

            def stacks(mode):
                S = mode.S
                if not n.parts:
                    fix_rows()

                def load(j, k, hh):
                    for dst, src in ((QS, q_heads), (KS, k_heads)):
                        sp.dma_start(dst[k][hh][0:LOAD_ROWS, :],
                                     src[bass.ds(2 * j + hh, 1)].rearrange("a r t -> (a r) t"))\
                          .then_inc(stack_in[k][hh], 16)

                for b in range(BATCH):
                    for parts, part_of, dst in ((Qp, Q_PART, q_dram), (Kp, K_PART, k_dram)):
                        n.parts += 1
                        sp.wait_ge(parts_ready, n.parts)
                        for grp in range(6):
                            rows = HEAD_ROWS[grp]
                            sp.dma_start(dst[b, :, rows.start:rows.stop, :], parts[part_of[grp]][:, b, :])\
                              .then_inc(stack_stored, 16)
                    n.stored += 16 * 12
                    sp.wait_ge(stack_stored, n.stored)
                    if b == 0:
                        for j in range(2):
                            for hh in range(2):
                                load(j, j, hh)
                with sp.Fori(0, JOBS // 2 - 1) as i:
                    for k in range(2):
                        for hh in range(2):
                            sp.wait_ge(st_ready, n.g + S * (2 * i + k) + mode.R * (hh + 1))
                            load(2 * i + (k + 2), k, hh)
                n.g += S * JOBS
                n.s_in += 16 * JOBS
                for k in range(2):
                    for hh in range(2):
                        sp.wait_ge(stack_in[k][hh], n.s_in)

            for kind, arg in PLAN:
                if kind == "moe":
                    experts(0)
                elif kind == "attn":
                    stacks(arg)
                else:
                    stacks(arg)
                    experts(1)
            sp.wait_ge(x_final, 1)
            sp.dma_start(out_tok, X[:, :, :]).then_inc(out_stored, 16)
            sp.wait_ge(out_stored, 16)

        @block.gpsimd
        def _(pool):
            n = Count()

            def link(ins):
                n.step += 1
                ins.then_inc(pool_step, 1)
                pool.wait_ge(pool_step, n.step)

            for t in (b2_0, b2_1, vec_rows):
                ins = pool.memset(t[:, :], 0.0)
                if t is not vec_rows:
                    link(ins)
            ins.then_inc(set_up, 1)
            pool.memset(gate_w[:, 2 * EXPERTS + 2:EXPERTS + WARM], 0.0)
            pool.memset(XT[:, :, 0:WIN], 0.0)
            link(pool.memset(XT[:, :, WIN + SEQ:PADDED], 0.0))
            pool.memset(memval[:, :, :], 0.0).then_inc(set_up, 1)
            for k in range(PARTS):
                pool.memset(Kp[k][:, :, 0:WIN], 0.0)
                ins = pool.memset(Kp[k][:, :, WIN + SEQ:PADDED], 0.0)
            link(ins)
            for k in range(2):
                link(pool.memset(VJ[k][:, :, :, :], 0.0))
                link(pool.memset(VJ[k][:, :, :, DH:DH + 1].rearrange("p h t d -> p (h t d)"), 1.0))
            link(pool.memset(zeros[:, :], 0.0))
            for k in range(2):
                for hh in range(2):
                    pool.memset(QS[k][hh][:, :], 0.0)
                    ins = pool.memset(KS[k][hh][:, :], 1.0 if k == 0 and hh == 0 else 0.0)
            link(ins)
            pool.sem_inc(set_up, 1)
            pool.wait_ge(fixed_rows, 64)
            link(pool.memset(KS[0][0][:, :], 0.0))
            pool.sem_inc(set_up, 1)

            def memory():
                pool.wait_ge(pts_ready, NT // 2)
                for c in range(LINE // 2, LINE):
                    line_part(pool, link, Lw, 3, 0, c, True, [p[:, :, :] for p in prod])
                pool.wait_ge(half_written, 1)
                pool.tensor_tensor(sq[:, :, :, :], Lw[:, :, :, :], Lw[:, :, :, :], ALU.mult).then_inc(sq_ready, 1)
                pool.wait_ge(rnorm_ready, 1)
                for half in range(2):
                    ins = scale_lines(pool, Lw, 0, half)
                ins.then_inc(lines_ready, 1)
                pool.wait_ge(lines_ready, 2)
                used = 0
                for t in range(NT):
                    k = t % 2
                    if t % TB:
                        if used >= 2:
                            pool.wait_ge(phi_used, used - 1)
                        for src, dst, tt in ((Lr, phiR[used % 2], t), (Lw, phiJ[used % 2], t - 1)):
                            line = src[:, tt, :, :]
                            for half in range(2):
                                hs = slice(half * HEADS // 2, (half + 1) * HEADS // 2)
                                ins = pool.tensor_tensor(
                                    dst[:, hs, :].rearrange("p h (a b) -> p h a b", a=LINE),
                                    line[:, hs, :].unsqueeze(3).broadcast_to([P, HEADS // 2, LINE, LINE]),
                                    line[:, hs, :].unsqueeze(2).broadcast_to([P, HEADS // 2, LINE, LINE]), ALU.mult)
                        ins.then_inc(phi_ready, 1)
                        used += 1
                        pool.wait_ge(phi_ready, used)
                    pool.wait_ge(lt_ready, t + 1)
                    if t >= 2:
                        pool.wait_ge(v_ready, MEM_V0 + (t - 2) * 4 + far_items(t - 2) + 4)
                    nl = HEADS * LINE
                    pool.tensor_tensor(JM[k][:, :, :], LT[k][:, 1, :].unsqueeze(1).broadcast_to([nl, HEADS, P]),
                                       C("same_head")[0:nl, :].unsqueeze(2).broadcast_to([nl, HEADS, P]), ALU.mult)\
                        .then_inc(jm_ready, 1)
                    pool.wait_ge(jm_ready, t + 1)

            for kind, arg in PLAN:
                if kind == "attn" and arg is CAUSAL:
                    memory()

        @block.tensor
        def _(pe):
            n = Count()

            def v_bank():
                k = n.v
                n.v += 1
                pe.wait_ge(v_free, k + 1)
                return pA[:, k % 2 * BLK:(k % 2 + 1) * BLK]

            def s_bank():
                k = n.s
                n.s += 1
                pe.wait_ge(s_free, k + 1)
                return pO[k % 2][:, :]

            def turn4(src, ready=None):
                bank = s_bank()
                for q, a in enumerate(src):
                    ins = pe.transpose(bank[:, q * P:(q + 1) * P], a, ident)
                ins.then_inc(s_ready, 1)

            def norm_turn():
                for q in range(4):
                    pe.wait_ge(xn_ready, n.xn + q + 1)
                    turn4([XN[:, 4 * q + r, :] for r in range(4)])
                n.xn += 4
                n.xt += 4

            def wait_xt():
                pe.wait_ge(xt_ready, n.xt)

            def gate(layer):
                wait_xt()
                bank = v_bank()
                step, at = (LOGITS1, EXPERTS) if layer else (EXPERTS, 0)
                for t in range(NT):
                    ins = pe.matmul(bank[:, t * step:t * step + WARM], tile_cols(t), gate_w[:, at:at + WARM], start=True, stop=True)
                ins.then_inc(v_ready, 1)
                if not layer:
                    pe.wait_ge(picks_ready, n.picks + 1)
                    n.picks += 1
                    for which, pick in enumerate((pick1b, pick2b)):
                        bank = v_bank()
                        ins = pe.matmul(bank[:, 0:NT * EXPERTS], M("before"), pick[:, :, :].rearrange("p t e -> p (t e)"),
                                        start=True, stop=False, skip_group_check=True)
                        for t in range(NT - 1):
                            k = NT - 1 - t
                            ins = pe.matmul(bank[:, (t + 1) * EXPERTS:NT * EXPERTS].rearrange("p (t e) -> p t e", t=k),
                                            M("ones"), pick[:, t, :].unsqueeze(1).broadcast_to([P, k, EXPERTS]),
                                            start=False, stop=(which == 0 and t == NT - 2), skip_group_check=True)
                        if which:
                            for t in range(NT):
                                ins = pe.matmul(bank[:, 0:NT * EXPERTS].rearrange("p (t e) -> p t e", t=NT), M("ones"),
                                                pick1b[:, t, :].unsqueeze(1).broadcast_to([P, NT, EXPERTS]),
                                                start=False, stop=(t == NT - 1), skip_group_check=True)
                        ins.then_inc(v_ready, 1)
                ne = EXPERTS + (1 if layer else 0)
                pe.wait_ge(coef_ready, n.coef + 1)
                n.coef += 1
                for q in range(4):
                    bank = s_bank()
                    for r in range(4):
                        ins = pe.matmul(bank[0:ne, r * P:(r + 1) * P], coef[:, 0:ne, 4 * q + r], ident, start=True, stop=True)
                    ins.then_inc(s_ready, 1)
                b2 = b2_1 if layer else b2_0
                for q in range(4):
                    n.coefT += 1
                    pe.wait_ge(coefT_ready, n.coefT)
                    bank = v_bank()
                    for r in range(4):
                        t = 4 * q + r
                        ins = pe.matmul(bank[:, r * P:(r + 1) * P], memval_rows[:, t * P:(t + 1) * P], b2[:, :],
                                        start=True, stop=True)
                    ins.then_inc(v_ready, 1)

            def up(k, u, blk):
                for c in range(FC):
                    pe.wait_ge(gelu_done, FC * u + (c + 1))
                    for m, (w, x) in enumerate(((0, 0), (0, 1), (1, 0))):
                        ins = pe.matmul(pS[c // 2][:, c % 2 * BLK:(c % 2 + 1) * BLK], W1S[k][w][:, c * P:(c + 1) * P],
                                        XS[x][:, blk, :], start=(m == 0), stop=(m == 2))
                    ins.then_inc(h_ready, 1)

            def down(k, u, blk):
                pe.wait_ge(gelu_done, FC * u + 2 * FC)
                pe.wait_ge(y_free, u + 1)
                y = pO[blk % 2]
                for r in range(4):
                    for c in range(FC):
                        ins = pe.matmul(y[:, r * P:(r + 1) * P], hidden[blk % 2][:, c, r * P:(r + 1) * P], W2[k][:, c, :],
                                        start=(c == 0), stop=(c == FC - 1))
                ins.then_inc(y_done, 1)

            def expert_units(uses, u0):
                units = [(k, b) for k in range(len(uses)) for b in range(NBLK)]
                for m, (k, b) in enumerate(units):
                    if b == 0:
                        pe.wait_ge(w_in[k], 32 * uses[k] + 32)
                        pe.wait_ge(w1_split[k], uses[k] + 1)
                    up(k, u0 + m, b)
                    if m:
                        down(units[m - 1][0], u0 + (m - 1), units[m - 1][1])
                down(units[-1][0], u0 + (len(units) - 1), units[-1][1])

            def experts(layer):
                pe.wait_ge(s_free, n.s + 2)
                n.xs += NBLK
                pe.wait_ge(x_split, n.xs)
                with pe.Fori(0, EXPERTS // 2) as i:
                    expert_units([n.w0 + i, n.w1 + i], n.u + 2 * NBLK * i)
                n.u += NBLK * EXPERTS
                n.w0 += EXPERTS // 2
                n.w1 += EXPERTS // 2
                if layer:
                    expert_units([n.w0], n.u)
                    n.u += NBLK
                    n.w0 += 1
                pe.wait_ge(y_free, n.u + 2)

            def project(mode):
                a = ATTN_OF[mode.kind]
                w = a["w"]
                wait_xt()
                projection_items.append(n.v)
                for which, blk in PROJECTIONS:
                    bank = v_bank()
                    pe.matmul(bank, w[:, which * DIM:(which + 1) * DIM], block_cols(blk), start=True, stop=True)\
                      .then_inc(v_ready, 1)
                if mode.kind == "causal":
                    memory_lines()
                wv = w[:, 2 * DIM:3 * DIM]
                if mode.kind == "window":
                    for q in range(2 * NT // 4):
                        bank = s_bank()
                        for m in range(4):
                            u = 4 * q + m
                            b, at = u // (2 * TB), u % (2 * TB) * WQ
                            o = bank[:, m * P:(m + 1) * P]
                            pe.matmul(o, XT[:, b, at:at + P], wv, start=True, stop=False)
                            ins = pe.matmul(o, valid[0:1, at:at + P], R(a["vb"]), start=False, stop=True)
                        ins.then_inc(s_ready, 1)
                        n.vp += 1
                else:
                    for q in range(4):
                        bank = s_bank()
                        for r in range(4):
                            o = bank[:, r * P:(r + 1) * P]
                            pe.matmul(o, tile_cols(4 * q + r), wv, start=True, stop=False)
                            ins = pe.matmul(o, valid[0:1, WIN:WIN + P], R(a["vb"]), start=False, stop=True)
                        ins.then_inc(s_ready, 1)
                        n.vp += 1

            def max_part(mode, k, a):
                hh, u = divmod(a, mode.U)
                t, at, w = mode.units[u]
                Q, K = QS[k][hh], KS[k][hh]
                o = pA[:, u % 2 * BLK:(u % 2 + 1) * BLK]
                if mode.kind == "window":
                    for m in range(2):
                        pe.matmul(o[:, m * SPAN:(m + 1) * SPAN], Q[:, (t + m) * P:(t + m + 1) * P],
                                  K[:, (t + m) * P:(t + m) * P + SPAN], start=(m == 0), stop=False, skip_group_check=True)
                    return pe.matmul(o[:, 0:2 * SPAN].rearrange("p (m s) -> p m s", m=2), identb,
                                     M("window_keys").unsqueeze(1).broadcast_to([P, 2, SPAN]),
                                     start=False, stop=True, skip_group_check=True)
                last = mode.kind == "causal" and at + w == (t + 1) * P
                ins = pe.matmul(o[:, 0:w], Q[:, t * P:(t + 1) * P], K[:, WIN + at:WIN + at + w],
                                start=True, stop=not last, skip_group_check=True)
                if last:
                    ins = pe.matmul(o[:, w - P:w], identb, M("later_key"), start=False, stop=True, skip_group_check=True)
                return ins

            def score_part(mode, k, s):
                hh, r = divmod(s, mode.R)
                Q, K = QS[k][hh], KS[k][hh]
                o = pS[s % 2]
                if mode.kind == "window":
                    per_bank = BLK // WQ
                    for u in range(2 * TB):
                        pe.matmul(o[:, u * WQ:(u + 1) * WQ], K[:, u * WQ:u * WQ + P], Q[:, u * WQ:(u + 1) * WQ],
                                  start=(u % per_bank == 0), stop=False, skip_group_check=True)
                    for bank in range(2):
                        ins = pe.matmul(o[:, bank * BLK:(bank + 1) * BLK].rearrange("p (u t) -> p u t", u=per_bank), identb,
                                        M("window_queries").unsqueeze(1).broadcast_to([P, per_bank, WQ]),
                                        start=False, stop=True, skip_group_check=True)
                    return ins
                causal = mode.kind == "causal"
                for kt, col in mode.steps[r]:
                    at, query = col, kt * P if causal else 0
                    while query < SEQ:
                        w = min(BLK - at % BLK, SEQ - query)
                        ins = pe.matmul(o[:, at:at + w], K[:, WIN + kt * P:WIN + (kt + 1) * P], Q[:, query:query + w],
                                        start=(at % BLK == 0), stop=not causal, skip_group_check=True)
                        at, query = at + w, query + w
                if causal:
                    for kt, col in mode.steps[r]:
                        ins = pe.matmul(o[:, col:col + P], identb, M("later_query"), start=False, stop=True,
                                        skip_group_check=True)
                return ins

            def value_part(mode, k, p):
                hh, m = divmod(p, mode.V)
                g, halves = mode.products[m]
                v, out = VJ[k], pO[hh]
                if mode.kind == "window":
                    e = PT[mode.buffer(k, hh)]
                    for b in range(TB // 2):
                        for c in range(2):
                            for h in range(2):
                                u, at = 2 * (2 * b + h) + c, QUAD * (2 * c + h)
                                ins = pe.matmul(out[at:at + QUAD, b * WQ:(b + 1) * WQ], v[:, hh, u, :],
                                                e[:, u * WQ:(u + 1) * WQ], start=(b == 0), stop=(b == TB // 2 - 1),
                                                skip_group_check=True)
                    return ins
                causal = mode.kind == "causal"
                products = {}
                for r in mode.groups[g]:
                    e = PT[mode.buffer(k, mode.R * hh + r)].rearrange("p (q t) -> p q t", t=P)
                    for kt, col in mode.steps[r]:
                        q0 = kt if causal else 0
                        for h in range(2):
                            quad = 2 * (kt % 2) + h
                            mine = [q for q in range(q0, TB) if q % 2 == h and q // (TB // 2) in halves]
                            if not mine:
                                continue
                            start = kt < 2 and 0 in halves
                            if mine[0] > 1:
                                if start:
                                    e0 = PT[mode.buffer(k, mode.R * hh)]
                                    products.setdefault(quad, []).append((zeros[:, :], e0[:, 0:P], 0, P, True))
                                start = False
                            at = col // P + mine[0] - q0
                            products.setdefault(quad, []).append(
                                (v[:, hh, kt, :], e[:, at:at + 2 * len(mine) - 1:2, :], mine[0] // 2 * P, len(mine) * P, start))
                for m in range(max(len(a) for a in products.values())):
                    for quad, a in sorted(products.items()):
                        if m < len(a):
                            w, e, at, width, start = a[m]
                            o = out[QUAD * quad:QUAD * (quad + 1), at:at + width]
                            if len(e.shape) == 3:
                                o = o.rearrange("p (q t) -> p q t", t=P)
                            ins = pe.matmul(o, w, e, start=start, stop=(p % mode.V == mode.V - 1), skip_group_check=True)
                return ins

            def gather_part(mode, s):
                for b in range(TB // 2):
                    cols = slice(b * GATHER, (b + 1) * GATHER)
                    if mode.kind == "window":
                        for c in range(2):
                            ins = pe.matmul(pO[s][c * WQ:(c + 1) * WQ, cols], OT[s][:, b * WQ:(b + 1) * WQ],
                                            C("gather_window")[:, c * GATHER:(c + 1) * GATHER], start=True, stop=True)
                    else:
                        ins = pe.matmul(pO[s][:, cols], OT[s][:, b * P:(b + 1) * P], C("gather"), start=True, stop=True)
                return ins

            def run(mode, j, k, events):
                S, U, per_head = mode.S, mode.U, mode.V
                ja, ka = j + 1, 1 - k
                units, rows_left = 0, None
                for what, s, prev in events:
                    jj, kk = (j - 1, 1 - k) if prev else (j, k)
                    if what == "scores":
                        if s % mode.R == 0:
                            pe.wait_ge(rows_ready, n.rows + 2 * j + (s // mode.R + 1))
                        pe.wait_ge(exp_done, n.g + S * j + (s + 1))
                        score_part(mode, k, s).then_inc(st_ready, 1)
                    elif what == "values":
                        hh, m = divmod(s, per_head)
                        g = mode.products[m][0]
                        pe.wait_ge(exp_done, n.g + S * jj + (mode.R * hh + mode.groups[g][-1] + 3))
                        if s == 0:
                            pe.wait_ge(vj_ready, n.jobs + jj + 1)
                        if m == 0:
                            pe.wait_ge(o_free, n.o + 2 * jj + (hh + 1))
                        value_part(mode, kk, s).then_inc(values_done, 1)
                    elif what == "gather":
                        pe.wait_ge(ot_ready, n.o + 2 * jj + (s + 1))
                        gather_part(mode, s).then_inc(gathered, 1)
                    elif what == "max":
                        if s % U == 0:
                            hh = s // U
                            pe.wait_ge(stack_in[ka][hh], n.jobs * 16 + (ja + (2 - ka)) * 16)
                        if rows_left is not None:
                            pe.wait_ge(rows_ready, rows_left)
                            rows_left = None
                        pe.wait_ge(a_free, n.a + 2 * U * ja + (s + 1))
                        max_part(mode, ka, s).then_inc(a_ready, 1)
                        units += 1
                    elif what == "rows":
                        jr = j if prev else ja
                        pe.wait_ge(negparts_ready, n.rows + 2 * jr + (s + 1))
                        pe.wait_ge(a_free, n.a + 2 * U * ja + (units + 2))
                        for t in range(TB):
                            ins = pe.matmul(pA[MAXROW:MAXROW + PARTS, t * P:(t + 1) * P], negparts[:, s, t, :], identb,
                                            start=True, stop=True)
                        ins.then_inc(rows_out, 1)
                        rows_left = n.rows + 2 * jr + (s + 1)

            def attention(mode):
                pe.wait_ge(v_free, n.v + 2)
                pe.wait_ge(s_free, n.s + 2)
                pe.wait_ge(v_in_place, n.vp)
                run_jobs(pe, mode, lambda j, k, events, i: run(mode, j, k, events))
                n.a += 2 * mode.U * JOBS
                n.g += mode.S * JOBS
                n.o += 2 * JOBS
                n.rows += 2 * JOBS
                n.jobs += JOBS
                pe.wait_ge(o_free, n.o + 2)

            def out_proj(mode):
                a = ATTN_OF[mode.kind]
                if mode.kind == "causal":
                    pe.wait_ge(ao_ready, 1)
                for q in range(4):
                    turn4([heads_of(4 * q + r).rearrange("p h d -> p (h d)") for r in range(4)])
                for q in range(4):
                    n.aot += 1
                    pe.wait_ge(aot_ready, n.aot)
                    bank = v_bank()
                    for r in range(4):
                        t = 4 * q + r
                        o = bank[:, r * P:(r + 1) * P]
                        pe.matmul(o, AOT[:, t * P:(t + 1) * P], a["wo"], start=True, stop=False)
                        ins = pe.matmul(o, valid[0:1, WIN:WIN + P], R(a["ob"]), start=False, stop=True)
                    ins.then_inc(v_ready, 1)

            def memory_lines():
                for q in range(NT // 2):
                    bank = s_bank()
                    for r in range(2):
                        t = 2 * q + r
                        pe.matmul(bank[:, r * 256 + P:(r + 1) * 256], tile_cols(t, -1),
                                  lines_w[:, 2:4, :].rearrange("p a b -> p (a b)"), start=True, stop=True)
                        ins = pe.matmul(bank[:, r * 256:r * 256 + 192], tile_cols(t),
                                        lines_w[:, 0:3, :].rearrange("p a b -> p (a b)"), start=True, stop=True)
                    ins.then_inc(s_ready, 1)

            def memory():
                for q in range(4):
                    bank = s_bank()
                    for r in range(4):
                        o = bank[:, r * P:(r + 1) * P]
                        pe.matmul(o, tile_cols(4 * q + r), memv_w, start=True, stop=False)
                        ins = pe.matmul(o, valid[0:1, WIN:WIN + P], R("memv_b"), start=False, stop=True)
                    ins.then_inc(s_ready, 1)
                bank = v_bank()
                for t in range(NT):
                    pe.matmul(bank[:, t * HEADS:t * HEADS + WARM], tile_cols(t), mem_w[:, 0:WARM], start=True, stop=False,
                              skip_group_check=True)
                    o = bank[:, t * HEADS:(t + 1) * HEADS]
                    ins = pe.matmul(o, valid[0:1, WIN:WIN + P], R("memg_b"), start=False, stop=True, skip_group_check=True)
                ins.then_inc(v_ready, 1)

            def memory_scores():
                pe.wait_ge(lines_ready, 2)
                assert n.v == MEM_V0, n.v
                nl = HEADS * LINE
                used = 0

                def turn(t):
                    bank = s_bank()
                    for m, src in enumerate((Lr, Lw)):
                        ins = pe.transpose(bank[0:nl, m * P:(m + 1) * P],
                                           src[:, t, :, :].rearrange("p h c -> p (h c)"), ident)
                    ins.then_inc(s_ready, 1)

                turn(0)
                for t in range(NT):
                    if t + 1 < NT:
                        turn(t + 1)
                    if t % TB:
                        pe.wait_ge(phi_ready, used + 1)
                        for half in range(2):
                            bank = v_bank()
                            hs = slice(half * HEADS // 2, (half + 1) * HEADS // 2)
                            pe.matmul(bank[:, 0:HEADS // 2 * PHI], C("decay_next"),
                                      phiJ[used % 2][:, hs, :].rearrange("p h c -> p (h c)"), start=True, stop=True)\
                              .then_inc(v_ready, 1)
                        used += 1
                    pe.wait_ge(jm_ready, t + 1)
                    for q in range(4):
                        bank = v_bank()
                        pe.matmul(bank, LT[t % 2][:, 0, :],
                                  JM[t % 2][:, 4 * q:4 * q + 4, :].rearrange("p h s -> p (h s)"), start=True, stop=True)\
                          .then_inc(v_ready, 1)

            def turn_weights():
                pe.wait_ge(loaded, 16 * len(LOADS[FIRST:]))
                bank = s_bank()
                pe.transpose(bank[:, 0:P], vec_rows[:, :], ident).then_inc(s_ready, 1)
                turn4([a1_raw[:, q, :] for q in range(4)])
                bank = v_bank()
                at = ROW["mem_scale"][0]
                pe.matmul(bank[:, 0:HEADS + 2], valid[0:1, WIN:WIN + P], row[0:1, at:at + HEADS + 2], start=True, stop=True)\
                  .then_inc(v_ready, 1)
                pe.wait_ge(vec_done, 2)

            pe.wait_ge(first_loaded, 16 * FIRST)
            pe.wait_ge(set_up, 2)
            pe.wait_ge(consts_done, 1)
            for kind, arg in PLAN:
                norm_turn()
                if kind == "moe":
                    gate(0)
                    if n.u == 0:
                        turn_weights()
                    experts(0)
                elif kind == "attn":
                    project(arg)
                    if arg is CAUSAL:
                        memory()
                        memory_scores()
                    attention(arg)
                    out_proj(arg)
                else:
                    project(arg)
                    attention(arg)
                    out_proj(arg)
                    norm_turn()
                    gate(1)
                    experts(1)

        @block.scalar
        def _(act):
            n = Count()
            act.sem_inc(s_free, 2)
            act.sem_inc(gelu_done, FC)
            act.sem_inc(exp_done, 2)

            def s_take():
                k = n.s
                n.s += 1
                act.wait_ge(s_ready, k + 1)
                return pO[k % 2][:, :]

            def norm_turn(gb=None):
                n.var += 1
                act.wait_ge(var_ready, n.var)
                act.activation(std[:, :], mv[:, :, 1], ACT.Sqrt).then_inc(std_ready, 1)
                for q in range(4):
                    bank = s_take()
                    b, at = q // 2, WIN + q % 2 * BLK
                    dst = XT[:, b, at:at + BLK]
                    if gb is None:
                        ins = act.activation(dst, bank[:, :], ACT.Copy)
                    else:
                        ins = act.activation(dst, bank[:, :], ACT.Identity, scale=vec[:, gb:gb + 1], bias=vec[:, gb + 1:gb + 2])
                    ins.then_inc(s_free, 1)
                    act.wait_ge(s_free, n.s + 2)
                    act.sem_inc(xt_ready, 1)

            def gate(layer):
                ne = EXPERTS + (1 if layer else 0)
                n.gate += 1
                act.wait_ge(gate_in, n.gate)
                act.activation(g[1][:, :, :], g[0][:, :, :], ACT.Exp).then_inc(gate_exp, 1)
                if layer:
                    n.gate += 1
                    act.wait_ge(gate_in, n.gate)
                    act.activation(coefe[:, :, :], coef2[:, :, :], ACT.Exp).then_inc(gate_exp, 1)
                for q in range(4):
                    bank = s_take()
                    act.activation(coefT[0:ne, q * BLK:(q + 1) * BLK], bank[0:ne, :], ACT.Copy).then_inc(s_free, 1)
                    act.wait_ge(s_free, n.s + 2)
                    act.sem_inc(coefT_ready, 1)

            def gelus(u, blk, k):
                act.wait_ge(y_done, u + 1)
                for c in range(FC):
                    act.wait_ge(h_ready, FC * u + (c + 1))
                    act.activation(hidden[blk % 2][:, c, :], pS[c // 2][:, c % 2 * BLK:(c % 2 + 1) * BLK], ACT.Gelu,
                                   bias=bias1[k][:, c:c + 1]).then_inc(gelu_done, 1)

            def experts(layer):
                act.preload_act_table(ACT.Gelu)
                with act.Fori(0, EXPERTS // 2) as i:
                    for k in range(2):
                        act.wait_ge(bias1_ready, n.bias1 + 2 * i + (k + 1))
                        for b in range(NBLK):
                            gelus(n.u + 2 * NBLK * i + (NBLK * k + b), b, k)
                n.u += NBLK * EXPERTS
                if layer:
                    act.wait_ge(bias1_ready, n.bias1 + EXPERTS + 1)
                    for b in range(NBLK):
                        gelus(n.u + b, b, 0)
                    n.u += NBLK
                n.bias1 += EXPERTS + 1

            def project(mode):
                if n.stored:
                    act.wait_ge(stack_stored, n.stored)
                n.stored += 16 * 24
                v0 = projection_items[n.projections]
                n.projections += 1
                a = ATTN_OF[mode.kind]
                for m, (which, blk) in enumerate(PROJECTIONS):
                    bias = a["kb"] if which else a["qb"]
                    act.wait_ge(v_ready, v0 + m + 1)
                    act.activation(parts_of(which, blk)[0], pA[:, (v0 + m) % 2 * BLK:((v0 + m) % 2 + 1) * BLK], ACT.Identity,
                                   bias=vec[:, bias:bias + 1]).then_inc(first_part, 1)
                if mode.kind == "causal":
                    memory_lines()
                if mode.kind == "window":
                    for q in range(2 * NT // 4):
                        bank = s_take()
                        b, u = 4 * q // (2 * TB), 4 * q % (2 * TB)
                        dst = VW[:, b * HEADS:(b + 1) * HEADS, u:u + 4, :].rearrange("p h u d -> p u h d")
                        act.activation(dst, bank[:, :].rearrange("p (u h d) -> p u h d", u=4, h=HEADS), ACT.Copy)\
                           .then_inc(s_free, 1)
                        act.wait_ge(s_free, n.s + 2)
                        act.sem_inc(v_in_place, 1)
                else:
                    for q in range(4):
                        bank = s_take()
                        b, t = 4 * q // TB, 4 * q % TB
                        dst = V[:, b * HEADS:(b + 1) * HEADS, t:t + 4, 0:DH].rearrange("p h t d -> p t h d")
                        act.activation(dst, bank[:, :].rearrange("p (t h d) -> p t h d", t=4, h=HEADS), ACT.Copy)\
                           .then_inc(s_free, 1)
                        act.wait_ge(s_free, n.s + 2)
                        act.sem_inc(v_in_place, 1)

            def run(mode, j, k, events):
                S, products = mode.S, 2 * mode.V
                for what, s, prev in events:
                    jj = j - 1 if prev else j
                    if what == "scores":
                        act.wait_ge(st_ready, n.g + S * j + (s + 1))
                        back = -(-max(4 - s, 0) // S)
                        hh, r = divmod(s - 4 + back * S, mode.R)
                        done = sum(r >= mode.groups[g][0] for g, _ in mode.products)
                        if not (isinstance(j, int) and j < back):
                            act.wait_ge(values_done, n.p + products * (j - back) + (mode.V * hh + done))
                        w = mode.width(s % mode.R)
                        act.activation(PT[mode.buffer(k, s)][:, 0:w], pS[s % 2][:, 0:w], ACT.Exp, scale=SCALE)\
                           .then_inc(exp_done, 1)
                    elif what == "take":
                        act.wait_ge(values_done, n.p + products * jj + mode.V * (s + 1))
                        w = BLK // 2 if mode.kind == "window" else BLK
                        act.activation(OT[s][:, 0:w], pO[s][:, 0:w], ACT.Copy).then_inc(ot_ready, 1)
                    elif what == "rows":
                        jr = j if prev else j + 1
                        act.wait_ge(rows_out, n.rows + 2 * jr + (s + 1))
                        act.activation(QS[k if prev else 1 - k][s][MAXROW:MAXROW + PARTS, :],
                                       pA[MAXROW:MAXROW + PARTS, 0:SEQ], ACT.Copy).then_inc(rows_ready, 1)

            def attention(mode):
                act.wait_ge(stack_stored, n.stored)
                run_jobs(act, mode, lambda j, k, events, i: run(mode, j, k, events))
                n.g += mode.S * JOBS
                n.p += 2 * mode.V * JOBS
                n.rows += 2 * JOBS

            def out_proj(mode):
                for q in range(4):
                    bank = s_take()
                    act.activation(AOT[:, q * BLK:(q + 1) * BLK], bank[:, :], ACT.Copy).then_inc(s_free, 1)
                    act.wait_ge(s_free, n.s + 2)
                    act.sem_inc(aot_ready, 1)

            def memory_lines():
                for q in range(NT // 2):
                    bank = s_take()
                    act.activation(pts[:, 2 * q:2 * q + 2, :, :, :].rearrange("p t g h c -> p (t g h c)"), bank[:, :], ACT.Copy)\
                       .then_inc(s_free, 1)
                    act.wait_ge(s_free, n.s + 2)
                    act.sem_inc(pts_ready, 1)

            def memory():
                for q in range(4):
                    bank = s_take()
                    act.activation(memval[:, 4 * q:4 * q + 4, :].rearrange("p t c -> p (t c)"), bank[:, :], ACT.Copy)\
                       .then_inc(s_free, 1)
                act.wait_ge(sig_in, 1)
                act.activation(gates[:, :, :], gates[:, :, :], ACT.Sigmoid).then_inc(sig_out, 1)
                for which in range(2):
                    act.wait_ge(norm_in, which + 1)
                    act.activation(norm[:, :, :], norm[:, :, :], ACT.Sqrt).then_inc(norm_out, 1)

            def memory_scores():
                def take(t):
                    bank = s_take()
                    if t >= 2:
                        act.wait_ge(v_ready, MEM_V0 + (t - 2) * 4 + far_items(t - 2) + 4)
                        act.wait_ge(jm_ready, t - 1)
                    act.activation(LT[t % 2][:, :, :].rearrange("p a b -> p (a b)"), bank[0:HEADS * LINE, 0:2 * P], ACT.Copy)\
                       .then_inc(s_free, 1)
                    act.wait_ge(s_free, n.s + 2)
                    act.sem_inc(lt_ready, 1)

                take(0)
                m = 0
                for t in range(NT):
                    if t + 1 < NT:
                        take(t + 1)
                    for q in range(4):
                        act.wait_ge(v_free, MEM_V0 + 4 * t + far_items(t) + q + 3)
                        act.activation(near2[m % 2][:, :, :], near[m % 2][:, :, :], ACT.Square).then_inc(near2_ready, 1)
                        m += 1
                act.wait_ge(sig_in, 2)
                act.activation(score_in[:, :, :], score_in[:, :, :], ACT.Sigmoid).then_inc(sig_out, 1)

            def turn_weights():
                bank = s_take()
                act.activation(vec[:, :], bank[:, 0:P], ACT.Copy).then_inc(s_free, 1)
                bank = s_take()
                act.activation(a1_w[:, :, :].rearrange("p a b -> p (a b)"), bank[:, :], ACT.Copy).then_inc(s_free, 1)
                act.wait_ge(s_free, n.s + 2)
                act.sem_inc(vec_done, 2)

            for kind, arg in PLAN:
                if kind == "moe":
                    norm_turn()
                    gate(0)
                    if n.u == 0:
                        turn_weights()
                    experts(0)
                elif kind == "attn":
                    norm_turn()
                    project(arg)
                    if arg is CAUSAL:
                        memory()
                        memory_scores()
                    attention(arg)
                    out_proj(arg)
                else:
                    n.var += 1
                    act.wait_ge(var_ready, n.var)
                    act.activation(std[:, :], mv[:, :, 1], ACT.Sqrt).then_inc(std_ready, 1)
                    norm_turn(VEC["ln1_g"])
                    project(arg)
                    attention(arg)
                    out_proj(arg)
                    norm_turn(VEC["ln2_g"])
                    gate(1)
                    experts(1)

        @block.vector
        def _(dve):
            n = Count()

            def link(ins):
                n.step += 1
                ins.then_inc(dve_step, 1)
                dve.wait_ge(dve_step, n.step)

            def v_take():
                k = n.v
                n.v += 1
                dve.wait_ge(v_ready, k + 1)
                return pA[:, k % 2 * BLK:(k % 2 + 1) * BLK]

            def layer_norm(src, dst, signal=True):
                for t in range(NT):
                    ins = dve.bn_stats(stats[:, t, :], src[:, t, :])
                link(ins)
                for t in range(NT):
                    ins = dve.bn_aggr(mv[:, t, :], stats[:, t, :])
                link(ins)
                dve.tensor_scalar(mv[:, :, 1], mv[:, :, 1], EPS, None, ALU.add).then_inc(var_ready, 1)
                n.std += 1
                dve.wait_ge(std_ready, n.std)
                link(dve.reciprocal(rstd[:, :], std[:, :]))
                for t in range(NT):
                    ins = dve.tensor_scalar(dst[:, t, :], src[:, t, :], mv[:, t, 0:1], rstd[:, t:t + 1], ALU.subtract, ALU.mult)
                    if signal and t % 4 == 3:
                        ins.then_inc(xn_ready, 1)
                if not signal:
                    link(ins)

            def bc(ap, k):
                return ap.unsqueeze(2).broadcast_to([P, NT, k])

            def pick_largest(src, dst, m):
                link(dve.tensor_reduce(m, src, AX_X, ALU.max))
                link(dve.tensor_tensor(g[2][:, :, :], src, bc(m, EXPERTS), ALU.is_equal))
                link(dve.tensor_tensor(g[2][:, :, :], g[2][:, :, :], C("rank").unsqueeze(1).broadcast_to([P, NT, EXPERTS]),
                                       ALU.mult))
                link(dve.tensor_reduce(s1[:, 11, :], g[2][:, :, :], AX_X, ALU.max))
                link(dve.tensor_tensor(dst[:, :, :], g[2][:, :, :], bc(s1[:, 11, :], EXPERTS), ALU.is_equal))

            def gate(layer):
                bank = v_take()
                m1, m2, z, rz, e2, g2, den, rden2, w1, w2 = (s1[:, q, :] for q in range(10))
                step = LOGITS1 if layer else EXPERTS
                both = bank[:, 0:NT * step].rearrange("p (t e) -> p t e", t=NT)
                ins = dve.tensor_copy(logits[:, :, :], both[:, :, 0:EXPERTS])
                if layer:
                    ins = dve.tensor_tensor(coef2[:, :, :], both[:, :, EXPERTS:LOGITS1],
                                            coef_b.unsqueeze(1).broadcast_to([P, NT, 2]), ALU.add)
                ins.then_inc(v_free, 1)
                dve.wait_ge(v_free, n.v + 2)
                pick_largest(logits[:, :, :], pick1, m1)
                dve.tensor_tensor(g[0][:, :, :], logits[:, :, :], bc(m1, EXPERTS), ALU.subtract).then_inc(gate_in, 1)
                if layer:
                    link(dve.tensor_reduce(m2, coef2[:, :, :], AX_X, ALU.max))
                    dve.tensor_tensor(coef2[:, :, :], coef2[:, :, :], bc(m2, 2), ALU.subtract).then_inc(gate_in, 1)
                    n.gexp += 2
                    dve.wait_ge(gate_exp, n.gexp)
                    link(dve.tensor_reduce(z, g[1][:, :, :], AX_X, ALU.add))
                    link(dve.tensor_reduce(e2, coefe[:, :, :], AX_X, ALU.add))
                    link(dve.reciprocal(rz, z))
                    link(dve.reciprocal(g2, e2))
                    link(dve.tensor_scalar(g2, g2, 0.5, None, ALU.mult))
                    link(dve.tensor_tensor(w1, coefe[:, :, 0], g2, ALU.mult))
                    link(dve.tensor_tensor(w1, w1, rz, ALU.mult))
                    dve.tensor_tensor(coef[:, EXPERTS, :], coefe[:, :, 1], g2, ALU.mult)
                    dve.tensor_tensor(coef[:, 0:EXPERTS, :].rearrange("p e t -> p t e"), pick1[:, :, :], bc(w1, EXPERTS),
                                      ALU.mult).then_inc(coef_ready, 1)
                else:
                    link(dve.scalar_tensor_tensor(g[3][:, :, :], pick1[:, :, :], -3e38, logits[:, :, :], ALU.mult, ALU.add))
                    pick_largest(g[3][:, :, :], pick2, m2)
                    dve.tensor_copy(pick1b[:, :, :], pick1[:, :, :])
                    dve.tensor_copy(pick2b[:, :, :], pick2[:, :, :]).then_inc(picks_ready, 1)
                    n.gexp += 1
                    dve.wait_ge(gate_exp, n.gexp)
                    link(dve.tensor_reduce(z, g[1][:, :, :], AX_X, ALU.add))
                    link(dve.reciprocal(rz, z))
                    link(dve.tensor_tensor(g[2][:, :, :], pick2[:, :, :], g[1][:, :, :], ALU.mult))
                    link(dve.tensor_reduce(e2, g[2][:, :, :], AX_X, ALU.add))
                    link(dve.tensor_tensor(g2, e2, rz, ALU.mult))
                    link(dve.scalar_tensor_tensor(den, rz, 1e-9, g2, ALU.add, ALU.add))
                    link(dve.reciprocal(rden2, den))
                    link(dve.scalar_tensor_tensor(w1, rz, 0.5, rden2, ALU.mult, ALU.mult))
                    link(dve.scalar_tensor_tensor(w2, g2, 0.5, rden2, ALU.mult, ALU.mult))
                    for which, (pick, w) in enumerate(((pick1, w1), (pick2, w2))):
                        bank = v_take()
                        dve.scalar_tensor_tensor(g[2 + which][:, :, :].rearrange("p t e -> p (t e)"), bank[:, 0:NT * EXPERTS],
                                                 float(CAPACITY), pick[:, :, :].rearrange("p t e -> p (t e)"),
                                                 ALU.is_lt, ALU.mult).then_inc(v_free, 1)
                        dve.wait_ge(v_free, n.v + 2)
                        link(dve.tensor_tensor(g[2 + which][:, :, :], g[2 + which][:, :, :], bc(w, EXPERTS), ALU.mult))
                    dve.tensor_tensor(coef[:, 0:EXPERTS, :].rearrange("p e t -> p t e"), g[2][:, :, :], g[3][:, :, :],
                                      ALU.add).then_inc(coef_ready, 1)
                split_tokens()
                for q in range(4):
                    bank = v_take()
                    x4 = X[:, 4 * q:4 * q + 4, :].rearrange("p t c -> p (t c)")
                    dve.tensor_tensor(x4, bank, x4, ALU.add).then_inc(v_free, 1)
                dve.wait_ge(v_free, n.v + 2)

            def add_unit(u, blk, e):
                dve.wait_ge(y_done, u + 3)
                dve.wait_ge(y_free, u + 2)
                for r in range(4):
                    t = 4 * blk + r
                    ins = dve.scalar_tensor_tensor(X[:, t, :], pO[blk % 2][:, r * P:(r + 1) * P], coef[:, bass.ds(e, 1), t]
                                                   , X[:, t, :], ALU.mult, ALU.add)
                ins.then_inc(y_free, 1)

            def take_bias(k, at):
                dve.tensor_scalar(bias1[k][:, :], vec[:, bass.ds(at, FC)], 1.0, None, ALU.mult).then_inc(bias1_ready, 1)

            def split_tokens():
                n.xt += 4
                dve.wait_ge(xt_ready, n.xt)
                for b in range(NBLK):
                    link(dve.tensor_copy(XS[0][:, b, :], block_cols(b)))
                    dve.tensor_tensor(XS[1][:, b, :], block_cols(b), XS[0][:, b, :].bitcast(F32), ALU.subtract)\
                       .then_inc(x_split, 1)

            def split_w1(k, uses):
                dve.wait_ge(w_in[k], 32 * uses + 32)
                dve.tensor_copy(W1S[k][0][:, :], W1[k][:, :]).then_inc(w1_high[k], 1)
                dve.wait_ge(w1_high[k], uses + 1)
                dve.tensor_tensor(W1S[k][1][:, :], W1[k][:, :], W1S[k][0][:, :].bitcast(F32), ALU.subtract).then_inc(w1_split[k], 1)

            def experts(layer):
                base = VEC["f1_b1" if layer else "f0_b1"]

                def pair(i, more):
                    take_bias(1, base + 2 * FC * i + FC)
                    for m in range(2 * NBLK):
                        add_unit(n.u + 2 * NBLK * i + m, m % NBLK, 2 * i + m // NBLK)
                        if m == 0:
                            split_w1(1, n.w1 + i)
                        if m == NBLK - 1:
                            take_bias(0, base + 2 * FC * i + 2 * FC)
                        if m == NBLK and more:
                            split_w1(0, n.w0 + i + 1)

                take_bias(0, base)
                split_w1(0, n.w0)
                with dve.Fori(0, EXPERTS // 2 - 1) as i:
                    pair(i, True)
                pair(EXPERTS // 2 - 1, layer == 1)
                n.u += NBLK * EXPERTS
                n.w0 += EXPERTS // 2
                n.w1 += EXPERTS // 2
                if layer:
                    for m in range(NBLK):
                        add_unit(n.u + m, m, EXPERTS)
                    n.u += NBLK
                    n.w0 += 1
                dve.wait_ge(y_free, n.u + 2)

            def project(mode):
                n.stored += 16 * 24
                for m, (which, blk) in enumerate(PROJECTIONS):
                    bank = v_take()
                    cols = parts_of(which, blk)
                    a = ATTN_OF[mode.kind]
                    bias = a["kb"] if which else a["qb"]
                    n.first += 1
                    dve.wait_ge(first_part, n.first)
                    dve.scalar_tensor_tensor(rest[:, :], bank, vec[:, bias:bias + 1], cols[0], ALU.add, ALU.subtract)\
                       .then_inc(v_free, 1)
                    dve.wait_ge(v_free, n.v + 2)
                    link(dve.tensor_copy(cols[1], rest[:, :]))
                    link(dve.tensor_tensor(cols[2], rest[:, :], cols[1], ALU.subtract))
                    if m % 2:
                        dve.sem_inc(parts_ready, 1)

            def copy_v(mode, j, k):
                if mode.kind == "window":
                    ins = dve.tensor_scalar(VJ[k][:, :, :, 0:DH], VW[:, bass.ds(2 * j, 2), :, :], 1.0, None, ALU.mult)
                else:
                    ins = dve.tensor_scalar(VJ[k][:, :, 0:TB, 0:DH], V[:, bass.ds(2 * j, 2), :, :], 1.0, None, ALU.mult)
                ins.then_inc(vj_ready, 1)

            def run(mode, j, k, events, base):
                U = mode.U
                ja, ka = j + 1, 1 - k
                with_a = ("split", 0, False) in events
                c = 0
                for what, s, prev in events:
                    jj = j - 1 if prev else j
                    if what == "max":
                        dve.wait_ge(a_ready, n.a + 2 * U * ja + (s + 1))
                        hh, u = divmod(s, U)
                        t, at, w = mode.units[u]
                        bank = pA[:, u % 2 * BLK:(u % 2 + 1) * BLK]
                        if mode.kind == "window":
                            src = bank[:, 0:2 * SPAN].rearrange("p (m s) -> p m s", m=2)
                            dst = negmax2[:, hh, t:t + 2, 0]
                        else:
                            src, dst = bank[:, 0:w], negmax2[:, hh, t, at // BLK:at // BLK + 1]
                        dve.tensor_reduce(dst, src, AX_X, ALU.max, negate=True).then_inc(a_free, 1)
                    elif what == "split":
                        dve.wait_ge(a_free, n.a + 2 + 2 * U * ja + U * (s + 1))
                        halves = negmax2[:, s, :, 0], negmax2[:, s, :, 1]
                        parts = [negparts[:, s, :, m] for m in range(PARTS)]
                        dve.tensor_tensor(negmax[:, s, :], *halves, ALU.min)
                        dve.tensor_tensor(parts[0], *halves, ALU.min).then_inc(dve_step, 1)
                        dve.wait_ge(dve_step, base + (c + 1))
                        dve.tensor_tensor(negrest[:, s, :], negmax[:, s, :], parts[0], ALU.subtract).then_inc(dve_step, 1)
                        dve.wait_ge(dve_step, base + (c + 2))
                        dve.tensor_copy(parts[1], negrest[:, s, :]).then_inc(dve_step, 1)
                        dve.wait_ge(dve_step, base + (c + 3))
                        dve.tensor_tensor(parts[2], negrest[:, s, :], parts[1], ALU.subtract).then_inc(negparts_ready, 1)
                        c += 3
                    elif what == "gather":
                        dve.wait_ge(o_free, n.o + 2 * jj + (s + 2))
                        dve.wait_ge(gathered, n.o + 2 * jj + (s + 1))
                        o = pO[s][:, 0:TB // 2 * GATHER].rearrange("p (b f) -> p b f", b=TB // 2)[:, :, 0:2 * (DH + 1)]\
                            .rearrange("p b (h d) -> p b h d", h=2)
                        c += 1
                        dve.reciprocal(rden[:, :, :], o[:, :, :, DH]).then_inc(dve_step, 1)
                        dve.wait_ge(dve_step, base + c)
                        dve.tensor_tensor(AO[:, :, bass.ds(2 * jj + s, 1), :].rearrange("p (b h) a d -> p b h (a d)", h=2),
                                          o[:, :, :, 0:DH], rden[:, :, :].unsqueeze(3).broadcast_to([P, 4, 2, DH]), ALU.mult)\
                            .then_inc(o_free, 1)
                        if s == 1 and with_a:
                            copy_v(mode, ja, ka)
                return c

            def attention(mode):
                if mode.kind != "full":
                    link(dve.memset(negmax2[:, :, :, 1], 3e38))
                n.vp += NT // 2 if mode.kind == "window" else NT // 4
                dve.wait_ge(v_in_place, n.vp)
                copy_v(mode, 0, 0)
                copy_v(mode, 1, 1)
                per_job = 8

                def job(j, k, events, i):
                    if i is None and j == JOBS - 1:
                        n.step += 2 * per_job * (JOBS // 2 - 1)
                    base = n.step if i is None else n.step + per_job * (1 - k) + 2 * per_job * i
                    c = run(mode, j, k, events, base)
                    if i is None:
                        n.step += c
                    else:
                        assert c == per_job

                run_jobs(dve, mode, job)
                n.a += 2 * mode.U * JOBS
                n.o += 2 * JOBS
                dve.wait_ge(o_free, n.o + 2)

            def out_proj(mode):
                for q in range(4):
                    bank = v_take()
                    ts = slice(4 * q, 4 * q + 4)
                    x4, lx4, x1 = (a[:, ts, :].rearrange("p t c -> p (t c)") for a in (X, LX, XN))
                    if mode.kind == "full":
                        dve.tensor_tensor(x1, bank, lx4, ALU.add).then_inc(v_free, 1)
                        dve.wait_ge(v_free, n.v + 2)
                        link(dve.scalar_tensor_tensor(x4, x1, 0.5, x4, ALU.mult, ALU.add))
                    else:
                        dve.tensor_tensor(x4, bank, x4, ALU.add).then_inc(v_free, 1)
                dve.wait_ge(v_free, n.v + 2)

            def memory():
                dve.wait_ge(pts_ready, NT // 2)
                prods = [rest[:, m * NT * HEADS:(m + 1) * NT * HEADS].rearrange("p (t h) -> p t h", h=HEADS)
                         for m in range(2)]
                for c in range(LINE // 2):
                    line_part(dve, link, Lw, 3, 0, c, True, prods)
                dve.sem_inc(half_written, 1)
                for c in range(LINE):
                    line_part(dve, link, Lr, 1, 2, c, False, prods)
                sq_read = LX_all[:, 0:n_line].rearrange("p (t h c) -> p t h c", t=NT, h=HEADS)
                link(dve.tensor_tensor(sq_read[:, :, :, :], Lr[:, :, :, :], Lr[:, :, :, :], ALU.mult))
                bank = v_take()
                dve.tensor_copy(gates[:, :, :].rearrange("p t h -> p (t h)"), bank[:, 0:NT * HEADS]).then_inc(v_free, 1)
                dve.wait_ge(v_free, n.v + 2)
                dve.sem_inc(sig_in, 1)
                for m, (squares, which) in enumerate(((sq_read, 1), (sq, 0))):
                    if which == 0:
                        dve.wait_ge(sq_ready, 1)
                    link(dve.tensor_reduce(norm[:, :, :].rearrange("p t h -> p (t h)"),
                                           squares[:, :, :, :].rearrange("p t h c -> p (t h) c"), AX_X, ALU.add))
                    dve.tensor_scalar(norm[:, :, :], norm[:, :, :], 1e-24, None, ALU.max).then_inc(norm_in, 1)
                    dve.wait_ge(norm_out, m + 1)
                    recip = dve.reciprocal(rnorm[which][:, :, :], norm[:, :, :])
                    if which == 0:
                        recip.then_inc(rnorm_ready, 1)
                        dve.wait_ge(rnorm_ready, 1)
                    else:
                        link(recip)
                for half in range(2):
                    ins = scale_lines(dve, Lr, 1, half)
                ins.then_inc(lines_ready, 1)

            def memory_scores():
                assert n.v == MEM_V0, n.v
                m, used = 0, 0

                def near_sum(m):
                    dve.wait_ge(near2_ready, m + 1)
                    return dve.tensor_reduce(score_in[:, m // 4, m % 4 * 4:m % 4 * 4 + 4], near2[m % 2][:, :, :], AX_X, ALU.add)

                for t in range(NT):
                    if t % TB:
                        dve.wait_ge(phi_ready, used + 1)
                        for half in range(2):
                            bank = v_take()
                            hs = slice(half * HEADS // 2, (half + 1) * HEADS // 2)
                            f = far[:, hs, :].rearrange("p h c -> p (h c)")
                            if t % TB == 1:
                                dve.tensor_copy(f, bank[:, 0:HEADS // 2 * PHI]).then_inc(v_free, 1)
                            else:
                                dve.scalar_tensor_tensor(f, f, DECAY ** P, bank[:, 0:HEADS // 2 * PHI], ALU.mult, ALU.add)\
                                    .then_inc(v_free, 1)
                            dve.wait_ge(v_free, n.v + 2)
                            link(dve.tensor_tensor(farp[:, :, :], far[:, hs, :], phiR[used % 2][:, hs, :], ALU.mult))
                            link(dve.tensor_reduce(score_far[:, t, hs], farp[:, :, :], AX_X, ALU.add))
                        used += 1
                        dve.sem_inc(phi_used, 1)
                    for q in range(4):
                        bank = v_take()
                        dve.tensor_tensor(near[m % 2][:, :, :], bank.rearrange("p (h s) -> p h s", h=4),
                                          C("decay_root").unsqueeze(1).broadcast_to([P, 4, P]), ALU.mult)\
                            .then_inc(v_free, 1)
                        dve.wait_ge(v_free, n.v + 2)
                        if m:
                            near_sum(m - 1)
                        m += 1
                link(near_sum(m - 1))
                for b in range(BATCH):
                    ts = slice(b * TB + 1, (b + 1) * TB)
                    link(dve.tensor_tensor(score_in[:, ts, :], score_in[:, ts, :], score_far[:, ts, :], ALU.add))
                dve.tensor_tensor(score_in[:, :, :], score_in[:, :, :], scale16.unsqueeze(1)
                                  .broadcast_to([P, NT, HEADS]), ALU.mult).then_inc(sig_in, 1)
                dve.wait_ge(sig_out, 2)
                link(dve.tensor_tensor(score_in[:, :, :], score_in[:, :, :], gates[:, :, :], ALU.mult))
                link(dve.tensor_reduce(gated[:, :], score_in[:, :, :], AX_X, ALU.add))
                link(dve.tensor_scalar(gated[:, :], gated[:, :], 1.0 / HEADS, None, ALU.mult))

            def add_memory():
                for t in range(NT):
                    a = heads_of(t)
                    ins = dve.scalar_tensor_tensor(a, memval[:, t, :].rearrange("p (h d) -> p h d", h=HEADS),
                                                   gated[:, t:t + 1], a, ALU.mult, ALU.add)
                link(ins)
                dve.sem_inc(ao_ready, 1)

            dve.sem_inc(v_free, 2)
            dve.sem_inc(y_free, 2)
            dve.sem_inc(y_done, 2)
            dve.sem_inc(a_free, 2)
            dve.sem_inc(o_free, 2)
            dve.wait_ge(first_loaded, 16 * FIRST)
            dve.tensor_copy(masks[:, :], mask_in[:, :]).then_inc(consts_done, 1)
            dve.wait_ge(x_loaded, 16)
            for kind, arg in PLAN:
                if kind == "moe":
                    layer_norm(X, XN)
                    gate(0)
                    if n.u == 0:
                        bank = v_take()
                        dve.tensor_copy(row_wide[:, :], bank[:, 0:HEADS + 2]).then_inc(v_free, 1)
                        dve.wait_ge(v_free, n.v + 2)
                        dve.wait_ge(vec_done, 2)
                        dve.wait_ge(set_up, 3)
                    experts(0)
                elif kind == "attn":
                    layer_norm(X, XN)
                    n.xt += 4
                    project(arg)
                    if arg is CAUSAL:
                        memory()
                        memory_scores()
                    attention(arg)
                    if arg is CAUSAL:
                        add_memory()
                    out_proj(arg)
                else:
                    layer_norm(X, LX, False)
                    layer_norm(LX, XN)
                    n.xt += 4
                    project(arg)
                    attention(arg)
                    out_proj(arg)
                    layer_norm(XN, XN)
                    gate(1)
                    experts(1)
            dve.sem_inc(x_final, 1)


_INS = ['L0_attn_x', 'L0_attn_qkv_w', 'L0_attn_qkv_b', 'L0_attn_w1w', 'L0_attn_w2w', 'L0_attn_r1w', 'L0_attn_r2w',
        'L0_attn_memv_w', 'L0_attn_memv_b', 'L0_attn_memg_w', 'L0_attn_memg_b', 'L0_attn_mem_scale', 'L0_attn_out_w',
        'L0_attn_out_b', 'L0_ffn_Wg', 'L0_ffn_W1', 'L0_ffn_b1', 'L0_ffn_W2', 'L0_ffn_b2', 'L1_attn_q_w', 'L1_attn_q_b',
        'L1_attn_k_w', 'L1_attn_k_b', 'L1_attn_v_w', 'L1_attn_v_b', 'L1_attn_o_w', 'L1_attn_o_b', 'L1_ffn_ln1_g',
        'L1_ffn_ln1_b', 'L1_ffn_Wqkv', 'L1_ffn_bqkv', 'L1_ffn_Wo', 'L1_ffn_bo', 'L1_ffn_ln2_g', 'L1_ffn_ln2_b',
        'L1_ffn_gate_w', 'L1_ffn_W1', 'L1_ffn_b1', 'L1_ffn_W2', 'L1_ffn_b2', 'L1_ffn_rW1', 'L1_ffn_rb1', 'L1_ffn_rW2',
        'L1_ffn_rb2', 'L1_ffn_coef_w', 'L1_ffn_coef_b']


def constants():
    at = np.arange(P)
    row_, col = at[:, None], at[None, :]
    co, nconst = offsets(CONST_COLS)
    mo, nmask = offsets(MASK_COLS)
    const = np.zeros((P, nconst), np.float32)
    mask = np.zeros((P, nmask), np.float32)

    def put(where, cols, name, value):
        where[:, cols[name][0]:cols[name][0] + cols[name][1]] = value

    far_off = -1e30
    put(const, co, "ident", row_ == col)
    put(const, co, "decay_root", np.where(col < row_, DECAY ** ((row_ - col) / 2.0), 0.0))
    put(const, co, "decay_next", DECAY ** (P + col - row_ + 0.0))
    put(const, co, "rank", EXPERTS - np.arange(EXPERTS)[None, :])
    put(const, co, "same_head", row_ // LINE == np.arange(HEADS)[None, :])
    j = np.arange(GATHER)[None, :]
    mine = (row_ // QUAD % 2 == j // (DH + 1)) & (row_ % QUAD == j % (DH + 1))
    put(const, co, "gather", mine)
    put(const, co, "gather_window", np.concatenate([mine & (row_ // (2 * QUAD) == c) for c in range(2)], 1))
    put(mask, mo, "ident", row_ == col)
    put(mask, mo, "before", row_ < col)
    put(mask, mo, "ones", 1.0)
    put(mask, mo, "later_key", np.where(col > row_, far_off, 0.0))
    put(mask, mo, "later_query", np.where(row_ > col, far_off, 0.0))
    key = np.arange(SPAN)[None, :]
    put(mask, mo, "window_keys", np.where((key >= row_) & (key <= row_ + 2 * WIN), 0.0, far_off))
    query = np.arange(WQ)[None, :]
    put(mask, mo, "window_queries", np.where((row_ >= query) & (row_ <= query + 2 * WIN), 0.0, far_off))
    valid = np.zeros((1, PADDED), np.float32)
    valid[:, WIN:WIN + SEQ] = 1.0
    return {"consts": const, "mask_consts": mask, "valid": valid}


def kernel(**inputs):
    import concourse.bacc as _bacc
    from concourse.bass_utils import run_bass_kernel_spmd as _run

    nc = _bacc.Bacc("TRN2", target_bir_lowering=False, num_devices=1)
    arrays, d = {}, {}
    given = {name: np.ascontiguousarray(inputs[name]) for name in _INS}
    for name, a in {**given, **constants()}.items():
        arrays[f"in_{name}_dram"] = a
        d[name] = nc.dram_tensor(f"in_{name}_dram", a.shape, mybir.dt.from_np(a.dtype), kind="ExternalInput").ap()
    out = nc.dram_tensor("out_0_dram", (BATCH, SEQ, DIM), F32, kind="ExternalOutput").ap()
    build(nc, d, out)
    r = _run(nc, [arrays], core_ids=[0])
    return r.results[0]["out_0_dram"]
```
